# Optimizing a Trainium2 kernel written in Bass

```python
import numpy as np
import jax
import jax.numpy as jnp

def _softmax(x, axis=-1):
    return jax.nn.softmax(x, axis=axis)

def _gelu(x):
    return jax.nn.gelu(x, approximate=True)

def _silu(x):
    return jax.nn.silu(x)

def _sigmoid(x):
    return jax.nn.sigmoid(x)

def _layernorm(x, axis=-1, eps=1e-05):
    m = jnp.mean(x, axis=axis, keepdims=True)
    v = jnp.var(x, axis=axis, keepdims=True)
    return (x - m) / jnp.sqrt(v + eps)

def _scatter_add(tgt, idx, src, axis=0):
    return tgt.at[idx].add(src)

def _segment_sum(src, seg, n):
    return jax.ops.segment_sum(src, seg, n)
kernel_name = 'mk_decoder_preln_d1_seqx_r4_b667c4'

def setup_inputs(seed: int=0):
    np.random.seed(seed)
    _w = jnp.asarray

    def _rec_inputs():
        import jax
        import jax.numpy as jnp
        _rk = jax.random.key(seed)
        x = -0.0003929 + 0.9999 * jax.random.normal(jax.random.fold_in(_rk, 1), (4, 512, 256), jnp.float32)
        _lenS = 512 - jax.random.randint(jax.random.fold_in(_rk, 7), (4,), 0, max(1, 512 // 4) + 1, jnp.int32)
        _lenS2 = 1601 - jax.random.randint(jax.random.fold_in(_rk, 8), (4,), 0, max(1, 1601 // 4) + 1, jnp.int32)
        _ctx_1024P = jax.random.normal(jax.random.fold_in(_rk, 11), (4, 16, 256), jnp.float32)
        _ctx_1024c = jax.random.dirichlet(jax.random.fold_in(_rk, 511), 0.3 * jnp.ones((16,), jnp.float32), (4, 1601))
        _ctx_1024t = jnp.einsum('bsk,bkd->bsd', _ctx_1024c, _ctx_1024P)
        _ctx_1024t = _ctx_1024t * jax.lax.rsqrt(jnp.mean(jnp.square(_ctx_1024t)) + 1e-12) * 0.953939
        ctx_1024 = 2.81802e-05 + 1.00001 * (_ctx_1024t + 0.3 * jax.random.normal(jax.random.fold_in(_rk, 611), (4, 1601, 256), jnp.float32))
        return (x, ctx_1024)
    x, ctx_1024 = _rec_inputs()

    def _L0_attn_setup():
        import jax, jax.numpy as jnp
        import numpy as np

        def _logcumsumexp(x, axis):
            return jax.lax.associative_scan(jnp.logaddexp, x, axis=axis)

        def _log_g(x):
            return jnp.where(x >= 0, jnp.log(jax.nn.relu(x) + 0.5), -jax.nn.softplus(-x))

        def _min_gru(x, Wz, bz, Wh, bh):
            k = x @ Wz + bz
            log_z = -jax.nn.softplus(-k)
            log_coeffs = -jax.nn.softplus(k)
            log_tilde_h = _log_g(x @ Wh + bh)
            a_star = jnp.cumsum(log_coeffs, axis=1)
            log_h = a_star + _logcumsumexp(log_z + log_tilde_h - a_star, axis=1)
            return jnp.exp(log_h)
        key = jax.random.key(seed)
        ks = jax.random.split(key, 7)
        B, S, D, H = (4, 1024, 256, 256)
        s_in = 1.0 / np.sqrt(D)
        s_cat = 1.0 / np.sqrt(2 * H)
        return {'x': jax.random.normal(ks[0], (B, S, D), jnp.float32), 'Wz_f': jax.random.normal(ks[1], (D, H), jnp.float32) * s_in, 'bz_f': jnp.zeros((H,), jnp.float32), 'Wh_f': jax.random.normal(ks[2], (D, H), jnp.float32) * s_in, 'bh_f': jnp.zeros((H,), jnp.float32), 'Wz_b': jax.random.normal(ks[3], (D, H), jnp.float32) * s_in, 'bz_b': jnp.zeros((H,), jnp.float32), 'Wh_b': jax.random.normal(ks[4], (D, H), jnp.float32) * s_in, 'bh_b': jnp.zeros((H,), jnp.float32), 'W_out': jax.random.normal(ks[5], (2 * H, H), jnp.float32) * s_cat, 'b_out': jnp.zeros((H,), jnp.float32)}
    _L0_attn_all = _L0_attn_setup()
    _L0_attn_in = {k: v for k, v in _L0_attn_all.items() if k in ('Wz_f', 'bz_f', 'Wh_f', 'bh_f', 'Wz_b', 'bz_b', 'Wh_b', 'bh_b', 'W_out', 'b_out')}
    del _L0_attn_all

    def _L0_xattn_setup():
        import jax, jax.numpy as jnp
        import numpy as np
        DIM = 256
        key = jax.random.key(seed)
        k1, k2, k3, k4, k5 = jax.random.split(key, 5)
        B, Sq, Skv = (8, 512, 512)
        x = jax.random.normal(k1, (B, Sq, DIM), dtype=jnp.float32)
        context = jax.random.normal(k2, (B, Skv, DIM), dtype=jnp.float32)
        s = DIM ** (-0.5)
        Wq = jax.random.normal(k3, (DIM, DIM), dtype=jnp.float32) * s
        Wk = jax.random.normal(k4, (DIM, DIM), dtype=jnp.float32) * s
        Wv = jax.random.normal(k5, (DIM, DIM), dtype=jnp.float32) * s
        return {'x': x, 'context': context, 'Wq': Wq, 'Wk': Wk, 'Wv': Wv}
    _L0_xattn_all = _L0_xattn_setup()
    _L0_xattn_in = {k: v for k, v in _L0_xattn_all.items() if k in ('Wq', 'Wk', 'Wv')}
    del _L0_xattn_all

    def _L0_ffn_setup():
        import jax, jax.numpy as jnp
        import numpy as np
        H = 8
        QD = 64
        HALF = QD // 2
        DIMS = (32, 32)
        TOPK = 16
        DTK = 4
        EPS_BN = 1e-05
        EPS_NORM = 1e-12

        def _l2norm(x):
            n = jnp.linalg.norm(x, axis=-1, keepdims=True)
            return x / jnp.maximum(n, EPS_NORM)
        key = jax.random.key(seed)
        ks = jax.random.split(key, 6)
        B, S, D, O, E = (2, 128, 256, 256, 256)
        hidden_states = jax.random.normal(ks[0], (B, S, D), jnp.float32)
        Wq = jax.random.normal(ks[1], (D, H * QD), jnp.float32) * 0.02
        bq = jnp.zeros((H * QD,), jnp.float32)
        bn_gamma = jnp.ones((QD,), jnp.float32)
        bn_beta = jnp.zeros((QD,), jnp.float32)
        sub_key0 = jax.random.normal(ks[2], (DIMS[0], HALF), jnp.float32) * 0.02
        sub_key1 = jax.random.normal(ks[3], (DIMS[1], HALF), jnp.float32) * 0.02
        expert_down = jax.random.normal(ks[4], (E, D), jnp.float32) * 0.02
        expert_up = jax.random.normal(ks[5], (E, O), jnp.float32) * 0.02
        return {'hidden_states': hidden_states, 'Wq': Wq, 'bq': bq, 'bn_gamma': bn_gamma, 'bn_beta': bn_beta, 'sub_key0': sub_key0, 'sub_key1': sub_key1, 'expert_down': expert_down, 'expert_up': expert_up}
    _L0_ffn_all = _L0_ffn_setup()
    _L0_ffn_in = {k: v for k, v in _L0_ffn_all.items() if k in ('Wq', 'bq', 'bn_gamma', 'bn_beta', 'sub_key0', 'sub_key1', 'expert_down', 'expert_up')}
    del _L0_ffn_all
    return {'x': x, 'ctx_1024': ctx_1024, 'L0_attn_Wz_f': _L0_attn_in['Wz_f'], 'L0_attn_bz_f': _L0_attn_in['bz_f'], 'L0_attn_Wh_f': _L0_attn_in['Wh_f'], 'L0_attn_bh_f': _L0_attn_in['bh_f'], 'L0_attn_Wz_b': _L0_attn_in['Wz_b'], 'L0_attn_bz_b': _L0_attn_in['bz_b'], 'L0_attn_Wh_b': _L0_attn_in['Wh_b'], 'L0_attn_bh_b': _L0_attn_in['bh_b'], 'L0_attn_W_out': _L0_attn_in['W_out'], 'L0_attn_b_out': _L0_attn_in['b_out'], 'L0_xattn_Wq': _L0_xattn_in['Wq'], 'L0_xattn_Wk': _L0_xattn_in['Wk'], 'L0_xattn_Wv': _L0_xattn_in['Wv'], 'L0_ffn_Wq': _L0_ffn_in['Wq'], 'L0_ffn_bq': _L0_ffn_in['bq'], 'L0_ffn_bn_gamma': _L0_ffn_in['bn_gamma'], 'L0_ffn_bn_beta': _L0_ffn_in['bn_beta'], 'L0_ffn_sub_key0': _L0_ffn_in['sub_key0'], 'L0_ffn_sub_key1': _L0_ffn_in['sub_key1'], 'L0_ffn_expert_down': _L0_ffn_in['expert_down'], 'L0_ffn_expert_up': _L0_ffn_in['expert_up']}

def reference(x, ctx_1024, L0_attn_Wz_f, L0_attn_bz_f, L0_attn_Wh_f, L0_attn_bh_f, L0_attn_Wz_b, L0_attn_bz_b, L0_attn_Wh_b, L0_attn_bh_b, L0_attn_W_out, L0_attn_b_out, L0_xattn_Wq, L0_xattn_Wk, L0_xattn_Wv, L0_ffn_Wq, L0_ffn_bq, L0_ffn_bn_gamma, L0_ffn_bn_beta, L0_ffn_sub_key0, L0_ffn_sub_key1, L0_ffn_expert_down, L0_ffn_expert_up):
    import jax
    import jax.numpy as jnp

    def _L0_attn_ref(x, Wz_f, bz_f, Wh_f, bh_f, Wz_b, bz_b, Wh_b, bh_b, W_out, b_out):
        import jax, jax.numpy as jnp
        import numpy as np

        def _logcumsumexp(x, axis):
            return jax.lax.associative_scan(jnp.logaddexp, x, axis=axis)

        def _log_g(x):
            return jnp.where(x >= 0, jnp.log(jax.nn.relu(x) + 0.5), -jax.nn.softplus(-x))

        def _min_gru(x, Wz, bz, Wh, bh):
            k = x @ Wz + bz
            log_z = -jax.nn.softplus(-k)
            log_coeffs = -jax.nn.softplus(k)
            log_tilde_h = _log_g(x @ Wh + bh)
            a_star = jnp.cumsum(log_coeffs, axis=1)
            log_h = a_star + _logcumsumexp(log_z + log_tilde_h - a_star, axis=1)
            return jnp.exp(log_h)
        x_rev = jnp.flip(x, axis=1)
        out_fwd = _min_gru(x, Wz_f, bz_f, Wh_f, bh_f)
        out_bwd = _min_gru(x_rev, Wz_b, bz_b, Wh_b, bh_b)
        concat = jnp.concatenate([out_fwd, out_bwd], axis=2)
        return concat @ W_out + b_out

    def _L0_xattn_ref(x, context, Wq, Wk, Wv):
        import jax, jax.numpy as jnp
        import numpy as np
        DIM = 256
        q = jnp.einsum('bsd,ed->bse', x, Wq)
        k = jnp.einsum('btd,ed->bte', context, Wk)
        v = jnp.einsum('btd,ed->bte', context, Wv)
        scale = Wq.shape[0] ** (-0.5)
        dots = jnp.einsum('bse,bte->bst', q, k) * scale
        attn = jax.nn.softmax(dots, axis=-1)
        out = jnp.einsum('bst,bte->bse', attn, v)
        return out

    def _L0_ffn_ref(hidden_states, Wq, bq, bn_gamma, bn_beta, sub_key0, sub_key1, expert_down, expert_up):
        import jax, jax.numpy as jnp
        import numpy as np
        H = 8
        QD = 64
        HALF = QD // 2
        DIMS = (32, 32)
        TOPK = 16
        DTK = 4
        EPS_BN = 1e-05
        EPS_NORM = 1e-12

        def _l2norm(x):
            n = jnp.linalg.norm(x, axis=-1, keepdims=True)
            return x / jnp.maximum(n, EPS_NORM)
        B, S, D = hidden_states.shape
        q = (hidden_states @ Wq + bq).reshape(B, S, H, QD)
        mean = q.mean(axis=(0, 1, 2))
        var = q.var(axis=(0, 1, 2))
        q = (q - mean) / jnp.sqrt(var + EPS_BN) * bn_gamma + bn_beta
        q0 = _l2norm(q[..., :HALF])
        q1 = _l2norm(q[..., HALF:])
        k0 = _l2norm(sub_key0)
        k1 = _l2norm(sub_key1)
        s0 = jnp.einsum('bshq,kq->bshk', q0, k0)
        s1 = jnp.einsum('bshq,kq->bshk', q1, k1)
        ts0, ti0 = jax.lax.top_k(s0, DTK)
        ts1, ti1 = jax.lax.top_k(s1, DTK)
        comb_s = (ts0[..., :, None] + ts1[..., None, :]).reshape(B, S, H, DTK * DTK)
        comb_i = (ti0[..., :, None] * DIMS[1] + ti1[..., None, :]).reshape(B, S, H, DTK * DTK)
        top_s, pos = jax.lax.top_k(comb_s, TOPK)
        idx = jnp.take_along_axis(comb_i, pos, axis=-1)
        w = jax.nn.softmax(top_s, axis=-1)
        down = expert_down[idx]
        up = expert_up[idx]
        eh = jnp.einsum('bshkd,bsd->bshk', down, hidden_states)
        eh = jax.nn.gelu(eh, approximate=False)
        out = jnp.einsum('bshko,bshk->bso', up, eh * w)
        return out
    x = x + _L0_attn_ref(_layernorm(x, axis=-1), L0_attn_Wz_f, L0_attn_bz_f, L0_attn_Wh_f, L0_attn_bh_f, L0_attn_Wz_b, L0_attn_bz_b, L0_attn_Wh_b, L0_attn_bh_b, L0_attn_W_out, L0_attn_b_out)
    x = x + _L0_xattn_ref(_layernorm(x, axis=-1), ctx_1024, L0_xattn_Wq, L0_xattn_Wk, L0_xattn_Wv)
    x = x + _L0_ffn_ref(_layernorm(x, axis=-1), L0_ffn_Wq, L0_ffn_bq, L0_ffn_bn_gamma, L0_ffn_bn_beta, L0_ffn_sub_key0, L0_ffn_sub_key1, L0_ffn_expert_down, L0_ffn_expert_up)
    return x

_drawn_inputs = setup_inputs


def setup_inputs(seed=0):
    import zlib

    import numpy as np

    out = dict(_drawn_inputs(seed))
    spreads = {'L0_attn_bz_f': (0.0, 0.8),
     'L0_attn_bh_f': (0.0, 0.1),
     'L0_attn_bz_b': (0.0, 0.8),
     'L0_attn_bh_b': (0.0, 0.1),
     'L0_attn_b_out': (0.0, 0.1),
     'L0_ffn_bq': (0.0, 0.8),
     'L0_ffn_bn_gamma': (1.0, 0.6),
     'L0_ffn_bn_beta': (0.0, 0.8)}
    factors = {'L0_ffn_Wq': 8.0,
     'L0_ffn_sub_key0': 8.0,
     'L0_ffn_sub_key1': 8.0,
     'L0_ffn_expert_down': 4.401,
     'L0_ffn_expert_up': 3.904}
    for name, (base, spread) in spreads.items():
        noise = np.random.default_rng([zlib.crc32(name.encode()), seed]).standard_normal(out[name].shape)
        drawn = base * np.exp(spread * noise) if base else spread * noise
        out[name] = jnp.asarray(drawn.astype(out[name].dtype))
    for name, factor in factors.items():
        out[name] = (out[name] * factor).astype(out[name].dtype)
    return out
```

```python
import concourse.bass as bass
from concourse import mybir
from contextlib import ExitStack

F32 = mybir.dt.float32
F32R = mybir.dt.float32r
ALU = mybir.AluOpType
ACT = mybir.ActivationFunctionType
AX = mybir.AxisListType

P = 128
BATCH, SEQ, D = 4, 512, 256
TOKENS = BATCH * SEQ
TPB = SEQ // P
TILES = TOKENS // P
DC = D // P
CTX = 1601
CT = -(-CTX // P)
CLAST = CTX - (CT - 1) * P
CPAD = CTX + CTX % 2
PIECES = DC * -(-CTX // SEQ) + (CT - 1) // 2 + 1
RAW = 4
LN_EPS = BN_EPS = 1e-5
NORM_EPS = 1e-12
HEADS, QD = 8, 64
HALF = QD // 2
KEYS, TOPK, EXPERTS = 32, 4, 256
QC = HEADS * QD // P
ATT_SCALE = float(D) ** -0.5


class Stage:

    def __init__(self, nc, ctx, name):
        self.nc, self.ctx, self.name = nc, ctx, name

    def sb(self, name, shape, dt=F32):
        return self.ctx.enter_context(self.nc.sbuf_tensor(f"{self.name}_{name}", shape, dt))

    def ps(self, name, shape, dt=F32):
        return self.ctx.enter_context(self.nc.psum_tensor(f"{self.name}_{name}", shape, dt))

    def sem(self, name):
        return self.ctx.enter_context(self.nc.semaphore(f"{self.name}_{name}"))


def context_pieces(d, keep, b):
    par = b % 2
    th, tl, ch, cl, raw = (keep[n] for n in ("cTh", "cTl", "cNh", "cNl", "raw"))
    out = []
    for k in range(DC):
        for a in range(0, CTX, SEQ):
            e = min(a + SEQ, CTX)
            out.append((d["ctxT"][b, k * P:(k + 1) * P, a:e], lambda s, n=e - a: raw[:, s, 0:n],
                        th[par][:, k, a:e], tl[par][:, k, a:e]))
    for t in range(0, CT - 1, 2):
        out.append((d["ctx"][b, t * P:(t + 2) * P, :].rearrange("(t p) d -> p t d", p=P),
                    lambda s: raw[:, s].rearrange("p (t d) -> p t d", d=D), ch[par][:, t:t + 2], cl[par][:, t:t + 2]))
    out.append((d["ctx"][b, (CT - 1) * P:CTX, :], lambda s: raw[0:CLAST, s, 0:D],
                ch[par][0:CLAST, CT - 1], cl[par][0:CLAST, CT - 1]))
    return out


def split_products(pe, out, pairs):
    n = len(pairs)
    for i, ((lh, ll), (rh, rl)) in enumerate(pairs):
        pe.matmul(out, lh, rh, start=(i == 0), stop=False)
        pe.matmul(out, lh, rl, start=False, stop=False)
        last = pe.matmul(out, ll, rh, start=False, stop=(i == n - 1))
    return last


def rstd_tail(dve, link, ve, root, y, t, u, rstd):
    link(dve.reciprocal(y, root))
    link(dve.tensor_tensor(t, y, y, ALU.mult))
    link(dve.scalar_tensor_tensor(out=u, in0=t, scalar=-0.5, in1=ve, op0=ALU.mult, op1=ALU.mult))
    return dve.scalar_tensor_tensor(out=rstd, in0=u, scalar=1.5, in1=y, op0=ALU.add, op1=ALU.mult)


def stage_gru(nc, keep, d):
    x_all, ident, mv2 = keep["x"], keep["ident"], keep["mv2"]
    Mh, Ml, WvTh, WvTl = keep["Mh"], keep["Ml"], keep["WvTh"], keep["WvTl"]
    with ExitStack() as ctx:
        st = Stage(nc, ctx, "gru")
        w = st.sb("w", [P, 4, DC, D])
        wh = st.sb("wh", [P, 4, DC, D], F32R)
        wl = st.sb("wl", [P, 4, DC, D], F32R)
        wout = st.sb("wout", [P, 2 * DC, D])
        wa = st.sb("wa", [P, 2, DC, D])
        wvT = st.sb("wvT", [P, DC, D])
        bias = st.sb("bias", [P, 4, DC])
        nbias = st.sb("nbias", [P, 4, DC])
        bout = st.sb("bout", [P, D])
        stats = st.sb("stats", [P, TILES, 6])
        mv1 = st.sb("mv1", [P, TILES, 2])
        stats2 = st.sb("stats2", [P, TILES, 6])
        ve, root, y0, t0, u0, rstd = (st.sb(n, [P, TILES]) for n in ("ve", "root", "y0", "t0", "u0", "rstd"))
        xn = st.sb("xn", [P, 2, TPB, D])
        xTh = st.sb("xTh", [P, 2, DC, SEQ], F32R)
        xTl = st.sb("xTl", [P, 2, DC, SEQ], F32R)
        z, c, sg, r, g, zg = (st.sb(n, [P, 2, SEQ]) for n in ("z", "c", "sg", "r", "g", "zg"))
        hT = st.sb("hT", [P, 2, 2 * DC, SEQ])
        pT = st.ps("pT", [P, DC, SEQ])
        pP = st.ps("pP", [P, 4, SEQ])
        pO = st.ps("pO", [P, 2, 2, D])

        def last_bank(t):
            return pO[:, t, 0] if t < 2 else pT[:, t - 2, 0:D]

        ld_x = [st.sem(f"ld_x{b}") for b in range(BATCH)]
        ld_w, ld_wa, ld_small, ld_wout, ld_ctx = (st.sem(n) for n in ("ld_w", "ld_wa", "ld_small", "ld_wout", "ld_ctx"))
        dve_chain, ident_set, ident_ready = st.sem("dve_chain"), st.sem("ident_set"), st.sem("ident_ready")
        ve_ready, root_ready, nbias_ready = st.sem("ve_ready"), st.sem("root_ready"), st.sem("nbias_ready")
        wh_ready, wl_ready = st.sem("wh_ready"), st.sem("wl_ready")
        prep_mm, prep_hi, prep_lo = st.sem("prep_mm"), st.sem("prep_hi"), st.sem("prep_lo")
        xn_ready, xT_mm, xTh_ready, xTl_ready = (st.sem(n) for n in ("xn_ready", "xT_mm", "xTh_ready", "xTl_ready"))
        proj_mm, gates, relu_ready, g_ready, zg_ready, h_ready = (
            st.sem(n) for n in ("proj_mm", "gates", "relu_ready", "g_ready", "zg_ready", "h_ready"))
        xb_ready, out_mm, x2_ready = st.sem("xb_ready"), st.sem("out_mm"), st.sem("x2_ready")
        ld_piece = [st.sem(f"ld_piece{n}") for n in range(RAW)]
        piece_hi, piece_lo, pad_set = st.sem("piece_hi"), st.sem("piece_lo"), st.sem("pad_set")
        pieces = context_pieces(d, keep, 0)
        FIRST = 2 * DC
        UNITS = 2 * DC

        def pieces_at(n):
            left = BATCH * UNITS - FIRST
            return range(PIECES * (n - FIRST) // left, PIECES * (n + 1 - FIRST) // left) if n >= FIRST else range(0)

        with nc.Block() as block:
            @block.sync
            def _(sp):
                for b in range(BATCH):
                    sp.dma_start(x_all[:, b * TPB:(b + 1) * TPB, :],
                                 d["x"][b].rearrange("(t p) d -> p t d", p=P)).then_inc(ld_x[b], 16)
                sp.dma_start(wout[:], d["W_out"].rearrange("(k p) n -> p k n", p=P)).then_inc(ld_wout, 16)
                for n, (src, raw, _, _) in enumerate(pieces):
                    if n >= RAW:
                        sp.wait_ge(piece_lo, n - RAW + 1)
                    sp.dma_start(raw(n % RAW), src).then_inc(ld_piece[n % RAW], 16)

            @block.gpsimd
            def _(pool):
                pool.memset(ident[:], 0.0).then_inc(ident_set, 1)
                pool.wait_ge(ident_set, 1)
                pool.affine_select(out=ident[:], in_=ident[:], compare_op=ALU.not_equal, fill=1.0, base=0,
                                   pattern=[[-1, P]], channel_multiplier=1).then_inc(ident_ready, 1)
                for m in range(4):
                    pool.wait_ge(wh_ready, m + 1)
                    pool.tensor_tensor(wl[:, m], w[:, m], wh[:, m].bitcast(F32), ALU.subtract).then_inc(wl_ready, 1)
                for m in (keep["cTh"][0], keep["cTl"][0]):
                    pool.memset(m[:, :, CTX:CPAD].bitcast(F32), 0.0).then_inc(pad_set, 1)
                pool.wait_ge(pad_set, 2)
                pool.wait_ge(ld_small, 32)
                for b in range(BATCH):
                    for u in range(UNITS):
                        n = b * UNITS + u
                        for i in pieces_at(n):
                            pool.wait_ge(piece_hi, i + 1)
                            _, raw, hi, lo = pieces[i]
                            pool.tensor_tensor(lo, raw(i % RAW), hi.bitcast(F32), ALU.subtract).then_inc(piece_lo, 1)
                        pool.wait_ge(gates, 3 * n + 1)
                        pool.wait_ge(g_ready, n + 1)
                        if n >= 2:
                            pool.wait_ge(h_ready, n - 1)
                        pool.tensor_tensor(zg[:, u % 2], z[:, u % 2], g[:, u % 2], ALU.mult).then_inc(zg_ready, 1)
                        if u == 1:
                            pool.wait_ge(xn_ready, b + 1)
                            xb = x_all[:, b * TPB:(b + 1) * TPB, :]
                            pool.tensor_tensor(xb, xb, bout[:].unsqueeze(1).broadcast_to([P, TPB, D]),
                                               ALU.add).then_inc(xb_ready, 1)

            @block.scalar
            def _(act):
                for m, n in enumerate(("Wz_f", "Wh_f", "Wz_b", "Wh_b")):
                    act.dma_start(w[:, m], d[n].rearrange("(k p) n -> p k n", p=P)).then_inc(ld_w, 16)
                act.dma_start(bias[:], d["gate_bias"]).then_inc(ld_small, 16)
                act.dma_start(bout[:], d["b_out"].partition_broadcast(P)).then_inc(ld_small, 16)
                for m, n in enumerate(("xWq", "xWk")):
                    act.dma_start(wa[:, m], d[n].rearrange("(k p) n -> p k n", p=P)).then_inc(ld_wa, 16)
                act.dma_start(wvT[:], d["xWvT"].rearrange("(k p) n -> p k n", p=P)).then_inc(ld_wa, 16)
                act.wait_ge(ve_ready, 1)
                act.activation(root[:, 0:TPB], ve[:, 0:TPB], ACT.Sqrt).then_inc(root_ready, 1)
                act.wait_ge(ld_w, 64)
                for m in range(4):
                    act.activation(wh[:, m], w[:, m], ACT.Copy).then_inc(wh_ready, 1)
                act.wait_ge(ve_ready, 2)
                act.activation(root[:, TPB:TILES], ve[:, TPB:TILES], ACT.Sqrt).then_inc(root_ready, 1)
                act.wait_ge(prep_mm, 1)
                act.activation(Mh[:], pP[:, 0:2, 0:D], ACT.Copy).then_inc(prep_hi, 1)
                act.wait_ge(ld_wa, 48)
                act.activation(WvTh[:], wvT[:], ACT.Copy).then_inc(prep_hi, 1)

                def high(b):
                    act.wait_ge(xT_mm, b + 1)
                    if b >= 2:
                        act.wait_ge(proj_mm, 2 * UNITS * (b - 1))
                    for k in range(DC):
                        last = act.activation(xTh[:, b % 2, k], pT[:, k], ACT.Copy)
                    last.then_inc(xTh_ready, 1)

                high(0)
                act.wait_ge(ld_small, 32)
                act.wait_ge(nbias_ready, 1)
                for b in range(BATCH):
                    for u in range(UNITS):
                        n, way, ch = b * UNITS + u, u // DC, u % DC
                        for i in pieces_at(n):
                            act.wait_ge(ld_piece[i % RAW], 16 * (i // RAW + 1))
                            _, raw, hi, _ = pieces[i]
                            act.activation(hi, raw(i % RAW), ACT.Copy).then_inc(piece_hi, 1)
                        act.wait_ge(proj_mm, 2 * n + 1)
                        if n >= 2:
                            act.wait_ge(zg_ready, n - 1)
                        zp = pP[:, (2 * n) % 4]
                        act.activation(z[:, u % 2], zp, ACT.Sigmoid,
                                       bias=bias[:, 2 * way, ch:ch + 1]).then_inc(gates, 1)
                        if n >= 2:
                            act.wait_ge(h_ready, n - 1)
                        act.activation(c[:, u % 2], zp, ACT.Sigmoid, scale=-1.0,
                                       bias=nbias[:, 2 * way, ch:ch + 1]).then_inc(gates, 1)
                        act.wait_ge(proj_mm, 2 * n + 2)
                        if n >= 2:
                            act.wait_ge(g_ready, n - 1)
                        act.activation(sg[:, u % 2], pP[:, (2 * n + 1) % 4], ACT.Sigmoid,
                                       bias=bias[:, 2 * way + 1, ch:ch + 1]).then_inc(gates, 1)
                        if u == 2 and b + 1 < BATCH:
                            high(b + 1)

            @block.vector
            def _(dve):
                chained = [0]

                def link(ins):
                    chained[0] += 1
                    ins.then_inc(dve_chain, 1)
                    dve.wait_ge(dve_chain, chained[0])

                def moments(tiles, out, stat):
                    for t in tiles:
                        last = dve.bn_stats(stat[:, t], x_all[:, t])
                    link(last)
                    for t in tiles:
                        last = dve.bn_aggr(out[:, t], stat[:, t])
                    link(last)

                def normalise(b):
                    if b >= 2:
                        dve.wait_ge(xT_mm, b - 1)
                    for t in range(TPB):
                        i = b * TPB + t
                        last = dve.tensor_scalar(xn[:, b % 2, t], x_all[:, i], mv1[:, i, 0:1], rstd[:, i:i + 1],
                                                 ALU.subtract, ALU.mult)
                    last.then_inc(xn_ready, 1)

                def low(b):
                    dve.wait_ge(xTh_ready, b + 1)
                    if b >= 2:
                        dve.wait_ge(proj_mm, 2 * UNITS * (b - 1))
                    for k in range(DC):
                        last = dve.tensor_tensor(xTl[:, b % 2, k], pT[:, k], xTh[:, b % 2, k].bitcast(F32),
                                                 ALU.subtract)
                    last.then_inc(xTl_ready, 1)

                groups = ((0, TPB), (TPB, TILES))
                for n, (a, e) in enumerate(groups):
                    for b in range(a // TPB, e // TPB):
                        dve.wait_ge(ld_x[b], 16)
                    moments(range(a, e), mv1, stats)
                    dve.tensor_scalar(ve[:, a:e], mv1[:, a:e, 1], LN_EPS, None, ALU.add).then_inc(ve_ready, 1)
                    dve.wait_ge(ve_ready, n + 1)
                for n, (a, e) in enumerate(groups):
                    dve.wait_ge(root_ready, n + 1)
                    link(rstd_tail(dve, link, ve[:, a:e], root[:, a:e], y0[:, a:e], t0[:, a:e], u0[:, a:e],
                                   rstd[:, a:e]))
                    normalise(n)
                dve.wait_ge(ld_small, 32)
                dve.tensor_scalar(nbias[:], bias[:], -1.0, None, ALU.mult).then_inc(nbias_ready, 1)
                dve.wait_ge(prep_hi, 1)
                dve.tensor_tensor(Ml[:], pP[:, 0:2, 0:D], Mh[:].bitcast(F32), ALU.subtract).then_inc(prep_lo, 1)
                dve.wait_ge(prep_hi, 2)
                dve.tensor_tensor(WvTl[:], wvT[:], WvTh[:].bitcast(F32), ALU.subtract).then_inc(prep_lo, 1)
                low(0)

                def scan(b, u):
                    n = b * UNITS + u
                    dve.wait_ge(zg_ready, n + 1)
                    dve.wait_ge(gates, 3 * n + 2)
                    if b >= 2 and u == 0:
                        dve.wait_ge(out_mm, TPB * (b - 1))
                    keepg, add = c[:, u % 2], zg[:, u % 2]
                    if u >= DC:
                        keepg, add = c[:, u % 2, ::-1], zg[:, u % 2, ::-1]
                    dve.tensor_tensor_scan(hT[:, b % 2, u], keepg, add, 0.0, ALU.mult, ALU.add).then_inc(h_ready, 1)

                def residual(b):
                    dve.wait_ge(xb_ready, b + 1)
                    xb = x_all[:, b * TPB:(b + 1) * TPB, :]
                    if b < BATCH - 1:
                        for n in range(2):
                            dve.wait_ge(out_mm, TPB * b + 2 * (n + 1))
                            last = dve.tensor_tensor(xb[:, 2 * n:2 * n + 2], pO[:, n], xb[:, 2 * n:2 * n + 2], ALU.add)
                    else:
                        for t in range(TPB):
                            dve.wait_ge(out_mm, TPB * b + t + 1)
                            last = dve.tensor_tensor(xb[:, t], last_bank(t), xb[:, t], ALU.add)
                    last.then_inc(x2_ready, 1)
                    dve.wait_ge(x2_ready, b + 1)
                    moments(range(b * TPB, (b + 1) * TPB), mv2, stats2)

                for b in range(BATCH):
                    for u in range(UNITS):
                        n, way, ch = b * UNITS + u, u // DC, u % DC
                        dve.wait_ge(gates, 3 * n + 3)
                        hp = pP[:, (2 * n + 1) % 4]
                        dve.tensor_scalar(r[:, u % 2], hp, bias[:, 2 * way + 1, ch:ch + 1], 0.0,
                                          ALU.add, ALU.max).then_inc(relu_ready, 1)
                        dve.wait_ge(relu_ready, n + 1)
                        if n >= 2:
                            dve.wait_ge(zg_ready, n - 1)
                        dve.scalar_tensor_tensor(out=g[:, u % 2], in0=sg[:, u % 2], scalar=0.5, in1=r[:, u % 2],
                                                 op0=ALU.min, op1=ALU.add).then_inc(g_ready, 1)
                        if n >= 1:
                            scan((n - 1) // UNITS, (n - 1) % UNITS)
                        if u == 0 and b + 2 < BATCH:
                            normalise(b + 2)
                        if u == 2 and b + 1 < BATCH:
                            low(b + 1)
                        if u == 0 and b >= 2:
                            residual(b - 2)
                    if b == BATCH - 1:
                        residual(b - 1)
                scan(BATCH - 1, UNITS - 1)
                residual(BATCH - 1)

            @block.tensor
            def _(pe):
                pe.wait_ge(ident_ready, 1)
                pe.wait_ge(ld_wa, 48)
                for ch in range(DC):
                    for k in range(DC):
                        last = pe.matmul(pP[:, ch, 0:D], wa[:, 0, k, ch * P:(ch + 1) * P], wa[:, 1, k],
                                         start=(k == 0), stop=(k == DC - 1))
                last.then_inc(prep_mm, 1)

                def transposes(b):
                    pe.wait_ge(xn_ready, b + 1)
                    if b >= 1:
                        pe.wait_ge(xTl_ready, b)
                    for k in range(DC):
                        for t in range(TPB):
                            last = pe.transpose(pT[:, k, t * P:(t + 1) * P], xn[:, b % 2, t, k * P:(k + 1) * P],
                                                ident[:])
                    last.then_inc(xT_mm, 1)

                def output(b, t):
                    if t == 0:
                        pe.wait_ge(h_ready, UNITS * (b + 1))
                        if b >= 1:
                            pe.wait_ge(x2_ready, b)
                    for k in range(2 * DC):
                        last = pe.matmul(pO[:, t // 2, t % 2], hT[:, b % 2, k, t * P:(t + 1) * P], wout[:, k],
                                         start=(k == 0), stop=(k == 2 * DC - 1))
                    last.then_inc(out_mm, 1)

                def last_output(b):
                    pe.wait_ge(x2_ready, b)
                    for k in range(2 * DC):
                        pe.wait_ge(h_ready, UNITS * b + k + 1)
                        for t in range(TPB):
                            mm = pe.matmul(last_bank(t), hT[:, b % 2, k, t * P:(t + 1) * P], wout[:, k],
                                           start=(k == 0), stop=(k == 2 * DC - 1))
                            if k == 2 * DC - 1:
                                mm.then_inc(out_mm, 1)

                transposes(0)
                pe.wait_ge(ld_wout, 16)
                pe.wait_ge(wl_ready, 4)
                pe.wait_ge(prep_lo, 2)
                for b in range(BATCH):
                    pe.wait_ge(xTl_ready, b + 1)
                    for j in range(2 * UNITS):
                        n = 2 * UNITS * b + j
                        way, ch, m = j // (2 * DC), (j // 2) % DC, j % 2
                        if n >= 4:
                            if m == 0:
                                pe.wait_ge(gates, 3 * ((n - 4) // 2) + 2)
                            else:
                                pe.wait_ge(gates, 3 * ((n - 4) // 2) + 3)
                                pe.wait_ge(relu_ready, (n - 4) // 2 + 1)
                        cols = slice(ch * P, (ch + 1) * P)
                        split_products(pe, pP[:, n % 4], [
                            ((wh[:, 2 * way + m, k, cols], wl[:, 2 * way + m, k, cols]),
                             (xTh[:, b % 2, k], xTl[:, b % 2, k])) for k in range(DC)]).then_inc(proj_mm, 1)
                        if j == UNITS - 1 and b + 1 < BATCH:
                            transposes(b + 1)
                        if j >= UNITS and b >= 1:
                            output(b - 1, j - UNITS)
                last_output(BATCH - 1)


def stage_attention(nc, keep, d):
    x_all, ident, mv2, mv3 = keep["x"], keep["ident"], keep["mv2"], keep["mv3"]
    Mh, Ml, WvTh, WvTl = keep["Mh"], keep["Ml"], keep["WvTh"], keep["WvTl"]
    cTh, cTl, cNh, cNl = keep["cTh"], keep["cTl"], keep["cNh"], keep["cNl"]
    KB = -(-CPAD // SEQ)
    RING = 3
    GROUPS = [range(i, min(i + 4, CT)) for i in range(0, CT, 4)]
    NG = len(GROUPS)

    def at_tile(g):
        out = []
        if 0 <= g - 2 < TILES:
            out.append(("V", g - 2, 0))
        if 0 <= g - 1 < TILES:
            out += [("P", g - 1, 0), ("P", g - 1, 1)]
        if 0 <= g < TILES:
            out.append(("E", g, 0))
        if 0 <= g - 2 < TILES:
            out.append(("O", g - 2, 0))
        if 0 <= g - 1 < TILES:
            out += [("P", g - 1, 2), ("A", g - 1, 0), ("P", g - 1, 3), ("A", g - 1, 1), ("A", g - 1, 2), ("A", g - 1, 3)]
        b = g // TPB + 1
        if b < BATCH and g % TPB == 1:
            out += [("X", b, 0), ("X", b, 1)]
        if b < BATCH and g % TPB == 2:
            out += [("Q", b, 0), ("Q", b, 1)]
        return out

    START = [("X", 0, 0), ("X", 0, 1), ("Q", 0, 0), ("Q", 0, 1)]
    SLOTS = [at_tile(g) for g in range(TILES + 2)]
    ring = [it for slot in [START] + SLOTS for it in slot if it[0] not in "EA"]
    place = {it: n for n, it in enumerate(ring)}
    halved = {it: n for n, it in enumerate([it for it in ring if it[0] != "O"])}

    with ExitStack() as ctx:
        st = Stage(nc, ctx, "att")
        ve, root, y0, t0, u0, rstd = (st.sb(n, [P, TILES]) for n in ("ve", "root", "y0", "t0", "u0", "rstd"))
        xn = st.sb("xn", [P, TPB, D])
        xT = [st.sb(n, [P, DC, SEQ], F32R) for n in ("xTh", "xTl")]
        qT = [st.sb(n, [P, 2, DC, SEQ], F32R) for n in ("qTh", "qTl")]
        prob = st.sb("prob", [P, 2, CTX])
        pT = [st.sb(n, [P, CT, P], F32R) for n in ("pTh", "pTl")]
        vT = [st.sb(n, [P, 2, DC, P], F32R) for n in ("vTh", "vTl")]
        val = st.sb("val", [P, 2, D])
        mx = st.sb("mx", [P, 2, KB])
        nmax = st.sb("nmax", [P, 2])
        tmax = st.sb("tmax", [P, 2])
        rowsum = st.sb("rowsum", [P, 2])
        rinv = st.sb("rinv", [P, 2])
        stats = st.sb("stats", [P, TILES, 6])
        pS = st.ps("pS", [P, KB * SEQ])
        pA = st.ps("pA", [P, SEQ])
        pR = st.ps("pR", [P, RING, SEQ])

        dve_chain, root_ready, ve_ready, xn_ready = (st.sem(n) for n in ("dve_chain", "root_ready", "ve_ready", "xn_ready"))
        ld_piece = [st.sem(f"ld_piece{n}") for n in range(RAW)]
        piece_hi, piece_lo, pad_set = st.sem("piece_hi"), st.sem("piece_lo"), st.sem("pad_set")
        bank_full, bank_high, bank_free = st.sem("bank_full"), st.sem("bank_high"), st.sem("bank_free")
        score_mm, max_ready, exp_ready, rinv_ready = (st.sem(n) for n in ("score_mm", "max_ready", "exp_ready", "rinv_ready"))
        value_mm, val_ready, x3_ready = st.sem("value_mm"), st.sem("val_ready"), st.sem("x3_ready")
        pieces = [p for b in range(1, BATCH) for p in context_pieces(d, keep, b)]

        def pieces_at(g):
            b, q = g // TPB, -(-PIECES // TPB)
            if b + 1 >= BATCH:
                return range(0)
            return range(b * PIECES + min(q * (g % TPB), PIECES), b * PIECES + min(q * (g % TPB + 1), PIECES))

        def half(it, which, n):
            kind, a, i = it
            bank = pR[:, n % RING]
            if kind == "X":
                return xT[which][:, i], bank
            if kind == "Q":
                return qT[which][:, a % 2, i], bank
            if kind == "P":
                rows = CLAST if GROUPS[i][-1] == CT - 1 else P
                m = len(GROUPS[i])
                return pT[which][0:rows, GROUPS[i][0]:GROUPS[i][0] + m], \
                    bank[0:rows, 0:m * P].rearrange("p (t n) -> p t n", n=P)
            return vT[which][:, a % 2], bank[:, 0:DC * P].rearrange("p (t n) -> p t n", n=P)

        def wait_overwrite(eng, it):
            kind, a, i = it
            if kind == "X" and a >= 1:
                eng.wait_ge(bank_full, place[("Q", a - 1, DC - 1)] + 1)
            elif kind == "Q" and a >= 2:
                eng.wait_ge(score_mm, KB * TPB * (a - 1))
            elif kind == "P" and a >= 1:
                eng.wait_ge(value_mm, NG * (a - 1) + i + 1)
            elif kind == "V" and a >= 2:
                eng.wait_ge(bank_full, place[("O", a - 2, 0)] + 1)

        with nc.Block() as block:
            @block.sync
            def _(sp):
                for n, (src, raw, _, _) in enumerate(pieces):
                    if n >= RAW:
                        sp.wait_ge(piece_lo, n - RAW + 1)
                    sp.dma_start(raw(n % RAW), src).then_inc(ld_piece[n % RAW], 16)

            @block.gpsimd
            def _(pool):
                for m in (cTh[1], cTl[1]):
                    pool.memset(m[:, :, CTX:CPAD].bitcast(F32), 0.0).then_inc(pad_set, 1)
                for g in range(TILES):
                    for i in pieces_at(g):
                        pool.wait_ge(piece_hi, i + 1)
                        b = i // PIECES + 1
                        if b >= 2:
                            pool.wait_ge(value_mm, NG * TPB * (b - 1))
                        _, raw, hi, lo = pieces[i]
                        pool.tensor_tensor(lo, raw(i % RAW), hi.bitcast(F32), ALU.subtract).then_inc(piece_lo, 1)

            @block.scalar
            def _(act):
                act.wait_ge(ve_ready, 1)
                act.activation(root[:], ve[:], ACT.Sqrt).then_inc(root_ready, 1)

                def high(it):
                    n = place[it]
                    act.wait_ge(bank_full, n + 1)
                    wait_overwrite(act, it)
                    to, bank = half(it, 0, n)
                    act.activation(to, bank, ACT.Copy).then_inc(bank_high, 1)

                def values(g):
                    act.wait_ge(value_mm, NG * (g + 1))
                    act.wait_ge(rinv_ready, g + 1)
                    if g >= 2:
                        act.wait_ge(bank_full, place[("V", g - 2, 0)] + 1)
                    act.activation(val[:, g % 2], pA[:, 0:D], ACT.Copy, scale=rinv[:, g % 2:g % 2 + 1])\
                        .then_inc(val_ready, 1)

                for it in START:
                    high(it)
                for g in range(TILES + 2):
                    if 0 <= g - 2 < TILES:
                        values(g - 2)
                    for it in SLOTS[g]:
                        if it[0] == "E":
                            act.wait_ge(max_ready, g + 1)
                            if g >= 2:
                                act.wait_ge(bank_full, place[("P", g - 2, NG - 1)] + 1)
                                act.wait_ge(rinv_ready, g - 1)
                            act.activation(prob[:, g % 2], pS[:, 0:CTX], ACT.Exp, bias=nmax[:, g % 2:g % 2 + 1],
                                           scale=ATT_SCALE, accum_out=rowsum[:, g % 2:g % 2 + 1]).then_inc(exp_ready, 1)
                        elif it[0] not in "AO":
                            high(it)
                    if g < TILES:
                        for i in pieces_at(g):
                            act.wait_ge(ld_piece[i % RAW], 16 * (i // RAW + 1))
                            b = i // PIECES + 1
                            if b >= 2:
                                act.wait_ge(value_mm, NG * TPB * (b - 1))
                            _, raw, hi, _ = pieces[i]
                            act.activation(hi, raw(i % RAW), ACT.Copy).then_inc(piece_hi, 1)

            @block.vector
            def _(dve):
                chained = [0]

                def link(ins):
                    chained[0] += 1
                    ins.then_inc(dve_chain, 1)
                    dve.wait_ge(dve_chain, chained[0])

                def normalise(b):
                    if b >= 1:
                        dve.wait_ge(bank_full, place[("X", b - 1, DC - 1)] + 1)
                    for t in range(TPB):
                        i = b * TPB + t
                        last = dve.tensor_scalar(xn[:, t], x_all[:, i], mv2[:, i, 0:1], rstd[:, i:i + 1],
                                                 ALU.subtract, ALU.mult)
                    last.then_inc(xn_ready, 1)

                def low(it):
                    n = place[it]
                    dve.wait_ge(bank_high, halved[it] + 1)
                    wait_overwrite(dve, it)
                    to, bank = half(it, 1, n)
                    dve.tensor_tensor(to, bank, half(it, 0, n)[0].bitcast(F32), ALU.subtract).then_inc(bank_free, 1)

                def output(g):
                    n = place[("O", g, 0)]
                    dve.wait_ge(bank_full, n + 1)
                    dve.tensor_tensor(x_all[:, g], pR[:, n % RING, 0:D], x_all[:, g], ALU.add).then_inc(bank_free, 1)
                    dve.wait_ge(bank_free, n + 1)
                    link(dve.bn_stats(stats[:, g], x_all[:, g]))
                    dve.bn_aggr(mv3[:, g], stats[:, g]).then_inc(x3_ready, 1)

                def row_max(g):
                    h = g % 2
                    for j in range(KB):
                        dve.wait_ge(score_mm, KB * g + j + 1)
                        last = dve.tensor_reduce(mx[:, h, j:j + 1], pS[:, j * SEQ:min((j + 1) * SEQ, CTX)], AX.X, ALU.max)
                    link(last)
                    link(dve.tensor_reduce(tmax[:, h:h + 1], mx[:, h], AX.X, ALU.max))
                    dve.tensor_scalar(nmax[:, h:h + 1], tmax[:, h:h + 1], -ATT_SCALE, None, ALU.mult).then_inc(max_ready, 1)

                dve.tensor_scalar(ve[:], mv2[:, :, 1], LN_EPS, None, ALU.add).then_inc(ve_ready, 1)
                dve.wait_ge(root_ready, 1)
                link(rstd_tail(dve, link, ve[:], root[:], y0[:], t0[:], u0[:], rstd[:]))
                normalise(0)
                for it in START:
                    low(it)
                for g in range(TILES + 2):
                    if 0 <= g - 1 < TILES:
                        dve.wait_ge(exp_ready, g)
                        if g >= 3:
                            dve.wait_ge(val_ready, g - 2)
                        dve.reciprocal(rinv[:, (g - 1) % 2:(g - 1) % 2 + 1], rowsum[:, (g - 1) % 2:(g - 1) % 2 + 1])\
                            .then_inc(rinv_ready, 1)
                    if g < TILES:
                        row_max(g)
                    for it in SLOTS[g]:
                        if it[0] == "O":
                            output(it[1])
                        elif it[0] not in "AE":
                            low(it)
                    if g % TPB == 0 and g // TPB + 1 < BATCH:
                        normalise(g // TPB + 1)

            @block.tensor
            def _(pe):
                def scores(g):
                    b, t = g // TPB, g % TPB
                    pe.wait_ge(bank_free, place[("Q", b, DC - 1)] + 1)
                    if b >= 1 and t == 0:
                        pe.wait_ge(piece_lo, PIECES * b)
                        pe.wait_ge(pad_set, 2)
                    if g >= 1:
                        pe.wait_ge(exp_ready, g)
                    for j in range(KB):
                        a, e = j * SEQ, min((j + 1) * SEQ, CPAD)
                        split_products(pe, pS[:, a:e], [
                            (tuple(q[:, b % 2, k, t * P:(t + 1) * P] for q in qT),
                             (cTh[b % 2][:, k, a:e], cTl[b % 2][:, k, a:e])) for k in range(DC)]).then_inc(score_mm, 1)

                def item(it):
                    kind, a, i = it
                    if kind == "A":
                        pe.wait_ge(bank_free, place[("P", a, i)] + 1)
                        if i == 0 and a >= 1:
                            pe.wait_ge(val_ready, a)
                        for kt in GROUPS[i]:
                            rows, par = (CLAST if kt == CT - 1 else P), (a // TPB) % 2
                            l = [p[0:rows, kt] for p in pT]
                            r = [c[par][0:rows, kt] for c in (cNh, cNl)]
                            pe.matmul(pA[:, 0:D], l[0], r[0], start=(kt == 0), stop=False)
                            pe.matmul(pA[:, 0:D], l[0], r[1], start=False, stop=False)
                            last = pe.matmul(pA[:, 0:D], l[1], r[0], start=False, stop=(kt == CT - 1))
                        last.then_inc(value_mm, 1)
                        return
                    n = place[it]
                    if n >= RING:
                        pe.wait_ge(bank_free, n - RING + 1)
                    bank = pR[:, n % RING]
                    if kind == "X":
                        pe.wait_ge(xn_ready, a + 1)
                        for t in range(TPB):
                            last = pe.transpose(bank[:, t * P:(t + 1) * P], xn[:, t, i * P:(i + 1) * P], ident[:])
                    elif kind == "Q":
                        pe.wait_ge(bank_free, place[("X", a, DC - 1)] + 1)
                        last = split_products(pe, bank, [
                            ((Mh[:, k, i * P:(i + 1) * P], Ml[:, k, i * P:(i + 1) * P]), (xT[0][:, k], xT[1][:, k]))
                            for k in range(DC)])
                    elif kind == "P":
                        pe.wait_ge(exp_ready, a + 1)
                        for m, kt in enumerate(GROUPS[i]):
                            rows = CLAST if kt == CT - 1 else P
                            last = pe.transpose(bank[0:rows, m * P:(m + 1) * P], prob[:, a % 2, kt * P:kt * P + rows],
                                                ident[:])
                    elif kind == "V":
                        pe.wait_ge(val_ready, a + 1)
                        for k in range(DC):
                            last = pe.transpose(bank[:, k * P:(k + 1) * P], val[:, a % 2, k * P:(k + 1) * P], ident[:])
                    else:
                        pe.wait_ge(bank_free, place[("V", a, 0)] + 1)
                        last = split_products(pe, bank[:, 0:D], [
                            ((vT[0][:, a % 2, k], vT[1][:, a % 2, k]), (WvTh[:, k], WvTl[:, k])) for k in range(DC)])
                    last.then_inc(bank_full, 1)

                for it in START:
                    item(it)
                for g in range(TILES + 2):
                    if g < TILES:
                        scores(g)
                    for it in SLOTS[g]:
                        if it[0] != "E":
                            item(it)


def stage_query(nc, keep, d):
    x_all, ident, mv3 = keep["x"], keep["ident"], keep["mv3"]
    qT, gT, keyT, bn = keep["qT"], keep["gT"], keep["keyT"], keep["bn"]
    OUTS = QC + DC
    with ExitStack() as ctx:
        st = Stage(nc, ctx, "query")
        wq = st.sb("wq", [P, DC, QC * P])
        down = st.sb("down", [P, DC, D])
        wqh, wql = (st.sb(n, [P, DC, QC * P], F32R) for n in ("wqh", "wql"))
        dnh, dnl = (st.sb(n, [P, DC, D], F32R) for n in ("dnh", "dnl"))
        bq = st.sb("bq", [P, QC])
        affine = st.sb("affine", [P, 2])
        key = st.sb("key", [P, P])
        keysq, keyn = st.sb("keysq", [P, P]), st.sb("keyn", [P, P])
        k2, kroot, ky, kt, ku, kinv = (st.sb(n, [P, 1]) for n in ("k2", "kroot", "ky", "kt", "ku", "kinv"))
        pair = st.sb("pair", [P, P])
        ve, root, y0, t0, u0, rstd = (st.sb(n, [P, TILES]) for n in ("ve", "root", "y0", "t0", "u0", "rstd"))
        xn = st.sb("xn", [P, 2, TPB, D])
        xTh, xTl = (st.sb(n, [P, 2, DC, SEQ], F32R) for n in ("xTh", "xTl"))
        stats = st.sb("stats", [P, BATCH * QC, 6])
        mv, mean, diff, spread = (st.sb(n, [P, 2]) for n in ("mv", "mean", "diff", "spread"))
        bve, broot, by, bt, bu, brstd = (st.sb(n, [P, 1]) for n in ("bve", "broot", "by", "bt", "bu", "brstd"))
        pT = st.ps("pT", [P, DC, SEQ])
        pQ = st.ps("pQ", [P, 4, SEQ])
        pK = st.ps("pK", [P, SEQ])
        pB = st.ps("pB", [P, SEQ])

        ld_w, ld_key, ld_up = st.sem("ld_w"), st.sem("ld_key"), st.sem("ld_up")
        zeroed, pair_ready, dve_chain = st.sem("zeroed"), st.sem("pair_ready"), st.sem("dve_chain")
        ve_ready, root_ready, w_high, w_low = (st.sem(n) for n in ("ve_ready", "root_ready", "w_high", "w_low"))
        keyn_ready, key_mm, key_ready = st.sem("keyn_ready"), st.sem("key_mm"), st.sem("key_ready")
        xn_ready, xT_mm, xTh_ready, xTl_ready = (st.sem(n) for n in ("xn_ready", "xT_mm", "xTh_ready", "xTl_ready"))
        proj_mm, proj_read = st.sem("proj_mm"), st.sem("proj_read")
        mv_ready, mean_mm, spread_ready, var_mm = (st.sem(n) for n in ("mv_ready", "mean_mm", "spread_ready", "var_mm"))

        with nc.Block() as block:
            @block.sync
            def _(sp):
                sp.dma_start(wq[:], d["fWq"].rearrange("(k p) n -> p k n", p=P)).then_inc(ld_w, 16)
                sp.dma_start(down[:], d["downT"].rearrange("(k p) n -> p k n", p=P)).then_inc(ld_w, 16)
                sp.dma_start(bq[:], d["fbq"]).then_inc(ld_w, 16)
                sp.dma_start(affine[:], d["bn"]).then_inc(ld_w, 16)
                sp.wait_ge(zeroed, 1)
                for h in range(2):
                    for s in range(2):
                        q = (2 * h + s) * HALF
                        sp.dma_start(key[q:q + HALF, q:q + HALF], d["keys"][s]).then_inc(ld_key, 16)
                sp.dma_start(keep["up"][:], d["up"].rearrange("(c p) n -> p c n", p=P)).then_inc(ld_up, 16)
                sp.wait_ge(ld_up, 16)

            @block.gpsimd
            def _(pool):
                pool.memset(key[:], 0.0).then_inc(zeroed, 1)
                pool.memset(pair[:], 0.0).then_inc(pair_ready, 1)
                for n, off in enumerate((0, QD, -QD)):
                    pool.wait_ge(pair_ready, n + 1)
                    pool.affine_select(out=pair[:], in_=pair[:], compare_op=ALU.not_equal, fill=0.5, base=off,
                                       pattern=[[-1, P]], channel_multiplier=1).then_inc(pair_ready, 1)

            @block.scalar
            def _(act):
                act.wait_ge(ve_ready, 1)
                act.activation(root[:], ve[:], ACT.Sqrt).then_inc(root_ready, 1)
                act.wait_ge(ve_ready, 2)
                act.activation(kroot[:], k2[:], ACT.Sqrt).then_inc(root_ready, 1)
                act.wait_ge(ld_w, 64)
                act.activation(wqh[:], wq[:], ACT.Copy).then_inc(w_high, 1)
                act.activation(dnh[:], down[:], ACT.Copy).then_inc(w_high, 1)

                def high(b):
                    act.wait_ge(xT_mm, b + 1)
                    if b >= 2:
                        act.wait_ge(proj_mm, OUTS * (b - 1))
                    for k in range(DC):
                        last = act.activation(xTh[:, b % 2, k], pT[:, k], ACT.Copy)
                    last.then_inc(xTh_ready, 1)

                high(0)
                for b in range(BATCH):
                    for j in range(OUTS):
                        n = b * OUTS + j
                        act.wait_ge(proj_mm, n + 1)
                        cols = slice(b * SEQ, (b + 1) * SEQ)
                        if j < QC:
                            act.activation(qT[:, j, cols], pQ[:, n % 4], ACT.Identity,
                                           bias=bq[:, j:j + 1]).then_inc(proj_read, 1)
                        else:
                            act.activation(gT[:, j - QC, cols], pQ[:, n % 4], ACT.Gelu).then_inc(proj_read, 1)
                        if j == 2 and b + 1 < BATCH:
                            high(b + 1)
                act.wait_ge(ve_ready, 3)
                act.activation(broot[:], bve[:], ACT.Sqrt).then_inc(root_ready, 1)

            @block.vector
            def _(dve):
                chained = [0]

                def link(ins):
                    chained[0] += 1
                    ins.then_inc(dve_chain, 1)
                    dve.wait_ge(dve_chain, chained[0])

                def normalise(b):
                    if b >= 2:
                        dve.wait_ge(xT_mm, b - 1)
                    for t in range(TPB):
                        i = b * TPB + t
                        last = dve.tensor_scalar(xn[:, b % 2, t], x_all[:, i], mv3[:, i, 0:1], rstd[:, i:i + 1],
                                                 ALU.subtract, ALU.mult)
                    last.then_inc(xn_ready, 1)

                def low(b):
                    dve.wait_ge(xTh_ready, b + 1)
                    if b >= 2:
                        dve.wait_ge(proj_mm, OUTS * (b - 1))
                    for k in range(DC):
                        last = dve.tensor_tensor(xTl[:, b % 2, k], pT[:, k], xTh[:, b % 2, k].bitcast(F32),
                                                 ALU.subtract)
                    last.then_inc(xTl_ready, 1)

                dve.tensor_scalar(ve[:], mv3[:, :, 1], LN_EPS, None, ALU.add).then_inc(ve_ready, 1)
                dve.wait_ge(root_ready, 1)
                link(rstd_tail(dve, link, ve[:], root[:], y0[:], t0[:], u0[:], rstd[:]))
                normalise(0)
                normalise(1)
                dve.wait_ge(ld_key, 64)
                link(dve.tensor_tensor(keysq[:], key[:], key[:], ALU.mult))
                link(dve.tensor_reduce(ku[:], keysq[:], AX.X, ALU.add))
                dve.tensor_scalar(k2[:], ku[:], NORM_EPS ** 2, None, ALU.max).then_inc(ve_ready, 1)
                dve.wait_ge(ve_ready, 2)
                dve.wait_ge(root_ready, 2)
                link(rstd_tail(dve, link, k2[:], kroot[:], ky[:], kt[:], ku[:], kinv[:]))
                dve.tensor_scalar(keyn[:], key[:], kinv[:], None, ALU.mult).then_inc(keyn_ready, 1)
                dve.wait_ge(w_high, 1)
                dve.tensor_tensor(wql[:], wq[:], wqh[:].bitcast(F32), ALU.subtract).then_inc(w_low, 1)
                dve.wait_ge(w_high, 2)
                dve.tensor_tensor(dnl[:], down[:], dnh[:].bitcast(F32), ALU.subtract).then_inc(w_low, 1)
                low(0)
                dve.wait_ge(key_mm, 1)
                dve.tensor_copy(keyT[:], pK[:, 0:P]).then_inc(key_ready, 1)
                for b in range(BATCH):
                    for j in range(QC):
                        dve.wait_ge(proj_read, b * OUTS + j + 1)
                        last = dve.bn_stats(stats[:, b * QC + j], qT[:, j, b * SEQ:(b + 1) * SEQ])
                        if j == 0 and b + 2 < BATCH:
                            normalise(b + 2)
                        if j == 2 and b + 1 < BATCH:
                            low(b + 1)
                link(last)
                dve.bn_aggr(mv[:], stats[:]).then_inc(mv_ready, 1)
                dve.wait_ge(mean_mm, 1)
                link(dve.tensor_copy(mean[:, 0:1], pB[:, 0:1]))
                link(dve.tensor_tensor(diff[:, 0:1], mv[:, 0:1], mean[:, 0:1], ALU.subtract))
                link(dve.tensor_tensor(diff[:, 1:2], diff[:, 0:1], diff[:, 0:1], ALU.mult))
                dve.tensor_tensor(spread[:, 0:1], diff[:, 1:2], mv[:, 1:2], ALU.add).then_inc(spread_ready, 1)
                dve.wait_ge(var_mm, 1)
                dve.tensor_scalar(bve[:], pB[:, 0:1], BN_EPS, None, ALU.add).then_inc(ve_ready, 1)
                dve.wait_ge(ve_ready, 3)
                dve.wait_ge(root_ready, 3)
                link(rstd_tail(dve, link, bve[:], broot[:], by[:], bt[:], bu[:], brstd[:]))
                link(dve.tensor_tensor(bn[:, 0:1], affine[:, 0:1], brstd[:], ALU.mult))
                link(dve.tensor_tensor(mean[:, 1:2], mean[:, 0:1], bn[:, 0:1], ALU.mult))
                link(dve.tensor_tensor(bn[:, 1:2], affine[:, 1:2], mean[:, 1:2], ALU.subtract))

            @block.tensor
            def _(pe):
                def transposes(b):
                    pe.wait_ge(xn_ready, b + 1)
                    if b >= 1:
                        pe.wait_ge(xTl_ready, b)
                    for k in range(DC):
                        for t in range(TPB):
                            last = pe.transpose(pT[:, k, t * P:(t + 1) * P], xn[:, b % 2, t, k * P:(k + 1) * P],
                                                ident[:])
                    last.then_inc(xT_mm, 1)

                transposes(0)
                pe.wait_ge(keyn_ready, 1)
                pe.transpose(pK[:, 0:P], keyn[:], ident[:]).then_inc(key_mm, 1)
                pe.wait_ge(w_low, 2)
                for b in range(BATCH):
                    pe.wait_ge(xTl_ready, b + 1)
                    for j in range(OUTS):
                        n = b * OUTS + j
                        if n >= 4:
                            pe.wait_ge(proj_read, n - 3)
                        wh, wl, c = (wqh, wql, j) if j < QC else (dnh, dnl, j - QC)
                        cols = slice(c * P, (c + 1) * P)
                        split_products(pe, pQ[:, n % 4], [
                            ((wh[:, k, cols], wl[:, k, cols]), (xTh[:, b % 2, k], xTl[:, b % 2, k]))
                            for k in range(DC)]).then_inc(proj_mm, 1)
                        if j == 1 and b + 1 < BATCH:
                            transposes(b + 1)
                pe.wait_ge(pair_ready, 4)
                pe.wait_ge(mv_ready, 1)
                pe.matmul(pB[:, 0:1], pair[:], mv[:, 0:1], start=True, stop=True).then_inc(mean_mm, 1)
                pe.wait_ge(spread_ready, 1)
                pe.matmul(pB[:, 0:1], pair[:], spread[:, 0:1], start=True, stop=True).then_inc(var_mm, 1)


def stage_experts(nc, keep, d):
    x_all, ident, qT, gT, keyT, bn, up = (keep[n] for n in ("x", "ident", "qT", "gT", "keyT", "bn", "up"))
    PER = 2
    GROUPS = TILES // PER
    HALVES = 2 * HEADS
    ROW = KEYS + TOPK
    ABOVE = 8.0
    FIRSTS = EXPERTS // KEYS
    COLS = PER * P
    WEIGH, SUM = 5, 3
    PB = 3
    with ExitStack() as ctx:
        st = Stage(nc, ctx, "exp")
        group_of = st.sb("group_of", [P, 4])
        sq = st.sb("sq", [P, QC, COLS])
        n2, nroot, ny, nt, nu, ninv = (st.sb(n, [P, 2, PER * HALVES]) for n in ("n2", "nroot", "ny", "nt", "nu", "ninv"))
        s = st.sb("s", [P, 2, PER, HALVES, ROW])
        picked = st.sb("picked", [P, 2, PER, HALVES, ROW])
        top = st.sb("top", [P, 2, PER, HALVES, 2 * TOPK])
        e = st.sb("e", [P, 2, PER, HALVES, KEYS])
        etop = st.sb("etop", [P, 2, PER, HALVES, TOPK])
        total = st.sb("total", [P, PER, HEADS, 2])
        inv = st.sb("inv", [P, PER, HEADS, 2])
        both = st.sb("both", [P, PER * HEADS])
        raw1 = st.sb("raw1", [P, PER * HEADS, FIRSTS])
        sum1, rest, restn = (st.sb(n, [P, PER, HEADS]) for n in ("sum1", "rest", "restn"))
        first = st.sb("first", [P, 2, PER, HEADS, FIRSTS])
        second = st.sb("second", [P, 2, PER, HEADS, KEYS])
        clamped = st.sb("clamped", [P, 2, PER])
        prod = st.sb("prod", [P, PB, HEADS, EXPERTS])
        hT = st.sb("hT", [P, 2, DC, P])
        pN = st.ps("pN", [P, SEQ])
        pS = st.ps("pS", [P, 2, SEQ])
        pW = st.ps("pW", [P, 2, SEQ])
        pO = st.ps("pO", [P, 2, SEQ])

        const_ready, dve_chain = st.sem("const_ready"), st.sem("dve_chain")
        sq_ready, q_ready, norm_mm, n2_ready, nroot_ready = (
            st.sem(n) for n in ("sq_ready", "q_ready", "norm_mm", "n2_ready", "nroot_ready"))
        score_mm, s_ready, top_ready, e_ready, etop_ready = (
            st.sem(n) for n in ("score_mm", "s_ready", "top_ready", "e_ready", "etop_ready"))
        weights_ready, prod_ready, weight_mm, h_ready, out_mm, y_ready, stored = (
            st.sem(n) for n in ("weights_ready", "prod_ready", "weight_mm", "h_ready", "out_mm", "y_ready", "stored"))

        with nc.Block() as block:
            @block.sync
            def _(sp):
                o = d["out"].rearrange("b (t p) d -> (b t) p d", p=P)
                for i in range(TILES):
                    sp.wait_ge(y_ready, i + 1)
                    sp.dma_start(o[i], x_all[:, i]).then_inc(stored, 16)
                sp.wait_ge(stored, 16 * TILES)

            @block.gpsimd
            def _(pool):
                pool.memset(group_of[:], 0.0).then_inc(const_ready, 1)
                pool.wait_ge(const_ready, 1)
                for q in range(4):
                    pool.memset(group_of[q * HALF:(q + 1) * HALF, q:q + 1], 1.0).then_inc(const_ready, 1)
                pool.wait_ge(const_ready, 5)
                pool.memset(s[:, :, :, :, KEYS:ROW], ABOVE).then_inc(const_ready, 1)
                for i in range(TILES):
                    n, t = i // PER, i % PER
                    pool.wait_ge(weights_ready, n + 1)
                    if i >= PB:
                        pool.wait_ge(weight_mm, i - PB + 1)
                    for a in (0, HEADS // 2):
                        hs = slice(a, a + HEADS // 2)
                        shape = [P, HEADS // 2, FIRSTS, KEYS]
                        pool.tensor_tensor(prod[:, i % PB, hs].rearrange("p h (i j) -> p h i j", j=KEYS),
                                           first[:, n % 2, t, hs].unsqueeze(3).broadcast_to(shape),
                                           second[:, n % 2, t, hs].unsqueeze(2).broadcast_to(shape),
                                           ALU.mult).then_inc(prod_ready, 1)
                    pool.wait_ge(prod_ready, 3 * i + 1)
                    last = prod[:, i % PB, 0, EXPERTS - 1:EXPERTS]
                    pool.tensor_tensor(last, last, clamped[:, n % 2, t:t + 1], ALU.add).then_inc(prod_ready, 1)

            @block.scalar
            def _(act):
                def normed(n):
                    cols = slice(n * COLS, (n + 1) * COLS)
                    if n >= 1:
                        act.wait_ge(norm_mm, n)
                    for c in range(QC):
                        last = act.activation(sq[:, c], qT[:, c, cols], ACT.Square, scale=bn[:, 0:1], bias=bn[:, 1:2])
                    last.then_inc(sq_ready, 1)
                    for c in range(QC):
                        last = act.activation(qT[:, c, cols], qT[:, c, cols], ACT.Identity, scale=bn[:, 0:1],
                                              bias=bn[:, 1:2])
                    last.then_inc(q_ready, 1)

                def root(n):
                    act.wait_ge(n2_ready, n + 1)
                    act.activation(nroot[:, n % 2], n2[:, n % 2], ACT.Sqrt).then_inc(nroot_ready, 1)

                def exponentials(i):
                    n, t = i // PER, i % PER
                    act.wait_ge(s_ready, i + 1)
                    if n >= 2:
                        act.wait_ge(weights_ready, n - 1)
                    act.activation(e[:, n % 2, t], s[:, n % 2, t, :, 0:KEYS], ACT.Exp).then_inc(e_ready, 1)

                normed(0)
                root(0)
                for n in range(GROUPS):
                    if n + 1 < GROUPS:
                        normed(n + 1)
                    for t in range(PER):
                        exponentials(PER * n + t)
                    act.wait_ge(top_ready, PER * (n + 1))
                    act.activation(etop[:, n % 2], top[:, n % 2, :, :, TOPK:], ACT.Exp).then_inc(etop_ready, 1)
                    if n + 1 < GROUPS:
                        root(n + 1)

            @block.vector
            def _(dve):
                chained = [0]

                def note(ins):
                    ins.then_inc(dve_chain, 1)
                    chained[0] += 1
                    return chained[0]

                def need(count):
                    dve.wait_ge(dve_chain, count)

                def squares(n):
                    dve.wait_ge(norm_mm, n + 1)
                    dve.tensor_scalar(n2[:, n % 2], pN[:, 0:PER * HALVES], NORM_EPS ** 2, None, ALU.max)\
                        .then_inc(n2_ready, 1)

                def inverse_norm_steps(n):
                    h = n % 2
                    y, t, u = ny[:, h], nt[:, h], nu[:, h]
                    if n > 0:
                        dve.wait_ge(nroot_ready, n + 1)
                    a = note(dve.reciprocal(y, nroot[:, h]))
                    yield
                    need(a)
                    a = note(dve.tensor_tensor(t, y, y, ALU.mult))
                    yield
                    need(a)
                    a = note(dve.scalar_tensor_tensor(out=u, in0=t, scalar=-0.5, in1=n2[:, h], op0=ALU.mult,
                                                      op1=ALU.mult))
                    yield
                    need(a)
                    norms_at.append(note(dve.scalar_tensor_tensor(out=ninv[:, h], in0=u, scalar=1.5, in1=y,
                                                                  op0=ALU.add, op1=ALU.mult)))
                    yield

                def top_scores(i, between, after):
                    n, t = i // PER, i % PER
                    h = n % 2
                    dve.wait_ge(score_mm, i + 1)
                    need(norms_at[n])
                    if n >= 2:
                        dve.wait_ge(e_ready, PER * (n - 1))
                    scale = ninv[:, h, t * HALVES:(t + 1) * HALVES].unsqueeze(2).broadcast_to([P, HALVES, KEYS])
                    dve.tensor_tensor(s[:, h, t, :, 0:KEYS], pS[:, i % 2].rearrange("p (g k) -> p g k", k=KEYS),
                                      scale, ALU.mult).then_inc(s_ready, 1)
                    between()
                    dve.wait_ge(s_ready, i + 1)
                    if n >= 2:
                        dve.wait_ge(etop_ready, n - 1)
                    for g in range(HALVES):
                        last = dve.max(top[:, h, t, g], s[:, h, t, g])
                    last.then_inc(top_ready, 1)
                    dve.wait_ge(top_ready, i + 1)
                    for g in range(HALVES):
                        last = dve.match_replace(picked[:, h, t, g], top[:, h, t, g], s[:, h, t, g], ABOVE)
                    picked_at.append(note(last))
                    after()

                def weights(n, norm_step):
                    h = n % 2
                    mark = picked[:, h].rearrange("p t (h s) k -> p (t h) s k", s=2)
                    ex = e[:, h].rearrange("p t (h s) k -> p (t h) s k", s=2)
                    dve.wait_ge(etop_ready, n + 1)
                    sums = note(dve.tensor_reduce(total[:].rearrange("p t h s -> p (t h s)"),
                                                  etop[:, h].rearrange("p t g k -> p (t g) k"), AX.X, ALU.add))
                    dve.wait_ge(e_ready, PER * (n + 1))
                    need(picked_at[PER * n + PER - 1])
                    own = note(dve.scalar_tensor_tensor(out=raw1[:], in0=mark[:, :, 0, 0:FIRSTS], scalar=ABOVE / 2,
                                                        in1=ex[:, :, 0, 0:FIRSTS], op0=ALU.is_gt, op1=ALU.mult))
                    need(sums)
                    inverse = note(dve.reciprocal(inv[:], total[:]))
                    if n >= 2:
                        dve.wait_ge(prod_ready, 3 * PER * (n - 1))
                    dve.scalar_tensor_tensor(out=second[:, h].rearrange("p t h k -> p (t h) k"),
                                             in0=mark[:, :, 1, 0:KEYS], scalar=ABOVE / 2, in1=ex[:, :, 1],
                                             op0=ALU.is_gt, op1=ALU.mult)
                    need(own)
                    owned = note(dve.tensor_reduce(sum1[:].rearrange("p t h -> p (t h)"), raw1[:], AX.X, ALU.add))
                    need(inverse)
                    product = note(dve.tensor_tensor(both[:].rearrange("p (t h) -> p t h", t=PER), inv[:, :, :, 0],
                                                     inv[:, :, :, 1], ALU.mult))
                    next(norm_step)
                    need(owned)
                    left = note(dve.tensor_tensor(rest[:], total[:, :, :, 0], sum1[:], ALU.subtract))
                    next(norm_step)
                    need(left)
                    left = note(dve.tensor_tensor(restn[:], rest[:], inv[:, :, :, 0], ALU.mult))
                    next(norm_step)
                    need(left)
                    dve.tensor_reduce(clamped[:, h], restn[:], AX.X, ALU.add)
                    need(product)
                    dve.tensor_tensor(first[:, h].rearrange("p t h i -> p (t h) i"), raw1[:],
                                      both[:].unsqueeze(2).broadcast_to([P, PER * HEADS, FIRSTS]),
                                      ALU.mult).then_inc(weights_ready, 1)
                    next(norm_step)

                def weigh(i):
                    dve.wait_ge(weight_mm, i + 1)
                    if i >= 2:
                        dve.wait_ge(out_mm, i - 1)
                    dve.tensor_tensor(hT[:, i % 2], pW[:, i % 2, 0:DC * P].rearrange("p (c n) -> p c n", n=P),
                                      gT[:, :, i * P:(i + 1) * P], ALU.mult).then_inc(h_ready, 1)

                def output(i):
                    dve.wait_ge(out_mm, i + 1)
                    dve.tensor_tensor(x_all[:, i], pO[:, i % 2, 0:D], x_all[:, i], ALU.add).then_inc(y_ready, 1)

                norms_at, picked_at = [], []
                squares(0)
                dve.wait_ge(nroot_ready, 1)
                for _ in inverse_norm_steps(0):
                    pass
                dve.wait_ge(const_ready, 6)
                for i in range(TILES + WEIGH + 1):
                    n, t = i // PER, i % PER

                    def between():
                        if 0 <= i - WEIGH < TILES:
                            weigh(i - WEIGH)

                    def after():
                        if i - WEIGH - 1 >= 0:
                            output(i - WEIGH - 1)

                    if i < TILES:
                        top_scores(i, between, after)
                        if t == PER - 1:
                            if n + 1 < GROUPS:
                                squares(n + 1)
                            weights(n, inverse_norm_steps(n + 1) if n + 1 < GROUPS else iter(range(PER * 2)))
                    else:
                        between()
                        after()

            @block.tensor
            def _(pe):
                def norms(n):
                    pe.wait_ge(sq_ready, n + 1)
                    if n >= 1:
                        pe.wait_ge(n2_ready, n)
                    for t in range(PER):
                        for c in range(QC):
                            a = t * HALVES + 4 * c
                            last = pe.matmul(pN[:, a:a + 4], sq[:, c, t * P:(t + 1) * P], group_of[:], start=True, stop=True)
                    last.then_inc(norm_mm, 1)

                def scores(i):
                    pe.wait_ge(q_ready, i // PER + 1)
                    if i >= 2:
                        pe.wait_ge(s_ready, i - 1)
                    for c in range(QC):
                        last = pe.matmul(pS[:, i % 2, c * P:(c + 1) * P], qT[:, c, i * P:(i + 1) * P], keyT[:],
                                         start=True, stop=True)
                    last.then_inc(score_mm, 1)

                def sum_heads(i):
                    if i >= 2:
                        pe.wait_ge(h_ready, i - 1)
                    pe.wait_ge(prod_ready, 3 * i + 3)
                    for c in range(DC):
                        for h in range(HEADS):
                            last = pe.matmul(pW[:, i % 2, c * P:(c + 1) * P], prod[:, i % PB, h, c * P:(c + 1) * P],
                                             ident[:], start=(h == 0), stop=(h == HEADS - 1))
                    last.then_inc(weight_mm, 1)

                def mix(i):
                    pe.wait_ge(h_ready, i + 1)
                    if i >= 2:
                        pe.wait_ge(y_ready, i - 1)
                    for c in range(DC):
                        last = pe.matmul(pO[:, i % 2, 0:D], hT[:, i % 2, c], up[:, c], start=(c == 0), stop=(c == DC - 1))
                    last.then_inc(out_mm, 1)

                pe.wait_ge(const_ready, 6)
                norms(0)
                scores(0)
                for i in range(TILES + WEIGH + 1):
                    n, t = i // PER, i % PER
                    if t == 0 and n + 1 < GROUPS:
                        norms(n + 1)
                    if i + 1 < TILES:
                        scores(i + 1)
                    if 0 <= i - WEIGH - 1 < TILES:
                        mix(i - WEIGH - 1)
                    if 0 <= i - SUM < TILES:
                        sum_heads(i - SUM)


def program(nc, d):
    with ExitStack() as ctx:
        st = Stage(nc, ctx, "keep")
        keep = {"x": st.sb("x", [P, TILES, D]), "ident": st.sb("ident", [P, P]), "mv2": st.sb("mv2", [P, TILES, 2]),
                "mv3": st.sb("mv3", [P, TILES, 2])}
        for n in ("Mh", "Ml", "WvTh", "WvTl"):
            keep[n] = st.sb(n, [P, DC, D], F32R)
        with ExitStack() as inner:
            att = Stage(nc, inner, "context")
            keep["raw"] = att.sb("raw", [P, RAW, SEQ])

            def halves(i):
                for n in ("cTh", "cTl"):
                    keep.setdefault(n, []).append(att.sb(f"{n}{i}", [P, DC, CPAD], F32R))
                for n in ("cNh", "cNl"):
                    keep.setdefault(n, []).append(att.sb(f"{n}{i}", [P, CT, D], F32R))

            halves(0)
            stage_gru(nc, keep, d)
            halves(1)
            stage_attention(nc, keep, d)
        for n, shape in (("qT", [P, QC, TOKENS]), ("gT", [P, DC, TOKENS]), ("keyT", [P, P]), ("bn", [P, 2]),
                         ("up", [P, DC, D])):
            keep[n] = st.sb(n, shape)
        stage_query(nc, keep, d)
        stage_experts(nc, keep, d)


def layout(np, i):
    def by_feature(v):
        return v.reshape(-1, P).T

    a = {"x": i["x"], "ctx": i["ctx_1024"], "ctxT": i["ctx_1024"].transpose(0, 2, 1),
         "W_out": i["L0_attn_W_out"], "b_out": i["L0_attn_b_out"],
         "xWq": i["L0_xattn_Wq"], "xWk": i["L0_xattn_Wk"], "xWvT": i["L0_xattn_Wv"].T,
         "gate_bias": np.stack([by_feature(i["L0_attn_" + n]) for n in ("bz_f", "bh_f", "bz_b", "bh_b")], 1),
         "fWq": i["L0_ffn_Wq"], "downT": i["L0_ffn_expert_down"].T, "up": i["L0_ffn_expert_up"],
         "fbq": by_feature(i["L0_ffn_bq"]),
         "bn": np.stack([np.concatenate([i["L0_ffn_bn_gamma"]] * 2), np.concatenate([i["L0_ffn_bn_beta"]] * 2)], 1),
         "keys": np.stack([i["L0_ffn_sub_key0"], i["L0_ffn_sub_key1"]])}
    for n in ("Wz_f", "Wh_f", "Wz_b", "Wh_b"):
        a[n] = i["L0_attn_" + n]
    return {n: np.ascontiguousarray(v) for n, v in a.items()}


def kernel(**inputs):
    import numpy as np
    import concourse.bacc as bacc
    from concourse.bass_utils import run_bass_kernel_spmd

    nc = bacc.Bacc("TRN2", target_bir_lowering=False, num_devices=1)
    arrays = layout(np, {n: np.asarray(v) for n, v in inputs.items()})
    d = {n: nc.dram_tensor(f"in_{n}", v.shape, mybir.dt.from_np(v.dtype), kind="ExternalInput").ap()
         for n, v in arrays.items()}
    d["out"] = nc.dram_tensor("out", (BATCH, SEQ, D), F32, kind="ExternalOutput").ap()
    program(nc, d)
    r = run_bass_kernel_spmd(nc, [{f"in_{n}": v for n, v in arrays.items()}], core_ids=[0])
    return r.results[0]["out"]
```

```python
import concourse.bass as bass
from concourse import mybir
from contextlib import ExitStack

F32 = mybir.dt.float32
F32R = mybir.dt.float32r
ALU = mybir.AluOpType
ACT = mybir.ActivationFunctionType
AX = mybir.AxisListType

P = 128
BATCH, SEQ, D = 4, 512, 256
TOKENS = BATCH * SEQ
TPB = SEQ // P
TILES = TOKENS // P
DC = D // P
CTX = 1601
CT = -(-CTX // P)
CLAST = CTX - (CT - 1) * P
CPAD = CTX + CTX % 2
PIECES = DC * -(-CTX // SEQ) + (CT - 1) // 2 + 1
RAW = 4
LN_EPS = BN_EPS = 1e-5
NORM_EPS = 1e-12
HEADS, QD = 8, 64
HALF = QD // 2
KEYS, TOPK, EXPERTS = 32, 4, 256
QC = HEADS * QD // P
ATT_SCALE = float(D) ** -0.5


class Stage:

    def __init__(self, nc, ctx, name):
        self.nc, self.ctx, self.name = nc, ctx, name

    def sb(self, name, shape, dt=F32):
        return self.ctx.enter_context(self.nc.sbuf_tensor(f"{self.name}_{name}", shape, dt))

    def ps(self, name, shape, dt=F32):
        return self.ctx.enter_context(self.nc.psum_tensor(f"{self.name}_{name}", shape, dt))

    def sem(self, name):
        return self.ctx.enter_context(self.nc.semaphore(f"{self.name}_{name}"))


def context_pieces(d, keep, b):
    par = b % 2
    th, tl, ch, cl, raw = (keep[n] for n in ("cTh", "cTl", "cNh", "cNl", "raw"))
    out = []
    for k in range(DC):
        for a in range(0, CTX, SEQ):
            e = min(a + SEQ, CTX)
            out.append((d["ctxT"][b, k * P:(k + 1) * P, a:e], lambda s, n=e - a: raw[:, s, 0:n],
                        th[par][:, k, a:e], tl[par][:, k, a:e]))
    for t in range(0, CT - 1, 2):
        out.append((d["ctx"][b, t * P:(t + 2) * P, :].rearrange("(t p) d -> p t d", p=P),
                    lambda s: raw[:, s].rearrange("p (t d) -> p t d", d=D), ch[par][:, t:t + 2], cl[par][:, t:t + 2]))
    out.append((d["ctx"][b, (CT - 1) * P:CTX, :], lambda s: raw[0:CLAST, s, 0:D],
                ch[par][0:CLAST, CT - 1], cl[par][0:CLAST, CT - 1]))
    return out


def split_products(pe, out, pairs):
    n = len(pairs)
    for i, ((lh, ll), (rh, rl)) in enumerate(pairs):
        pe.matmul(out, lh, rh, start=(i == 0), stop=False)
        pe.matmul(out, lh, rl, start=False, stop=False)
        last = pe.matmul(out, ll, rh, start=False, stop=(i == n - 1))
    return last


def rstd_tail(dve, link, ve, root, y, t, u, rstd):
    link(dve.reciprocal(y, root))
    link(dve.tensor_tensor(t, y, y, ALU.mult))
    link(dve.scalar_tensor_tensor(out=u, in0=t, scalar=-0.5, in1=ve, op0=ALU.mult, op1=ALU.mult))
    return dve.scalar_tensor_tensor(out=rstd, in0=u, scalar=1.5, in1=y, op0=ALU.add, op1=ALU.mult)


def stage_gru(nc, keep, d):
    x_all, ident, mv2 = keep["x"], keep["ident"], keep["mv2"]
    Mh, Ml, WvTh, WvTl = keep["Mh"], keep["Ml"], keep["WvTh"], keep["WvTl"]
    q0h, q0l = keep["qT0"]
    with ExitStack() as ctx:
        st = Stage(nc, ctx, "gru")
        w = st.sb("w", [P, 4, DC, D])
        wh = st.sb("wh", [P, 4, DC, D], F32R)
        wl = st.sb("wl", [P, 4, DC, D], F32R)
        wout = st.sb("wout", [P, 2 * DC, D])
        wa = st.sb("wa", [P, 2, DC, D])
        wvT = st.sb("wvT", [P, DC, D])
        bias = st.sb("bias", [P, 4, DC])
        nbias = st.sb("nbias", [P, 4, DC])
        bout = st.sb("bout", [P, D])
        stats = st.sb("stats", [P, TILES, 6])
        mv1 = st.sb("mv1", [P, TILES, 2])
        stats2 = st.sb("stats2", [P, TILES, 6])
        ve, root, y0, t0, u0, rstd = (st.sb(n, [P, TILES]) for n in ("ve", "root", "y0", "t0", "u0", "rstd"))
        xn = st.sb("xn", [P, 2, TPB, D])
        xTh = st.sb("xTh", [P, 2, DC, SEQ], F32R)
        xTl = st.sb("xTl", [P, 2, DC, SEQ], F32R)
        z, c, sg, r, g = (st.sb(n, [P, 2, SEQ]) for n in ("z", "c", "sg", "r", "g"))
        hT = st.sb("hT", [P, 2, 2 * DC, SEQ])
        pT = st.ps("pT", [P, DC, SEQ])
        pP = st.ps("pP", [P, 4, SEQ])
        pO = st.ps("pO", [P, 2, 2, D])

        def last_bank(t):
            return pO[:, t, 0] if t < 2 else pT[:, t - 2, 0:D]

        ld_x = [st.sem(f"ld_x{b}") for b in range(BATCH)]
        ld_w, ld_wa, ld_small, ld_wout, ld_ctx = (st.sem(n) for n in ("ld_w", "ld_wa", "ld_small", "ld_wout", "ld_ctx"))
        dve_chain, ident_set, ident_ready = st.sem("dve_chain"), st.sem("ident_set"), st.sem("ident_ready")
        ve_ready, root_ready, nbias_ready = st.sem("ve_ready"), st.sem("root_ready"), st.sem("nbias_ready")
        wh_ready, wl_ready = st.sem("wh_ready"), st.sem("wl_ready")
        prep_mm, prep_hi, prep_lo = st.sem("prep_mm"), st.sem("prep_hi"), st.sem("prep_lo")
        xn_ready, xT_mm, xTh_ready, xTl_ready = (st.sem(n) for n in ("xn_ready", "xT_mm", "xTh_ready", "xTl_ready"))
        proj_mm, gates, relu_ready, g_ready, zg_ready, h_ready = (
            st.sem(n) for n in ("proj_mm", "gates", "relu_ready", "g_ready", "zg_ready", "h_ready"))
        ve2_ready, x0_mm, x0_high, x0_low, q0_mm, q0_high = (
            st.sem(n) for n in ("ve2_ready", "x0_mm", "x0_high", "x0_low", "q0_mm", "q0_high"))
        xb_ready, out_mm, x2_ready = st.sem("xb_ready"), st.sem("out_mm"), st.sem("x2_ready")
        ld_piece = [st.sem(f"ld_piece{n}") for n in range(RAW)]
        piece_hi, piece_lo, pad_set = st.sem("piece_hi"), st.sem("piece_lo"), st.sem("pad_set")
        pieces = context_pieces(d, keep, 0)
        FIRST = 2 * DC
        UNITS = 2 * DC

        def pieces_at(n):
            left = BATCH * UNITS - FIRST
            return range(PIECES * (n - FIRST) // left, PIECES * (n + 1 - FIRST) // left) if n >= FIRST else range(0)

        with nc.Block() as block:
            @block.sync
            def _(sp):
                for b in range(BATCH):
                    sp.dma_start(x_all[:, b * TPB:(b + 1) * TPB, :],
                                 d["x"][b].rearrange("(t p) d -> p t d", p=P)).then_inc(ld_x[b], 16)
                sp.dma_start(wout[:], d["W_out"].rearrange("(k p) n -> p k n", p=P)).then_inc(ld_wout, 16)
                for n, (src, raw, _, _) in enumerate(pieces):
                    if n >= RAW:
                        sp.wait_ge(piece_lo, n - RAW + 1)
                    sp.dma_start(raw(n % RAW), src).then_inc(ld_piece[n % RAW], 16)

            @block.gpsimd
            def _(pool):
                pool.memset(ident[:], 0.0).then_inc(ident_set, 1)
                pool.wait_ge(ident_set, 1)
                pool.affine_select(out=ident[:], in_=ident[:], compare_op=ALU.not_equal, fill=1.0, base=0,
                                   pattern=[[-1, P]], channel_multiplier=1).then_inc(ident_ready, 1)
                for m in range(4):
                    pool.wait_ge(wh_ready, m + 1)
                    pool.tensor_tensor(wl[:, m], w[:, m], wh[:, m].bitcast(F32), ALU.subtract).then_inc(wl_ready, 1)
                for m in (keep["cTh"][0], keep["cTl"][0]):
                    pool.memset(m[:, :, CTX:CPAD].bitcast(F32), 0.0).then_inc(pad_set, 1)
                pool.wait_ge(pad_set, 2)
                pool.wait_ge(ld_small, 32)
                for b in range(BATCH):
                    for u in range(UNITS):
                        n = b * UNITS + u
                        for i in pieces_at(n):
                            pool.wait_ge(piece_hi, i + 1)
                            _, raw, hi, lo = pieces[i]
                            pool.tensor_tensor(lo, raw(i % RAW), hi.bitcast(F32), ALU.subtract).then_inc(piece_lo, 1)
                        pool.wait_ge(gates, 3 * n + 1)
                        pool.wait_ge(g_ready, n + 1)
                        pool.tensor_tensor(z[:, u % 2], z[:, u % 2], g[:, u % 2], ALU.mult).then_inc(zg_ready, 1)
                        if u == 1:
                            pool.wait_ge(xn_ready, b + 1)
                            xb = x_all[:, b * TPB:(b + 1) * TPB, :]
                            pool.tensor_tensor(xb, xb, bout[:].unsqueeze(1).broadcast_to([P, TPB, D]),
                                               ALU.add).then_inc(xb_ready, 1)

            @block.scalar
            def _(act):
                for m, n in enumerate(("Wz_f", "Wh_f", "Wz_b", "Wh_b")):
                    act.dma_start(w[:, m], d[n].rearrange("(k p) n -> p k n", p=P)).then_inc(ld_w, 16)
                act.dma_start(bias[:], d["gate_bias"]).then_inc(ld_small, 16)
                act.dma_start(bout[:], d["b_out"].partition_broadcast(P)).then_inc(ld_small, 16)
                for m, n in enumerate(("xWq", "xWk")):
                    act.dma_start(wa[:, m], d[n].rearrange("(k p) n -> p k n", p=P)).then_inc(ld_wa, 16)
                act.dma_start(wvT[:], d["xWvT"].rearrange("(k p) n -> p k n", p=P)).then_inc(ld_wa, 16)
                act.wait_ge(ve_ready, 1)
                act.activation(root[:, 0:TPB], ve[:, 0:TPB], ACT.Sqrt).then_inc(root_ready, 1)
                act.wait_ge(ld_w, 64)
                for m in range(4):
                    act.activation(wh[:, m], w[:, m], ACT.Copy).then_inc(wh_ready, 1)
                act.wait_ge(ve_ready, 2)
                act.activation(root[:, TPB:TILES], ve[:, TPB:TILES], ACT.Sqrt).then_inc(root_ready, 1)
                act.wait_ge(prep_mm, 1)
                act.activation(Mh[:], pP[:, 0:2, 0:D], ACT.Copy).then_inc(prep_hi, 1)
                act.wait_ge(ld_wa, 48)
                act.activation(WvTh[:], wvT[:], ACT.Copy).then_inc(prep_hi, 1)

                def high(b):
                    act.wait_ge(xT_mm, b + 1)
                    if b >= 2:
                        act.wait_ge(proj_mm, 2 * UNITS * (b - 1))
                    for k in range(DC):
                        last = act.activation(xTh[:, b % 2, k], pT[:, k], ACT.Copy)
                    last.then_inc(xTh_ready, 1)

                high(0)
                act.wait_ge(ld_small, 32)
                act.wait_ge(nbias_ready, 1)
                for b in range(BATCH):
                    for u in range(UNITS):
                        n, way, ch = b * UNITS + u, u // DC, u % DC
                        for i in pieces_at(n):
                            act.wait_ge(ld_piece[i % RAW], 16 * (i // RAW + 1))
                            _, raw, hi, _ = pieces[i]
                            act.activation(hi, raw(i % RAW), ACT.Copy).then_inc(piece_hi, 1)
                        act.wait_ge(proj_mm, 2 * n + 1)
                        if n >= 2:
                            act.wait_ge(h_ready, n - 1)
                        zp = pP[:, (2 * n) % 4]
                        act.activation(z[:, u % 2], zp, ACT.Sigmoid,
                                       bias=bias[:, 2 * way, ch:ch + 1]).then_inc(gates, 1)
                        act.activation(c[:, u % 2], zp, ACT.Sigmoid, scale=-1.0,
                                       bias=nbias[:, 2 * way, ch:ch + 1]).then_inc(gates, 1)
                        act.wait_ge(proj_mm, 2 * n + 2)
                        if n >= 2:
                            act.wait_ge(g_ready, n - 1)
                        act.activation(sg[:, u % 2], pP[:, (2 * n + 1) % 4], ACT.Sigmoid,
                                       bias=bias[:, 2 * way + 1, ch:ch + 1]).then_inc(gates, 1)
                        if u == 2 and b + 1 < BATCH:
                            high(b + 1)
                act.wait_ge(ve2_ready, 1)
                act.activation(root[:, 0:TPB], ve[:, 0:TPB], ACT.Sqrt).then_inc(root_ready, 1)
                for k in range(DC):
                    act.wait_ge(x0_mm, k + 1)
                    act.activation(xTh[:, 0, k], pP[:, k], ACT.Copy).then_inc(x0_high, 1)
                for k in range(DC):
                    act.wait_ge(q0_mm, k + 1)
                    act.activation(q0h[:, k], pP[:, 2 + k], ACT.Copy).then_inc(q0_high, 1)

            @block.vector
            def _(dve):
                chained = [0]

                def link(ins):
                    chained[0] += 1
                    ins.then_inc(dve_chain, 1)
                    dve.wait_ge(dve_chain, chained[0])

                def moments(tiles, out, stat):
                    for t in tiles:
                        last = dve.bn_stats(stat[:, t], x_all[:, t])
                    link(last)
                    for t in tiles:
                        last = dve.bn_aggr(out[:, t], stat[:, t])
                    link(last)

                def normalise(b):
                    if b >= 2:
                        dve.wait_ge(xT_mm, b - 1)
                    for t in range(TPB):
                        i = b * TPB + t
                        last = dve.tensor_scalar(xn[:, b % 2, t], x_all[:, i], mv1[:, i, 0:1], rstd[:, i:i + 1],
                                                 ALU.subtract, ALU.mult)
                    last.then_inc(xn_ready, 1)

                def low(b):
                    dve.wait_ge(xTh_ready, b + 1)
                    if b >= 2:
                        dve.wait_ge(proj_mm, 2 * UNITS * (b - 1))
                    for k in range(DC):
                        last = dve.tensor_tensor(xTl[:, b % 2, k], pT[:, k], xTh[:, b % 2, k].bitcast(F32),
                                                 ALU.subtract)
                    last.then_inc(xTl_ready, 1)

                groups = ((0, TPB), (TPB, TILES))
                for n, (a, e) in enumerate(groups):
                    for b in range(a // TPB, e // TPB):
                        dve.wait_ge(ld_x[b], 16)
                    moments(range(a, e), mv1, stats)
                    dve.tensor_scalar(ve[:, a:e], mv1[:, a:e, 1], LN_EPS, None, ALU.add).then_inc(ve_ready, 1)
                    dve.wait_ge(ve_ready, n + 1)
                for n, (a, e) in enumerate(groups):
                    dve.wait_ge(root_ready, n + 1)
                    link(rstd_tail(dve, link, ve[:, a:e], root[:, a:e], y0[:, a:e], t0[:, a:e], u0[:, a:e],
                                   rstd[:, a:e]))
                    normalise(n)
                dve.wait_ge(ld_small, 32)
                dve.tensor_scalar(nbias[:], bias[:], -1.0, None, ALU.mult).then_inc(nbias_ready, 1)
                dve.wait_ge(prep_hi, 1)
                dve.tensor_tensor(Ml[:], pP[:, 0:2, 0:D], Mh[:].bitcast(F32), ALU.subtract).then_inc(prep_lo, 1)
                dve.wait_ge(prep_hi, 2)
                dve.tensor_tensor(WvTl[:], wvT[:], WvTh[:].bitcast(F32), ALU.subtract).then_inc(prep_lo, 1)
                low(0)

                def scan(b, u):
                    n = b * UNITS + u
                    dve.wait_ge(zg_ready, n + 1)
                    dve.wait_ge(gates, 3 * n + 2)
                    if b >= 2 and u == 0:
                        dve.wait_ge(out_mm, TPB * (b - 1))
                    keepg, add = c[:, u % 2], z[:, u % 2]
                    if u >= DC:
                        keepg, add = c[:, u % 2, ::-1], z[:, u % 2, ::-1]
                    dve.tensor_tensor_scan(hT[:, b % 2, u], keepg, add, 0.0, ALU.mult, ALU.add).then_inc(h_ready, 1)

                def residual(b):
                    dve.wait_ge(xb_ready, b + 1)
                    xb = x_all[:, b * TPB:(b + 1) * TPB, :]
                    if b < BATCH - 1:
                        for n in range(2):
                            dve.wait_ge(out_mm, TPB * b + 2 * (n + 1))
                            last = dve.tensor_tensor(xb[:, 2 * n:2 * n + 2], pO[:, n], xb[:, 2 * n:2 * n + 2], ALU.add)
                    else:
                        for t in range(TPB):
                            dve.wait_ge(out_mm, TPB * b + t + 1)
                            last = dve.tensor_tensor(xb[:, t], last_bank(t), xb[:, t], ALU.add)
                    last.then_inc(x2_ready, 1)
                    dve.wait_ge(x2_ready, b + 1)
                    if b < BATCH - 1:
                        moments(range(b * TPB, (b + 1) * TPB), mv2, stats2)

                for b in range(BATCH):
                    for u in range(UNITS):
                        n, way, ch = b * UNITS + u, u // DC, u % DC
                        dve.wait_ge(gates, 3 * n + 3)
                        hp = pP[:, (2 * n + 1) % 4]
                        dve.tensor_scalar(r[:, u % 2], hp, bias[:, 2 * way + 1, ch:ch + 1], 0.0,
                                          ALU.add, ALU.max).then_inc(relu_ready, 1)
                        dve.wait_ge(relu_ready, n + 1)
                        if n >= 2:
                            dve.wait_ge(zg_ready, n - 1)
                        dve.scalar_tensor_tensor(out=g[:, u % 2], in0=sg[:, u % 2], scalar=0.5, in1=r[:, u % 2],
                                                 op0=ALU.min, op1=ALU.add).then_inc(g_ready, 1)
                        if n >= 1:
                            scan((n - 1) // UNITS, (n - 1) % UNITS)
                        if u == 0 and b + 2 < BATCH:
                            normalise(b + 2)
                        if u == 2 and b + 1 < BATCH:
                            low(b + 1)
                        if u == 0 and b >= 2:
                            residual(b - 2)
                            if b == 2:
                                dve.tensor_scalar(ve[:, 0:TPB], mv2[:, 0:TPB, 1], LN_EPS, None, ALU.add)\
                                    .then_inc(ve2_ready, 1)
                    if b == BATCH - 1:
                        residual(b - 1)
                scan(BATCH - 1, UNITS - 1)
                dve.wait_ge(root_ready, 3)
                link(rstd_tail(dve, link, ve[:, 0:TPB], root[:, 0:TPB], y0[:, 0:TPB], t0[:, 0:TPB], u0[:, 0:TPB],
                               rstd[:, 0:TPB]))
                dve.wait_ge(xT_mm, BATCH - 1)
                for t in range(TPB):
                    last = dve.tensor_scalar(xn[:, 0, t], x_all[:, t], mv2[:, t, 0:1], rstd[:, t:t + 1],
                                             ALU.subtract, ALU.mult)
                last.then_inc(xn_ready, 1)
                for k in range(DC):
                    dve.wait_ge(x0_high, k + 1)
                    dve.tensor_tensor(xTl[:, 0, k], pP[:, k], xTh[:, 0, k].bitcast(F32), ALU.subtract).then_inc(x0_low, 1)
                residual(BATCH - 1)
                for k in range(DC):
                    dve.wait_ge(q0_high, k + 1)
                    dve.tensor_tensor(q0l[:, k], pP[:, 2 + k], q0h[:, k].bitcast(F32), ALU.subtract)

            @block.tensor
            def _(pe):
                pe.wait_ge(ident_ready, 1)
                pe.wait_ge(ld_wa, 48)
                for ch in range(DC):
                    for k in range(DC):
                        last = pe.matmul(pP[:, ch, 0:D], wa[:, 0, k, ch * P:(ch + 1) * P], wa[:, 1, k],
                                         start=(k == 0), stop=(k == DC - 1))
                last.then_inc(prep_mm, 1)

                def transposes(b):
                    pe.wait_ge(xn_ready, b + 1)
                    if b >= 1:
                        pe.wait_ge(xTl_ready, b)
                    for k in range(DC):
                        for t in range(TPB):
                            last = pe.transpose(pT[:, k, t * P:(t + 1) * P], xn[:, b % 2, t, k * P:(k + 1) * P],
                                                ident[:])
                    last.then_inc(xT_mm, 1)

                def output(b, t):
                    if t == 0:
                        pe.wait_ge(h_ready, UNITS * (b + 1))
                        if b >= 1:
                            pe.wait_ge(x2_ready, b)
                    for k in range(2 * DC):
                        last = pe.matmul(pO[:, t // 2, t % 2], hT[:, b % 2, k, t * P:(t + 1) * P], wout[:, k],
                                         start=(k == 0), stop=(k == 2 * DC - 1))
                    last.then_inc(out_mm, 1)

                def last_output(b):
                    pe.wait_ge(x2_ready, b)
                    for k in range(2 * DC):
                        if k == 2 * DC - 2:
                            pe.wait_ge(xn_ready, BATCH + 1)
                            pe.wait_ge(gates, 3 * BATCH * UNITS)
                            pe.wait_ge(relu_ready, BATCH * UNITS)
                            for c in range(DC):
                                for t in range(TPB):
                                    mm = pe.transpose(pP[:, c, t * P:(t + 1) * P], xn[:, 0, t, c * P:(c + 1) * P],
                                                      ident[:])
                                mm.then_inc(x0_mm, 1)
                        pe.wait_ge(h_ready, UNITS * b + k + 1)
                        for t in range(TPB):
                            mm = pe.matmul(last_bank(t), hT[:, b % 2, k, t * P:(t + 1) * P], wout[:, k],
                                           start=(k == 0), stop=(k == 2 * DC - 1))
                            if k == 2 * DC - 1:
                                mm.then_inc(out_mm, 1)

                transposes(0)
                pe.wait_ge(ld_wout, 16)
                pe.wait_ge(wl_ready, 4)
                pe.wait_ge(prep_lo, 2)
                for b in range(BATCH):
                    pe.wait_ge(xTl_ready, b + 1)
                    for j in range(2 * UNITS):
                        n = 2 * UNITS * b + j
                        way, ch, m = j // (2 * DC), (j // 2) % DC, j % 2
                        if n >= 4:
                            if m == 0:
                                pe.wait_ge(gates, 3 * ((n - 4) // 2) + 2)
                            else:
                                pe.wait_ge(gates, 3 * ((n - 4) // 2) + 3)
                                pe.wait_ge(relu_ready, (n - 4) // 2 + 1)
                        cols = slice(ch * P, (ch + 1) * P)
                        split_products(pe, pP[:, n % 4], [
                            ((wh[:, 2 * way + m, k, cols], wl[:, 2 * way + m, k, cols]),
                             (xTh[:, b % 2, k], xTl[:, b % 2, k])) for k in range(DC)]).then_inc(proj_mm, 1)
                        if j == UNITS - 1 and b + 1 < BATCH:
                            transposes(b + 1)
                        if j >= UNITS and b >= 1:
                            output(b - 1, j - UNITS)
                last_output(BATCH - 1)
                pe.wait_ge(x0_low, DC)
                for c in range(DC):
                    split_products(pe, pP[:, 2 + c], [
                        ((Mh[:, k, c * P:(c + 1) * P], Ml[:, k, c * P:(c + 1) * P]), (xTh[:, 0, k], xTl[:, 0, k]))
                        for k in range(DC)]).then_inc(q0_mm, 1)


def stage_attention(nc, keep, d):
    x_all, ident, mv2, mv3 = keep["x"], keep["ident"], keep["mv2"], keep["mv3"]
    Mh, Ml, WvTh, WvTl = keep["Mh"], keep["Ml"], keep["WvTh"], keep["WvTl"]
    cTh, cTl, cNh, cNl = keep["cTh"], keep["cTl"], keep["cNh"], keep["cNl"]
    xT, qT0 = keep["xT0"], keep["qT0"]
    KB = -(-CPAD // SEQ)
    RING = 3
    GROUPS = [range(i, min(i + 4, CT)) for i in range(0, CT, 4)]
    NG = len(GROUPS)

    def at_tile(g):
        out = []
        if 0 <= g - 2 < TILES:
            out.append(("V", g - 2, 0))
        if 0 <= g - 1 < TILES:
            out += [("P", g - 1, 0), ("P", g - 1, 1)]
        if 0 <= g < TILES:
            out.append(("E", g, 0))
        if 0 <= g - 2 < TILES:
            out.append(("O", g - 2, 0))
        if 0 <= g - 1 < TILES:
            out += [("P", g - 1, 2), ("A", g - 1, 0), ("P", g - 1, 3), ("A", g - 1, 1), ("A", g - 1, 2), ("A", g - 1, 3)]
        b = g // TPB + 1
        if b < BATCH and g % TPB == 1:
            out += [("X", b, 0), ("X", b, 1)]
        if b < BATCH and g % TPB == 2:
            out += [("Q", b, 0), ("Q", b, 1)]
        if g == TILES:
            out += [("X", BATCH, 0), ("X", BATCH, 1)]
        return out

    SLOTS = [at_tile(g) for g in range(TILES + 2)]
    ring = [it for slot in SLOTS for it in slot if it[0] not in "EA"]
    place = {it: n for n, it in enumerate(ring)}
    halved = {it: n for n, it in enumerate([it for it in ring if it[0] != "O"])}

    with ExitStack() as ctx:
        st = Stage(nc, ctx, "att")
        ve, root, y0, t0, u0, rstd = (st.sb(n, [P, TILES]) for n in ("ve", "root", "y0", "t0", "u0", "rstd"))
        xn = st.sb("xn", [P, TPB, D])
        qT1 = [st.sb(n, [P, DC, SEQ], F32R) for n in ("qT1h", "qT1l")]
        qT = (qT0, qT1)
        prob = st.sb("prob", [P, 2, CTX])
        pT = [st.sb(n, [P, CT, P], F32R) for n in ("pTh", "pTl")]
        vT = [st.sb(n, [P, 2, DC, P], F32R) for n in ("vTh", "vTl")]
        val = st.sb("val", [P, 2, D])
        mx = st.sb("mx", [P, 2, KB])
        nmax = st.sb("nmax", [P, 2])
        tmax = st.sb("tmax", [P, 2])
        rowsum = st.sb("rowsum", [P, 2])
        rinv = st.sb("rinv", [P, 2])
        stats = st.sb("stats", [P, TILES, 6])
        pS = st.ps("pS", [P, KB * SEQ])
        pA = st.ps("pA", [P, SEQ])
        pR = st.ps("pR", [P, RING, SEQ])

        dve_chain, root_ready, ve_ready, xn_ready = (st.sem(n) for n in ("dve_chain", "root_ready", "ve_ready", "xn_ready"))
        ld_piece = [st.sem(f"ld_piece{n}") for n in range(RAW)]
        piece_hi, piece_lo, pad_set = st.sem("piece_hi"), st.sem("piece_lo"), st.sem("pad_set")
        bank_full, bank_high, bank_free = st.sem("bank_full"), st.sem("bank_high"), st.sem("bank_free")
        score_mm, max_ready, exp_ready, rinv_ready = (st.sem(n) for n in ("score_mm", "max_ready", "exp_ready", "rinv_ready"))
        value_mm, val_ready, x3_ready = st.sem("value_mm"), st.sem("val_ready"), st.sem("x3_ready")
        pieces = [p for b in range(1, BATCH) for p in context_pieces(d, keep, b)]
        for k in range(DC):
            pieces.append((d["fWq"][k * P:(k + 1) * P, :], lambda s: keep["raw"][:, s], keep["wqh"][:, k], keep["wql"][:, k]))

        def pieces_at(g):
            b, q = g // TPB, -(-PIECES // TPB)
            if b + 1 >= BATCH:
                n = PIECES * (BATCH - 1) + g - TPB * (BATCH - 1)
                return range(n, min(n + 1, len(pieces)))
            return range(b * PIECES + min(q * (g % TPB), PIECES), b * PIECES + min(q * (g % TPB + 1), PIECES))

        def half(it, which, n):
            kind, a, i = it
            bank = pR[:, n % RING]
            if kind == "X":
                return xT[which][:, i], bank
            if kind == "Q":
                return qT[a % 2][which][:, i], bank
            if kind == "P":
                rows = CLAST if GROUPS[i][-1] == CT - 1 else P
                m = len(GROUPS[i])
                return pT[which][0:rows, GROUPS[i][0]:GROUPS[i][0] + m], \
                    bank[0:rows, 0:m * P].rearrange("p (t n) -> p t n", n=P)
            return vT[which][:, a % 2], bank[:, 0:DC * P].rearrange("p (t n) -> p t n", n=P)

        def wait_overwrite(eng, it):
            kind, a, i = it
            if kind == "X" and a >= 2:
                eng.wait_ge(bank_full, place[("Q", a - 1, DC - 1)] + 1)
            elif kind == "Q" and a >= 2:
                eng.wait_ge(score_mm, KB * TPB * (a - 1))
            elif kind == "P" and a >= 1:
                eng.wait_ge(value_mm, NG * (a - 1) + i + 1)
            elif kind == "V" and a >= 2:
                eng.wait_ge(bank_full, place[("O", a - 2, 0)] + 1)

        with nc.Block() as block:
            @block.sync
            def _(sp):
                for n, (src, raw, _, _) in enumerate(pieces):
                    if n >= RAW:
                        sp.wait_ge(piece_lo, n - RAW + 1)
                    sp.dma_start(raw(n % RAW), src).then_inc(ld_piece[n % RAW], 16)

            @block.gpsimd
            def _(pool):
                for m in (cTh[1], cTl[1]):
                    pool.memset(m[:, :, CTX:CPAD].bitcast(F32), 0.0).then_inc(pad_set, 1)
                for g in range(TILES):
                    for i in pieces_at(g):
                        pool.wait_ge(piece_hi, i + 1)
                        b = i // PIECES + 1
                        if 2 <= b < BATCH:
                            pool.wait_ge(value_mm, NG * TPB * (b - 1))
                        _, raw, hi, lo = pieces[i]
                        pool.tensor_tensor(lo, raw(i % RAW), hi.bitcast(F32), ALU.subtract).then_inc(piece_lo, 1)

            @block.scalar
            def _(act):
                act.wait_ge(ve_ready, 1)
                act.activation(root[:, TPB:], ve[:, TPB:], ACT.Sqrt).then_inc(root_ready, 1)

                def high(it):
                    n = place[it]
                    act.wait_ge(bank_full, n + 1)
                    wait_overwrite(act, it)
                    to, bank = half(it, 0, n)
                    act.activation(to, bank, ACT.Copy).then_inc(bank_high, 1)

                def values(g):
                    act.wait_ge(value_mm, NG * (g + 1))
                    act.wait_ge(rinv_ready, g + 1)
                    if g >= 2:
                        act.wait_ge(bank_full, place[("V", g - 2, 0)] + 1)
                    act.activation(val[:, g % 2], pA[:, 0:D], ACT.Copy, scale=rinv[:, g % 2:g % 2 + 1])\
                        .then_inc(val_ready, 1)

                for g in range(TILES + 2):
                    if 0 <= g - 2 < TILES:
                        values(g - 2)
                    for it in SLOTS[g]:
                        if it[0] == "E":
                            act.wait_ge(max_ready, g + 1)
                            if g >= 2:
                                act.wait_ge(bank_full, place[("P", g - 2, NG - 1)] + 1)
                                act.wait_ge(rinv_ready, g - 1)
                            act.activation(prob[:, g % 2], pS[:, 0:CTX], ACT.Exp, bias=nmax[:, g % 2:g % 2 + 1],
                                           scale=ATT_SCALE, accum_out=rowsum[:, g % 2:g % 2 + 1]).then_inc(exp_ready, 1)
                        elif it[0] not in "AO":
                            high(it)
                    if g < TILES:
                        for i in pieces_at(g):
                            act.wait_ge(ld_piece[i % RAW], 16 * (i // RAW + 1))
                            b = i // PIECES + 1
                            if 2 <= b < BATCH:
                                act.wait_ge(value_mm, NG * TPB * (b - 1))
                            _, raw, hi, _ = pieces[i]
                            act.activation(hi, raw(i % RAW), ACT.Copy).then_inc(piece_hi, 1)
                    if g == TILES - 1:
                        act.wait_ge(ve_ready, 2)
                        act.activation(root[:, 0:TPB], ve[:, 0:TPB], ACT.Sqrt).then_inc(root_ready, 1)

            @block.vector
            def _(dve):
                chained = [0]

                def link(ins):
                    chained[0] += 1
                    ins.then_inc(dve_chain, 1)
                    dve.wait_ge(dve_chain, chained[0])

                def inverse_roots(a, e):
                    return rstd_tail(dve, link, ve[:, a:e], root[:, a:e], y0[:, a:e], t0[:, a:e], u0[:, a:e],
                                     rstd[:, a:e])

                def normalise(b):
                    if b >= 2:
                        dve.wait_ge(bank_full, place[("X", b - 1, DC - 1)] + 1)
                    for t in range(TPB):
                        i = (b % BATCH) * TPB + t
                        mv = mv2 if b < BATCH else mv3
                        last = dve.tensor_scalar(xn[:, t], x_all[:, i], mv[:, i, 0:1], rstd[:, i:i + 1],
                                                 ALU.subtract, ALU.mult)
                    last.then_inc(xn_ready, 1)

                def low(it):
                    n = place[it]
                    dve.wait_ge(bank_high, halved[it] + 1)
                    wait_overwrite(dve, it)
                    to, bank = half(it, 1, n)
                    dve.tensor_tensor(to, bank, half(it, 0, n)[0].bitcast(F32), ALU.subtract).then_inc(bank_free, 1)

                def output(g):
                    n = place[("O", g, 0)]
                    dve.wait_ge(bank_full, n + 1)
                    dve.tensor_tensor(x_all[:, g], pR[:, n % RING, 0:D], x_all[:, g], ALU.add).then_inc(bank_free, 1)
                    dve.wait_ge(bank_free, n + 1)
                    link(dve.bn_stats(stats[:, g], x_all[:, g]))
                    dve.bn_aggr(mv3[:, g], stats[:, g]).then_inc(x3_ready, 1)

                def row_max(g):
                    h = g % 2
                    for j in range(KB):
                        dve.wait_ge(score_mm, KB * g + j + 1)
                        last = dve.tensor_reduce(mx[:, h, j:j + 1], pS[:, j * SEQ:min((j + 1) * SEQ, CTX)], AX.X, ALU.max)
                    link(last)
                    link(dve.tensor_reduce(tmax[:, h:h + 1], mx[:, h], AX.X, ALU.max))
                    dve.tensor_scalar(nmax[:, h:h + 1], tmax[:, h:h + 1], -ATT_SCALE, None, ALU.mult).then_inc(max_ready, 1)

                for t in range(TILES - TPB, TILES):
                    last = dve.bn_stats(stats[:, t], x_all[:, t])
                link(last)
                for t in range(TILES - TPB, TILES):
                    last = dve.bn_aggr(mv2[:, t], stats[:, t])
                link(last)
                dve.tensor_scalar(ve[:, TPB:], mv2[:, TPB:, 1], LN_EPS, None, ALU.add).then_inc(ve_ready, 1)
                for g in range(TILES + 2):
                    if 0 <= g - 1 < TILES:
                        dve.wait_ge(exp_ready, g)
                        if g >= 3:
                            dve.wait_ge(val_ready, g - 2)
                        dve.reciprocal(rinv[:, (g - 1) % 2:(g - 1) % 2 + 1], rowsum[:, (g - 1) % 2:(g - 1) % 2 + 1])\
                            .then_inc(rinv_ready, 1)
                    if g < TILES:
                        row_max(g)
                    for it in SLOTS[g]:
                        if it[0] == "O":
                            output(it[1])
                        elif it[0] not in "AE":
                            low(it)
                    if g == 0:
                        dve.wait_ge(root_ready, 1)
                        link(inverse_roots(TPB, TILES))
                    if g % TPB == 0 and g // TPB + 1 < BATCH:
                        normalise(g // TPB + 1)
                    if g == TPB + 1:
                        dve.wait_ge(x3_ready, TPB)
                        dve.tensor_scalar(ve[:, 0:TPB], mv3[:, 0:TPB, 1], LN_EPS, None, ALU.add).then_inc(ve_ready, 1)
                    if g == TILES - 1:
                        dve.wait_ge(root_ready, 2)
                        link(inverse_roots(0, TPB))
                        normalise(BATCH)

            @block.tensor
            def _(pe):
                def scores(g):
                    b, t = g // TPB, g % TPB
                    if b >= 1:
                        pe.wait_ge(bank_free, place[("Q", b, DC - 1)] + 1)
                    if b >= 1 and t == 0:
                        pe.wait_ge(piece_lo, PIECES * b)
                        pe.wait_ge(pad_set, 2)
                    if g >= 1:
                        pe.wait_ge(exp_ready, g)
                    for j in range(KB):
                        a, e = j * SEQ, min((j + 1) * SEQ, CPAD)
                        split_products(pe, pS[:, a:e], [
                            (tuple(q[:, k, t * P:(t + 1) * P] for q in qT[b % 2]),
                             (cTh[b % 2][:, k, a:e], cTl[b % 2][:, k, a:e])) for k in range(DC)]).then_inc(score_mm, 1)

                def item(it):
                    kind, a, i = it
                    if kind == "A":
                        pe.wait_ge(bank_free, place[("P", a, i)] + 1)
                        if i == 0 and a >= 1:
                            pe.wait_ge(val_ready, a)
                        for kt in GROUPS[i]:
                            rows, par = (CLAST if kt == CT - 1 else P), (a // TPB) % 2
                            l = [p[0:rows, kt] for p in pT]
                            r = [c[par][0:rows, kt] for c in (cNh, cNl)]
                            pe.matmul(pA[:, 0:D], l[0], r[0], start=(kt == 0), stop=False)
                            pe.matmul(pA[:, 0:D], l[0], r[1], start=False, stop=False)
                            last = pe.matmul(pA[:, 0:D], l[1], r[0], start=False, stop=(kt == CT - 1))
                        last.then_inc(value_mm, 1)
                        return
                    n = place[it]
                    if n >= RING:
                        pe.wait_ge(bank_free, n - RING + 1)
                    bank = pR[:, n % RING]
                    if kind == "X":
                        pe.wait_ge(xn_ready, a)
                        for t in range(TPB):
                            last = pe.transpose(bank[:, t * P:(t + 1) * P], xn[:, t, i * P:(i + 1) * P], ident[:])
                    elif kind == "Q":
                        pe.wait_ge(bank_free, place[("X", a, DC - 1)] + 1)
                        last = split_products(pe, bank, [
                            ((Mh[:, k, i * P:(i + 1) * P], Ml[:, k, i * P:(i + 1) * P]), (xT[0][:, k], xT[1][:, k]))
                            for k in range(DC)])
                    elif kind == "P":
                        pe.wait_ge(exp_ready, a + 1)
                        for m, kt in enumerate(GROUPS[i]):
                            rows = CLAST if kt == CT - 1 else P
                            last = pe.transpose(bank[0:rows, m * P:(m + 1) * P], prob[:, a % 2, kt * P:kt * P + rows],
                                                ident[:])
                    elif kind == "V":
                        pe.wait_ge(val_ready, a + 1)
                        for k in range(DC):
                            last = pe.transpose(bank[:, k * P:(k + 1) * P], val[:, a % 2, k * P:(k + 1) * P], ident[:])
                    else:
                        pe.wait_ge(bank_free, place[("V", a, 0)] + 1)
                        last = split_products(pe, bank[:, 0:D], [
                            ((vT[0][:, a % 2, k], vT[1][:, a % 2, k]), (WvTh[:, k], WvTl[:, k])) for k in range(DC)])
                    last.then_inc(bank_full, 1)

                for g in range(TILES + 2):
                    if g < TILES:
                        scores(g)
                    for it in SLOTS[g]:
                        if it[0] != "E":
                            item(it)


def stage_ffn(nc, keep, d):
    x_all, ident, mv3 = keep["x"], keep["ident"], keep["mv3"]
    wqh, wql = keep["wqh"], keep["wql"]
    PER = 2
    GROUPS = TILES // PER
    HALVES = 2 * HEADS
    ROW = KEYS + TOPK
    ABOVE = 8.0
    FIRSTS = EXPERTS // KEYS
    COLS = PER * P
    WEIGH, SUM = 5, 3
    PB = 3
    QS = BATCH * QC
    ES = BATCH * DC
    with ExitStack() as ctx:
        st = Stage(nc, ctx, "ffn")
        down = st.sb("down", [P, DC, D])
        dnh, dnl = (st.sb(n, [P, DC, D], F32R) for n in ("dnh", "dnl"))
        up = st.sb("up", [P, DC, D])
        bq = st.sb("bq", [P, QC])
        affine = st.sb("affine", [P, 2])
        key = st.sb("key", [P, P])
        keysq, keyn, keyT = st.sb("keysq", [P, P]), st.sb("keyn", [P, P]), st.sb("keyT", [P, P])
        k2, kroot, ky, kt, ku, kinv = (st.sb(n, [P, 1]) for n in ("k2", "kroot", "ky", "kt", "ku", "kinv"))
        pair = st.sb("pair", [P, P])
        group_of = st.sb("group_of", [P, 4])
        ve, root, y0, t0, u0, rstd = (st.sb(n, [P, TILES]) for n in ("ve", "root", "y0", "t0", "u0", "rstd"))
        xn = st.sb("xn", [P, 2, TPB, D])
        xTs = [keep["xT0"]] + [[st.sb(f"xT{b}{n}", [P, DC, SEQ], F32R) for n in "hl"] for b in range(1, BATCH)]
        qT = st.sb("qT", [P, QC, TOKENS])
        gT = st.sb("gT", [P, DC, TOKENS])
        stats = st.sb("stats", [P, QS, 6])
        mv, avg = st.sb("mv", [P, 2]), st.sb("avg", [P, 2])
        nmean, diff, bve, broot, by, bt, bu, brstd = (
            st.sb(n, [P, 1]) for n in ("nmean", "diff", "bve", "broot", "by", "bt", "bu", "brstd"))
        bn = st.sb("bn", [P, 2])
        sq = st.sb("sq", [P, QC, COLS])
        n2, nroot, ny, nt, nu, ninv = (st.sb(n, [P, 2, PER * HALVES]) for n in ("n2", "nroot", "ny", "nt", "nu", "ninv"))
        s = st.sb("s", [P, 2, PER, HALVES, ROW])
        picked = st.sb("picked", [P, PER, HALVES, ROW])
        top = st.sb("top", [P, 2, PER, HALVES, 2 * TOPK])
        e = st.sb("e", [P, 2, PER, HALVES, KEYS])
        etop = st.sb("etop", [P, 2, PER, HALVES, TOPK])
        total = st.sb("total", [P, PER, HEADS, 2])
        inv = st.sb("inv", [P, PER, HEADS, 2])
        both = st.sb("both", [P, PER * HEADS])
        raw1 = st.sb("raw1", [P, PER * HEADS, FIRSTS])
        sum1, rest, restn = (st.sb(n, [P, PER, HEADS]) for n in ("sum1", "rest", "restn"))
        first = st.sb("first", [P, 2, PER, HEADS, FIRSTS])
        second = st.sb("second", [P, 2, PER, HEADS, KEYS])
        clamped = st.sb("clamped", [P, 2, PER])
        prod = st.sb("prod", [P, PB, HEADS, EXPERTS])
        hT = st.sb("hT", [P, 2, DC, P])
        y = st.sb("y", [P, 2, D])
        pT = pW = st.ps("pT", [P, DC, SEQ])
        pO = st.ps("pO", [P, 2, SEQ])
        pS = st.ps("pS", [P, 2, SEQ])
        pK = pN = st.ps("pK", [P, SEQ])
        pB = st.ps("pB", [P, SEQ])

        def query_bank(n):
            return pO[:, n % 4] if n % 4 < 2 else pS[:, n % 4 - 2]

        def expert_bank(m):
            return pO[:, m % 4] if m % 4 < 2 else pT[:, m % 4 - 2]

        ld_down, ld_small, ld_key, ld_up = st.sem("ld_down"), st.sem("ld_small"), st.sem("ld_key"), st.sem("ld_up")
        zeroed, pair_ready, const_ready, dve_chain = (st.sem(n) for n in ("zeroed", "pair_ready", "const_ready", "dve_chain"))
        ve_ready, root_ready, down_high, down_low = (st.sem(n) for n in ("ve_ready", "root_ready", "down_high", "down_low"))
        keyn_ready, key_mm, key_ready = st.sem("keyn_ready"), st.sem("key_mm"), st.sem("key_ready")
        xn_ready, xT_mm, xTh_ready, xTl_ready = (st.sem(n) for n in ("xn_ready", "xT_mm", "xTh_ready", "xTl_ready"))
        query_mm, query_read, expert_mm, gelu_ready = (
            st.sem(n) for n in ("query_mm", "query_read", "expert_mm", "gelu_ready"))
        mv_ready, avg_mm, bn_ready = st.sem("mv_ready"), st.sem("avg_mm"), st.sem("bn_ready")
        sq_ready, norm_mm, n2_ready, nroot_ready = (
            st.sem(n) for n in ("sq_ready", "norm_mm", "n2_ready", "nroot_ready"))
        q_ready_dve, q_ready_pool, q_ready_act = (st.sem(n) for n in ("q_ready_dve", "q_ready_pool", "q_ready_act"))
        score_mm, s_ready, top_ready, e_ready, etop_ready = (
            st.sem(n) for n in ("score_mm", "s_ready", "top_ready", "e_ready", "etop_ready"))
        weights_ready, prod_ready, prod_done, weight_mm, h_ready, out_mm = (
            st.sem(n) for n in ("weights_ready", "prod_ready", "prod_done", "weight_mm", "h_ready", "out_mm"))
        out_read, y_ready, stored = st.sem("out_read"), st.sem("y_ready"), st.sem("stored")
        ADD = WEIGH + 2
        POOL_ADDS = TILES - WEIGH
        FIRST_POOL, FIRST_ACT = 2, 4
        LEFT = TILES - WEIGH + 1
        LASTS = TILES - PER
        SHARE = 5

        def wait_query(eng, n, chunks):
            if n < FIRST_POOL:
                eng.wait_ge(q_ready_dve, QC * n + chunks)
            elif n < FIRST_ACT:
                eng.wait_ge(q_ready_pool, QC * (n - FIRST_POOL) + chunks)
            else:
                eng.wait_ge(q_ready_act, QC * (n - FIRST_ACT) + chunks)

        def outer(eng, i, a, b):
            n, t = i // PER, i % PER
            shape = [P, b - a, FIRSTS, KEYS]
            return eng.tensor_tensor(prod[:, i % PB, a:b].rearrange("p h (i j) -> p h i j", j=KEYS),
                                     first[:, n % 2, t, a:b].unsqueeze(3).broadcast_to(shape),
                                     second[:, n % 2, t, a:b].unsqueeze(2).broadcast_to(shape), ALU.mult)

        with nc.Block() as block:
            @block.sync
            def _(sp):
                sp.dma_start(bq[:], d["fbq"]).then_inc(ld_small, 16)
                sp.dma_start(affine[:], d["bn"]).then_inc(ld_small, 16)
                sp.dma_start(down[:], d["downT"].rearrange("(k p) n -> p k n", p=P)).then_inc(ld_down, 16)
                sp.wait_ge(zeroed, 1)
                for h in range(2):
                    for half in range(2):
                        q = (2 * h + half) * HALF
                        sp.dma_start(key[q:q + HALF, q:q + HALF], d["keys"][half]).then_inc(ld_key, 16)
                sp.dma_start(up[:], d["up"].rearrange("(c p) n -> p c n", p=P)).then_inc(ld_up, 16)
                o = d["out"].rearrange("b (t p) d -> (b t) p d", p=P)
                for i in range(TILES):
                    sp.wait_ge(y_ready, i + 1)
                    sp.dma_start(o[i], x_all[:, i]).then_inc(stored, 16)
                sp.wait_ge(stored, 16 * TILES)

            @block.gpsimd
            def _(pool):
                pool.memset(key[:], 0.0).then_inc(zeroed, 1)
                pool.memset(pair[:], 0.0).then_inc(pair_ready, 1)
                pool.memset(group_of[:], 0.0).then_inc(const_ready, 1)
                for n, off in enumerate((0, QD, -QD)):
                    pool.wait_ge(pair_ready, n + 1)
                    pool.affine_select(out=pair[:], in_=pair[:], compare_op=ALU.not_equal, fill=0.5, base=off,
                                       pattern=[[-1, P]], channel_multiplier=1).then_inc(pair_ready, 1)
                pool.wait_ge(const_ready, 1)
                pool.wait_ge(pair_ready, 4)
                for q in range(4):
                    pool.memset(group_of[q * HALF:(q + 1) * HALF, q:q + 1], 1.0).then_inc(const_ready, 1)
                pool.wait_ge(const_ready, 5)
                pool.memset(s[:, :, :, :, KEYS:ROW], ABOVE).then_inc(const_ready, 1)

                pool.wait_ge(bn_ready, 1)
                for n in range(FIRST_POOL, FIRST_ACT):
                    for c in range(QC):
                        q = qT[:, c, n * COLS:(n + 1) * COLS]
                        pool.tensor_scalar(q, q, bn[:, 0:1], bn[:, 1:2], ALU.mult, ALU.add).then_inc(q_ready_pool, 1)

                def add_output(i):
                    pool.wait_ge(out_read, i + 1)
                    pool.tensor_tensor(x_all[:, i], y[:, i % 2], x_all[:, i], ALU.add).then_inc(y_ready, 1)

                for i in range(TILES):
                    n, t = i // PER, i % PER
                    if t == 0:
                        for j in range(max(i - ADD, 0), i - ADD + PER):
                            add_output(j)
                    pool.wait_ge(weights_ready, n + 1)
                    if i >= PB:
                        pool.wait_ge(weight_mm, i - PB + 1)
                    if i < LASTS:
                        outer(pool, i, 0, HEADS // 2).then_inc(prod_ready, 1)
                        pool.wait_ge(prod_ready, i + 1)
                        last = prod[:, i % PB, 0, EXPERTS - 1:EXPERTS]
                        pool.tensor_tensor(last, last, clamped[:, n % 2, t:t + 1], ALU.add).then_inc(prod_done, 1)
                        outer(pool, i, HEADS // 2, HEADS).then_inc(prod_done, 1)
                    else:
                        outer(pool, i, SHARE, HEADS).then_inc(prod_done, 1)
                for i in range(TILES - ADD, POOL_ADDS):
                    add_output(i)

            @block.scalar
            def _(act):
                act.wait_ge(ve_ready, 1)
                act.activation(root[:, TPB:], ve[:, TPB:], ACT.Sqrt).then_inc(root_ready, 1)

                def high(b):
                    act.wait_ge(xT_mm, b)
                    for k in range(DC):
                        last = act.activation(xTs[b][0][:, k], pT[:, k], ACT.Copy)
                    last.then_inc(xTh_ready, 1)

                act.wait_ge(ld_small, 32)
                for b in range(BATCH):
                    for j in range(QC):
                        n = b * QC + j
                        act.wait_ge(query_mm, n + 1)
                        act.activation(qT[:, j, b * SEQ:(b + 1) * SEQ], query_bank(n), ACT.Identity,
                                       bias=bq[:, j:j + 1]).then_inc(query_read, 1)
                        if j == 1 and b + 1 < BATCH:
                            high(b + 1)
                    if b == 0:
                        act.wait_ge(ve_ready, 2)
                        act.activation(kroot[:], k2[:], ACT.Sqrt).then_inc(root_ready, 1)
                        act.wait_ge(ld_down, 16)
                        act.activation(dnh[:], down[:], ACT.Copy).then_inc(down_high, 1)
                act.wait_ge(ve_ready, 3)
                act.activation(broot[:], bve[:], ACT.Sqrt).then_inc(root_ready, 1)

                def normed(n):
                    for c in range(QC):
                        q = qT[:, c, n * COLS:(n + 1) * COLS]
                        act.activation(q, q, ACT.Identity, scale=bn[:, 0:1], bias=bn[:, 1:2])\
                            .then_inc(q_ready_act, 1)

                def squared(n):
                    if n >= 1:
                        act.wait_ge(norm_mm, n)
                    for c in range(QC):
                        wait_query(act, n, c + 1)
                        last = act.activation(sq[:, c], qT[:, c, n * COLS:(n + 1) * COLS], ACT.Square)
                    last.then_inc(sq_ready, 1)

                def norm_root(n):
                    act.wait_ge(n2_ready, n + 1)
                    act.activation(nroot[:, n % 2], n2[:, n % 2], ACT.Sqrt).then_inc(nroot_ready, 1)

                def exponentials(i):
                    n, t = i // PER, i % PER
                    act.wait_ge(s_ready, i + 1)
                    if n >= 2:
                        act.wait_ge(weights_ready, n - 1)
                    act.activation(e[:, n % 2, t], s[:, n % 2, t, :, 0:KEYS], ACT.Exp).then_inc(e_ready, 1)

                def read_output(i):
                    act.wait_ge(out_mm, i + 1)
                    if i >= 2:
                        act.wait_ge(y_ready, i - 1)
                    act.activation(y[:, i % 2], pO[:, i % 2, 0:D], ACT.Copy).then_inc(out_read, 1)

                for n in range(2):
                    squared(n)
                    norm_root(n)
                squared(2)
                for n in range(GROUPS):
                    if n >= 1 and n + 1 < GROUPS:
                        if n + 1 >= FIRST_ACT:
                            normed(n + 1)
                        if n + 1 > 2:
                            squared(n + 1)
                    for t in range(PER):
                        i = PER * n + t
                        exponentials(i)
                        if i - WEIGH - 1 >= 0:
                            read_output(i - WEIGH - 1)
                    act.wait_ge(top_ready, PER * (n + 1))
                    act.activation(etop[:, n % 2], top[:, n % 2, :, :, TOPK:], ACT.Exp).then_inc(etop_ready, 1)
                    if n >= 1 and n + 1 < GROUPS:
                        norm_root(n + 1)
                    if n == 0:
                        for m in range(ES):
                            b, c = m // DC, m % DC
                            act.wait_ge(expert_mm, m + 1)
                            act.activation(gT[:, c, b * SEQ:(b + 1) * SEQ], expert_bank(m), ACT.Gelu)\
                                .then_inc(gelu_ready, 1)
                for i in range(TILES - WEIGH - 1, POOL_ADDS):
                    read_output(i)

            @block.vector
            def _(dve):
                chained = [0]

                def note(ins):
                    ins.then_inc(dve_chain, 1)
                    chained[0] += 1
                    return chained[0]

                def need(count):
                    dve.wait_ge(dve_chain, count)

                def link(ins):
                    need(note(ins))

                def normalise(b):
                    if b >= 3:
                        dve.wait_ge(xT_mm, b - 2)
                    for t in range(TPB):
                        i = b * TPB + t
                        last = dve.tensor_scalar(xn[:, b % 2, t], x_all[:, i], mv3[:, i, 0:1], rstd[:, i:i + 1],
                                                 ALU.subtract, ALU.mult)
                    last.then_inc(xn_ready, 1)

                def low(b):
                    dve.wait_ge(xTh_ready, b)
                    for k in range(DC):
                        last = dve.tensor_tensor(xTs[b][1][:, k], pT[:, k], xTs[b][0][:, k].bitcast(F32), ALU.subtract)
                    last.then_inc(xTl_ready, 1)

                dve.tensor_scalar(ve[:, TPB:], mv3[:, TPB:, 1], LN_EPS, None, ALU.add).then_inc(ve_ready, 1)
                dve.wait_ge(root_ready, 1)
                link(rstd_tail(dve, link, ve[:, TPB:], root[:, TPB:], y0[:, TPB:], t0[:, TPB:], u0[:, TPB:], rstd[:, TPB:]))
                normalise(1)
                dve.wait_ge(ld_key, 64)
                link(dve.tensor_tensor(keysq[:], key[:], key[:], ALU.mult))
                link(dve.tensor_reduce(ku[:], keysq[:], AX.X, ALU.add))
                dve.tensor_scalar(k2[:], ku[:], NORM_EPS ** 2, None, ALU.max).then_inc(ve_ready, 1)
                for b in range(BATCH):
                    for j in range(QC):
                        n = b * QC + j
                        dve.wait_ge(query_read, n + 1)
                        last = dve.bn_stats(stats[:, n], qT[:, j, b * SEQ:(b + 1) * SEQ])
                        if j == 1 and b + 1 < BATCH:
                            low(b + 1)
                            if b + 2 < BATCH:
                                normalise(b + 2)
                    if b == 0:
                        dve.wait_ge(ve_ready, 2)
                        dve.wait_ge(root_ready, 2)
                        link(rstd_tail(dve, link, k2[:], kroot[:], ky[:], kt[:], ku[:], kinv[:]))
                        dve.tensor_scalar(keyn[:], key[:], kinv[:], None, ALU.mult).then_inc(keyn_ready, 1)
                        dve.wait_ge(down_high, 1)
                        dve.tensor_tensor(dnl[:], down[:], dnh[:].bitcast(F32), ALU.subtract).then_inc(down_low, 1)
                    if b == 1:
                        dve.wait_ge(key_mm, 1)
                        dve.tensor_copy(keyT[:], pK[:, 0:P]).then_inc(key_ready, 1)
                link(last)
                dve.bn_aggr(mv[:], stats[:]).then_inc(mv_ready, 1)
                dve.wait_ge(avg_mm, 1)
                dve.tensor_scalar(avg[:, 1:2], pB[:, 1:2], BN_EPS, None, ALU.add)
                dve.tensor_scalar(nmean[:], pB[:, 0:1], -1.0, None, ALU.mult)
                link(dve.tensor_tensor(diff[:], mv[:, 0:1], pB[:, 0:1], ALU.subtract))
                dve.tensor_scalar(bve[:], diff[:], diff[:], avg[:, 1:2], ALU.mult, ALU.add).then_inc(ve_ready, 1)
                dve.wait_ge(ve_ready, 3)
                dve.wait_ge(root_ready, 3)
                link(rstd_tail(dve, link, bve[:], broot[:], by[:], bt[:], bu[:], brstd[:]))
                link(dve.tensor_tensor(bn[:, 0:1], affine[:, 0:1], brstd[:], ALU.mult))
                dve.tensor_scalar(bn[:, 1:2], bn[:, 0:1], nmean[:], affine[:, 1:2], ALU.mult, ALU.add).then_inc(bn_ready, 1)
                dve.wait_ge(bn_ready, 1)

                def normed(n):
                    for c in range(QC):
                        q = qT[:, c, n * COLS:(n + 1) * COLS]
                        dve.tensor_scalar(q, q, bn[:, 0:1], bn[:, 1:2], ALU.mult, ALU.add).then_inc(q_ready_dve, 1)

                def squares(n):
                    dve.wait_ge(norm_mm, n + 1)
                    dve.tensor_scalar(n2[:, n % 2], pN[:, 0:PER * HALVES], NORM_EPS ** 2, None, ALU.max)\
                        .then_inc(n2_ready, 1)

                def inverse_norm_steps(n):
                    h = n % 2
                    yy, t, u = ny[:, h], nt[:, h], nu[:, h]
                    dve.wait_ge(nroot_ready, n + 1)
                    a = note(dve.reciprocal(yy, nroot[:, h]))
                    yield
                    need(a)
                    a = note(dve.tensor_tensor(t, yy, yy, ALU.mult))
                    yield
                    need(a)
                    a = note(dve.scalar_tensor_tensor(out=u, in0=t, scalar=-0.5, in1=n2[:, h], op0=ALU.mult,
                                                      op1=ALU.mult))
                    yield
                    need(a)
                    norms_at.append(note(dve.scalar_tensor_tensor(out=ninv[:, h], in0=u, scalar=1.5, in1=yy,
                                                                  op0=ALU.add, op1=ALU.mult)))
                    yield

                def top_scores(i, between):
                    n, t = i // PER, i % PER
                    h = n % 2
                    dve.wait_ge(score_mm, i + 1)
                    need(norms_at[n])
                    if n >= 2:
                        dve.wait_ge(e_ready, PER * (n - 1))
                    scale = ninv[:, h, t * HALVES:(t + 1) * HALVES].unsqueeze(2).broadcast_to([P, HALVES, KEYS])
                    dve.tensor_tensor(s[:, h, t, :, 0:KEYS], pS[:, i % 2].rearrange("p (g k) -> p g k", k=KEYS),
                                      scale, ALU.mult).then_inc(s_ready, 1)
                    between()
                    dve.wait_ge(s_ready, i + 1)
                    if n >= 2:
                        dve.wait_ge(etop_ready, n - 1)
                    for g in range(HALVES):
                        last = dve.max(top[:, h, t, g], s[:, h, t, g])
                    last.then_inc(top_ready, 1)
                    dve.wait_ge(top_ready, i + 1)
                    for g in range(HALVES):
                        last = dve.match_replace(picked[:, t, g], top[:, h, t, g], s[:, h, t, g], ABOVE)
                    picked_at.append(note(last))

                def weights(n, norm_step):
                    h = n % 2
                    mark = picked[:].rearrange("p t (h s) k -> p (t h) s k", s=2)
                    ex = e[:, h].rearrange("p t (h s) k -> p (t h) s k", s=2)
                    dve.wait_ge(etop_ready, n + 1)
                    sums = note(dve.tensor_reduce(total[:].rearrange("p t h s -> p (t h s)"),
                                                  etop[:, h].rearrange("p t g k -> p (t g) k"), AX.X, ALU.add))
                    dve.wait_ge(e_ready, PER * (n + 1))
                    need(picked_at[PER * n + PER - 1])
                    own = note(dve.scalar_tensor_tensor(out=raw1[:], in0=mark[:, :, 0, 0:FIRSTS], scalar=ABOVE / 2,
                                                        in1=ex[:, :, 0, 0:FIRSTS], op0=ALU.is_gt, op1=ALU.mult))
                    need(sums)
                    inverse = note(dve.reciprocal(inv[:], total[:]))
                    if n >= 2:
                        dve.wait_ge(prod_done, 2 * PER * (n - 1))
                    dve.scalar_tensor_tensor(out=second[:, h].rearrange("p t h k -> p (t h) k"),
                                             in0=mark[:, :, 1, 0:KEYS], scalar=ABOVE / 2, in1=ex[:, :, 1],
                                             op0=ALU.is_gt, op1=ALU.mult)
                    need(own)
                    owned = note(dve.tensor_reduce(sum1[:].rearrange("p t h -> p (t h)"), raw1[:], AX.X, ALU.add))
                    need(inverse)
                    product = note(dve.tensor_tensor(both[:].rearrange("p (t h) -> p t h", t=PER), inv[:, :, :, 0],
                                                     inv[:, :, :, 1], ALU.mult))
                    next(norm_step)
                    need(owned)
                    left = note(dve.tensor_tensor(rest[:], total[:, :, :, 0], sum1[:], ALU.subtract))
                    next(norm_step)
                    need(left)
                    left = note(dve.tensor_tensor(restn[:], rest[:], inv[:, :, :, 0], ALU.mult))
                    next(norm_step)
                    need(left)
                    dve.tensor_reduce(clamped[:, h], restn[:], AX.X, ALU.add)
                    need(product)
                    dve.tensor_tensor(first[:, h].rearrange("p t h i -> p (t h) i"), raw1[:],
                                      both[:].unsqueeze(2).broadcast_to([P, PER * HEADS, FIRSTS]),
                                      ALU.mult).then_inc(weights_ready, 1)
                    next(norm_step)

                def shared_products(i):
                    n, t = i // PER, i % PER
                    dve.wait_ge(weights_ready, n + 1)
                    dve.wait_ge(weight_mm, i - PB + 1)
                    a = note(outer(dve, i, 0, 1))
                    outer(dve, i, 1, SHARE)
                    last = prod[:, i % PB, 0, EXPERTS - 1:EXPERTS]
                    need(a)
                    dve.tensor_tensor(last, last, clamped[:, n % 2, t:t + 1], ALU.add).then_inc(prod_done, 1)

                def weigh(i):
                    dve.wait_ge(weight_mm, i + 1)
                    if i >= 2:
                        dve.wait_ge(out_mm, i - 1)
                    dve.tensor_tensor(hT[:, i % 2], pW[:, i % 2, 0:DC * P].rearrange("p (c n) -> p c n", n=P),
                                      gT[:, :, i * P:(i + 1) * P], ALU.mult).then_inc(h_ready, 1)

                def output(i):
                    dve.wait_ge(out_mm, i + 1)
                    dve.wait_ge(y_ready, i)
                    dve.tensor_tensor(x_all[:, i], pO[:, i % 2, 0:D], x_all[:, i], ALU.add).then_inc(y_ready, 1)

                norms_at, picked_at = [], []
                normed(0)
                normed(1)
                squares(0)
                for _ in inverse_norm_steps(0):
                    pass
                dve.wait_ge(const_ready, 6)
                for i in range(TILES):
                    n, t = i // PER, i % PER
                    top_scores(i, lambda: weigh(i - WEIGH) if i >= WEIGH else squares(1) if i == 0 else None)
                    if i == TILES - 1:
                        weigh(i - WEIGH + 1)
                    if t == PER - 1:
                        if 1 <= n and n + 1 < GROUPS:
                            squares(n + 1)
                        weights(n, inverse_norm_steps(n + 1) if n + 1 < GROUPS else iter(range(PER * 2)))
                for i in range(LEFT, TILES):
                    if i - LEFT < PER:
                        shared_products(LASTS + i - LEFT)
                    weigh(i)
                    if i - 1 >= POOL_ADDS:
                        output(i - 1)
                output(TILES - 1)

            @block.tensor
            def _(pe):
                def transposes(b):
                    pe.wait_ge(xn_ready, b)
                    if b >= 2:
                        pe.wait_ge(xTl_ready, b - 1)
                    for k in range(DC):
                        for t in range(TPB):
                            last = pe.transpose(pT[:, k, t * P:(t + 1) * P], xn[:, b % 2, t, k * P:(k + 1) * P],
                                                ident[:])
                    last.then_inc(xT_mm, 1)

                def expert_product(m):
                    b, c = m // DC, m % DC
                    if m < 2:
                        pe.wait_ge(query_read, QS - 3 + m)
                    elif m < 4:
                        pe.wait_ge(xTl_ready, BATCH - 1)
                    else:
                        pe.wait_ge(gelu_ready, m - 3)
                    split_products(pe, expert_bank(m), [
                        ((dnh[:, k, c * P:(c + 1) * P], dnl[:, k, c * P:(c + 1) * P]), (xTs[b][0][:, k], xTs[b][1][:, k]))
                        for k in range(DC)]).then_inc(expert_mm, 1)

                def norms(n):
                    pe.wait_ge(sq_ready, n + 1)
                    if n >= 1:
                        pe.wait_ge(n2_ready, n)
                    for t in range(PER):
                        for c in range(QC):
                            a = t * HALVES + 4 * c
                            last = pe.matmul(pN[:, a:a + 4], sq[:, c, t * P:(t + 1) * P], group_of[:], start=True, stop=True)
                    last.then_inc(norm_mm, 1)

                def scores(i):
                    wait_query(pe, i // PER, QC)
                    if i >= 2:
                        pe.wait_ge(s_ready, i - 1)
                    for c in range(QC):
                        last = pe.matmul(pS[:, i % 2, c * P:(c + 1) * P], qT[:, c, i * P:(i + 1) * P], keyT[:],
                                         start=True, stop=True)
                    last.then_inc(score_mm, 1)

                def sum_heads(i):
                    if i >= 2:
                        pe.wait_ge(h_ready, i - 1)
                    pe.wait_ge(prod_done, 2 * (i + 1))
                    for c in range(DC):
                        for h in range(HEADS):
                            last = pe.matmul(pW[:, i % 2, c * P:(c + 1) * P], prod[:, i % PB, h, c * P:(c + 1) * P],
                                             ident[:], start=(h == 0), stop=(h == HEADS - 1))
                    last.then_inc(weight_mm, 1)

                def mix(i):
                    pe.wait_ge(h_ready, i + 1)
                    if i >= 2:
                        if i - 2 < POOL_ADDS:
                            pe.wait_ge(out_read, i - 1)
                        else:
                            pe.wait_ge(y_ready, i - 1)
                    for c in range(DC):
                        last = pe.matmul(pO[:, i % 2, 0:D], hT[:, i % 2, c], up[:, c], start=(c == 0), stop=(c == DC - 1))
                    last.then_inc(out_mm, 1)

                for b in range(BATCH):
                    if b >= 1:
                        pe.wait_ge(xTl_ready, b)
                    for j in range(QC):
                        n = b * QC + j
                        if n >= 4:
                            pe.wait_ge(query_read, n - 3)
                        split_products(pe, query_bank(n), [
                            ((wqh[:, k, j * P:(j + 1) * P], wql[:, k, j * P:(j + 1) * P]),
                             (xTs[b][0][:, k], xTs[b][1][:, k])) for k in range(DC)]).then_inc(query_mm, 1)
                        if j == 1 and b + 1 < BATCH:
                            transposes(b + 1)
                    if b == 1:
                        pe.wait_ge(keyn_ready, 1)
                        pe.transpose(pK[:, 0:P], keyn[:], ident[:]).then_inc(key_mm, 1)
                pe.wait_ge(down_low, 1)
                expert_product(0)
                pe.wait_ge(pair_ready, 4)
                pe.wait_ge(mv_ready, 1)
                pe.matmul(pB[:, 0:2], pair[:], mv[:], start=True, stop=True).then_inc(avg_mm, 1)
                for m in range(1, 3):
                    expert_product(m)
                pe.wait_ge(const_ready, 6)
                pe.wait_ge(key_ready, 1)
                pe.wait_ge(query_read, QS)
                scores(0)
                norms(0)
                scores(1)
                expert_product(3)
                norms(1)
                scores(2)
                norms(2)
                scores(3)
                for m in range(4, ES):
                    expert_product(m)
                pe.wait_ge(gelu_ready, ES)
                pe.wait_ge(ld_up, 16)
                for i in range(TILES):
                    n, t = i // PER, i % PER
                    if t == PER - 1 and 2 <= n and n + 1 < GROUPS:
                        norms(n + 1)
                    if 3 <= i and i + 1 < TILES:
                        scores(i + 1)
                    if 0 <= i - WEIGH - 1:
                        mix(i - WEIGH - 1)
                    if 0 <= i - SUM:
                        sum_heads(i - SUM)
                mix(TILES - WEIGH - 1)
                for i in range(TILES - SUM, TILES):
                    mix(i - 2)
                    sum_heads(i)
                mix(TILES - 2)
                mix(TILES - 1)


def program(nc, d):
    with ExitStack() as ctx:
        st = Stage(nc, ctx, "keep")
        keep = {"x": st.sb("x", [P, TILES, D]), "ident": st.sb("ident", [P, P]), "mv2": st.sb("mv2", [P, TILES, 2]),
                "mv3": st.sb("mv3", [P, TILES, 2])}
        for n in ("Mh", "Ml", "WvTh", "WvTl"):
            keep[n] = st.sb(n, [P, DC, D], F32R)
        for n in ("wqh", "wql"):
            keep[n] = st.sb(n, [P, DC, QC * P], F32R)
        keep["xT0"] = [st.sb(n, [P, DC, SEQ], F32R) for n in ("xT0h", "xT0l")]
        with ExitStack() as inner:
            att = Stage(nc, inner, "context")
            keep["raw"] = att.sb("raw", [P, RAW, SEQ])
            keep["qT0"] = [att.sb(n, [P, DC, SEQ], F32R) for n in ("qT0h", "qT0l")]

            def halves(i):
                for n in ("cTh", "cTl"):
                    keep.setdefault(n, []).append(att.sb(f"{n}{i}", [P, DC, CPAD], F32R))
                for n in ("cNh", "cNl"):
                    keep.setdefault(n, []).append(att.sb(f"{n}{i}", [P, CT, D], F32R))

            halves(0)
            stage_gru(nc, keep, d)
            halves(1)
            stage_attention(nc, keep, d)
        stage_ffn(nc, keep, d)


def layout(np, i):
    def by_feature(v):
        return v.reshape(-1, P).T

    a = {"x": i["x"], "ctx": i["ctx_1024"], "ctxT": i["ctx_1024"].transpose(0, 2, 1),
         "W_out": i["L0_attn_W_out"], "b_out": i["L0_attn_b_out"],
         "xWq": i["L0_xattn_Wq"], "xWk": i["L0_xattn_Wk"], "xWvT": i["L0_xattn_Wv"].T,
         "gate_bias": np.stack([by_feature(i["L0_attn_" + n]) for n in ("bz_f", "bh_f", "bz_b", "bh_b")], 1),
         "fWq": i["L0_ffn_Wq"], "downT": i["L0_ffn_expert_down"].T, "up": i["L0_ffn_expert_up"],
         "fbq": by_feature(i["L0_ffn_bq"]),
         "bn": np.stack([np.concatenate([i["L0_ffn_bn_gamma"]] * 2), np.concatenate([i["L0_ffn_bn_beta"]] * 2)], 1),
         "keys": np.stack([i["L0_ffn_sub_key0"], i["L0_ffn_sub_key1"]])}
    for n in ("Wz_f", "Wh_f", "Wz_b", "Wh_b"):
        a[n] = i["L0_attn_" + n]
    return {n: np.ascontiguousarray(v) for n, v in a.items()}


def kernel(**inputs):
    import numpy as np
    import concourse.bacc as bacc
    from concourse.bass_utils import run_bass_kernel_spmd

    nc = bacc.Bacc("TRN2", target_bir_lowering=False, num_devices=1)
    arrays = layout(np, {n: np.asarray(v) for n, v in inputs.items()})
    d = {n: nc.dram_tensor(f"in_{n}", v.shape, mybir.dt.from_np(v.dtype), kind="ExternalInput").ap()
         for n, v in arrays.items()}
    d["out"] = nc.dram_tensor("out", (BATCH, SEQ, D), F32, kind="ExternalOutput").ap()
    program(nc, d)
    r = run_bass_kernel_spmd(nc, [{f"in_{n}": v for n, v in arrays.items()}], core_ids=[0])
    return r.results[0]["out"]
```

```python
import concourse.bass as bass
from concourse import mybir
from contextlib import ExitStack

F32 = mybir.dt.float32
F32R = mybir.dt.float32r
ALU = mybir.AluOpType
ACT = mybir.ActivationFunctionType
AX = mybir.AxisListType

P = 128
BATCH, SEQ, D = 4, 512, 256
TOKENS = BATCH * SEQ
TPB = SEQ // P
TILES = TOKENS // P
DC = D // P
CTX = 1601
CT = -(-CTX // P)
CLAST = CTX - (CT - 1) * P
CPAD = CTX + CTX % 2
PIECES = DC * -(-CTX // SEQ) + (CT - 1) // 2 + 1
RAW = 4
LN_EPS = BN_EPS = 1e-5
NORM_EPS = 1e-12
HEADS, QD = 8, 64
HALF = QD // 2
KEYS, TOPK, EXPERTS = 32, 4, 256
QC = HEADS * QD // P
ATT_SCALE = float(D) ** -0.5


class Stage:

    def __init__(self, nc, ctx, name):
        self.nc, self.ctx, self.name = nc, ctx, name

    def sb(self, name, shape, dt=F32):
        return self.ctx.enter_context(self.nc.sbuf_tensor(f"{self.name}_{name}", shape, dt))

    def ps(self, name, shape, dt=F32):
        return self.ctx.enter_context(self.nc.psum_tensor(f"{self.name}_{name}", shape, dt))

    def sem(self, name):
        return self.ctx.enter_context(self.nc.semaphore(f"{self.name}_{name}"))


def context_pieces(d, keep, b):
    par = b % 2
    th, tl, ch, cl, raw = (keep[n] for n in ("cTh", "cTl", "cNh", "cNl", "raw"))
    out = []
    for k in range(DC):
        for a in range(0, CTX, SEQ):
            e = min(a + SEQ, CTX)
            out.append((d["ctxT"][b, k * P:(k + 1) * P, a:e], lambda s, n=e - a: raw[:, s, 0:n],
                        th[par][:, k, a:e], tl[par][:, k, a:e]))
    for t in range(0, CT - 1, 2):
        out.append((d["ctx"][b, t * P:(t + 2) * P, :].rearrange("(t p) d -> p t d", p=P),
                    lambda s: raw[:, s].rearrange("p (t d) -> p t d", d=D), ch[par][:, t:t + 2], cl[par][:, t:t + 2]))
    out.append((d["ctx"][b, (CT - 1) * P:CTX, :], lambda s: raw[0:CLAST, s, 0:D],
                ch[par][0:CLAST, CT - 1], cl[par][0:CLAST, CT - 1]))
    return out


def split_products(pe, out, pairs):
    n = len(pairs)
    for i, ((lh, ll), (rh, rl)) in enumerate(pairs):
        pe.matmul(out, lh, rh, start=(i == 0), stop=False)
        pe.matmul(out, lh, rl, start=False, stop=False)
        last = pe.matmul(out, ll, rh, start=False, stop=(i == n - 1))
    return last


def rstd_tail(dve, link, ve, root, y, t, u, rstd):
    link(dve.reciprocal(y, root))
    link(dve.tensor_tensor(t, y, y, ALU.mult))
    link(dve.scalar_tensor_tensor(out=u, in0=t, scalar=-0.5, in1=ve, op0=ALU.mult, op1=ALU.mult))
    return dve.scalar_tensor_tensor(out=rstd, in0=u, scalar=1.5, in1=y, op0=ALU.add, op1=ALU.mult)


def stage_gru(nc, keep, d):
    x_all, ident, mv2 = keep["x"], keep["ident"], keep["mv2"]
    Mh, Ml, WvTh, WvTl = keep["Mh"], keep["Ml"], keep["WvTh"], keep["WvTl"]
    q0h, q0l = keep["qT0"]
    with ExitStack() as ctx:
        st = Stage(nc, ctx, "gru")
        UNDONE = keep["moments_left"]
        ZB = 3
        w = st.sb("w", [P, 4, DC, D])
        wh = st.sb("wh", [P, 4, DC, D], F32R)
        wl = st.sb("wl", [P, 4, DC, D], F32R)
        wout = st.sb("wout", [P, 2 * DC, D])
        wa = st.sb("wa", [P, 2, DC, D])
        wvT = st.sb("wvT", [P, DC, D])
        bias = st.sb("bias", [P, 4, DC])
        nbias = st.sb("nbias", [P, 4, DC])
        bout = st.sb("bout", [P, D])
        stats = st.sb("stats", [P, TILES, 6])
        mv1 = st.sb("mv1", [P, TILES, 2])
        stats2 = st.sb("stats2", [P, TILES, 6])
        ve, root, y0, t0, u0, rstd = (st.sb(n, [P, TILES]) for n in ("ve", "root", "y0", "t0", "u0", "rstd"))
        xn = st.sb("xn", [P, 2, TPB, D])
        xTh = st.sb("xTh", [P, 2, DC, SEQ], F32R)
        xTl = st.sb("xTl", [P, 2, DC, SEQ], F32R)
        z, c = (st.sb(n, [P, ZB, SEQ]) for n in ("z", "c"))
        sg, g = (st.sb(n, [P, 2, SEQ]) for n in ("sg", "g"))
        hT = st.sb("hT", [P, 2, 2 * DC, SEQ])
        pT = st.ps("pT", [P, DC, SEQ])
        pP = st.ps("pP", [P, 4, SEQ])
        pO = st.ps("pO", [P, 2, 2, D])

        GATES = ("Wz_f", "Wh_f", "Wz_b", "Wh_b")

        def last_bank(t):
            return pO[:, t, 0] if t < 2 else pT[:, t - 2, 0:D]

        ld_x = [st.sem(f"ld_x{b}") for b in range(BATCH)]
        ld_w = [st.sem(f"ld_{n}") for n in GATES]
        ld_wa, ld_small, ld_wout = (st.sem(n) for n in ("ld_wa", "ld_small", "ld_wout"))
        dve_chain, ident_set, ident_ready = st.sem("dve_chain"), st.sem("ident_set"), st.sem("ident_ready")
        ve_ready, root_ready, nbias_ready = st.sem("ve_ready"), st.sem("root_ready"), st.sem("nbias_ready")
        wh_ready, wl_pool, wl_dve = st.sem("wh_ready"), st.sem("wl_pool"), st.sem("wl_dve")
        prep_mm, prep_hi, prep_lo = st.sem("prep_mm"), st.sem("prep_hi"), st.sem("prep_lo")
        xn_ready, xT_mm, xTh_ready, xTl_ready = (st.sem(n) for n in ("xn_ready", "xT_mm", "xTh_ready", "xTl_ready"))
        proj_mm, gates, relu_ready, g_ready, zg_ready, h_ready = (
            st.sem(n) for n in ("proj_mm", "gates", "relu_ready", "g_ready", "zg_ready", "h_ready"))
        ve2_ready, x0_mm, x0_high, x0_low, q0_mm, q0_high = (
            st.sem(n) for n in ("ve2_ready", "x0_mm", "x0_high", "x0_low", "q0_mm", "q0_high"))
        xb_ready, out_mm, x2_ready = st.sem("xb_ready"), st.sem("out_mm"), st.sem("x2_ready")
        ld_piece = [st.sem(f"ld_piece{n}") for n in range(RAW)]
        piece_hi, piece_lo, pad_set = st.sem("piece_hi"), st.sem("piece_lo"), st.sem("pad_set")
        pieces = context_pieces(d, keep, 0)
        FIRST = 6
        UNITS = 2 * DC

        def pieces_at(n):
            left = BATCH * UNITS - FIRST
            return range(PIECES * (n - FIRST) // left, PIECES * (n + 1 - FIRST) // left) if n >= FIRST else range(0)

        with nc.Block() as block:
            @block.sync
            def _(sp):
                for b in range(BATCH):
                    sp.dma_start(x_all[:, b * TPB:(b + 1) * TPB, :],
                                 d["x"][b].rearrange("(t p) d -> p t d", p=P)).then_inc(ld_x[b], 16)
                    if b == 0:
                        for m in (1, 3):
                            sp.dma_start(w[:, m], d[GATES[m]].rearrange("(k p) n -> p k n", p=P)).then_inc(ld_w[m], 16)
                for m, n in enumerate(("xWq", "xWk")):
                    sp.dma_start(wa[:, m], d[n].rearrange("(k p) n -> p k n", p=P)).then_inc(ld_wa, 16)
                sp.dma_start(wvT[:], d["xWvT"].rearrange("(k p) n -> p k n", p=P)).then_inc(ld_wa, 16)
                sp.dma_start(wout[:], d["W_out"].rearrange("(k p) n -> p k n", p=P)).then_inc(ld_wout, 16)
                for n, (src, raw, _, _) in enumerate(pieces):
                    if n >= RAW:
                        sp.wait_ge(piece_lo, n - RAW + 1)
                    sp.dma_start(raw(n % RAW), src).then_inc(ld_piece[n % RAW], 16)

            @block.gpsimd
            def _(pool):
                pool.memset(ident[:], 0.0).then_inc(ident_set, 1)
                pool.wait_ge(ident_set, 1)
                pool.affine_select(out=ident[:], in_=ident[:], compare_op=ALU.not_equal, fill=1.0, base=0,
                                   pattern=[[-1, P]], channel_multiplier=1).then_inc(ident_ready, 1)
                for m in (0, 2):
                    pool.wait_ge(wh_ready, m + 1)
                    pool.tensor_tensor(wl[:, m], w[:, m], wh[:, m].bitcast(F32), ALU.subtract).then_inc(wl_pool, 1)
                for m in (keep["cTh"][0], keep["cTl"][0]):
                    pool.memset(m[:, :, CTX:CPAD].bitcast(F32), 0.0).then_inc(pad_set, 1)
                pool.wait_ge(pad_set, 2)
                pool.wait_ge(ld_small, 32)
                for b in range(BATCH):
                    for u in range(UNITS):
                        n = b * UNITS + u
                        for i in pieces_at(n):
                            pool.wait_ge(piece_hi, i + 1)
                            _, raw, hi, lo = pieces[i]
                            pool.tensor_tensor(lo, raw(i % RAW), hi.bitcast(F32), ALU.subtract).then_inc(piece_lo, 1)
                        pool.wait_ge(gates, 3 * n + 1)
                        pool.wait_ge(g_ready, n + 1)
                        pool.tensor_tensor(z[:, n % ZB], z[:, n % ZB], g[:, u % 2], ALU.mult).then_inc(zg_ready, 1)
                        if u == 1:
                            pool.wait_ge(xn_ready, b + 1)
                            xb = x_all[:, b * TPB:(b + 1) * TPB, :]
                            pool.tensor_tensor(xb, xb, bout[:].unsqueeze(1).broadcast_to([P, TPB, D]),
                                               ALU.add).then_inc(xb_ready, 1)

            @block.scalar
            def _(act):
                for m in (0, 2):
                    act.dma_start(w[:, m], d[GATES[m]].rearrange("(k p) n -> p k n", p=P)).then_inc(ld_w[m], 16)
                act.dma_start(bias[:], d["gate_bias"]).then_inc(ld_small, 16)
                act.dma_start(bout[:], d["b_out"].partition_broadcast(P)).then_inc(ld_small, 16)
                def roots(n, a, e):
                    act.wait_ge(ve_ready, n + 1)
                    act.activation(root[:, a:e], ve[:, a:e], ACT.Sqrt).then_inc(root_ready, 1)

                roots(0, 0, TPB)
                for m in range(2):
                    act.wait_ge(ld_w[m], 16)
                    act.activation(wh[:, m], w[:, m], ACT.Copy).then_inc(wh_ready, 1)

                def high(b):
                    act.wait_ge(xT_mm, b + 1)
                    if b >= 2:
                        act.wait_ge(proj_mm, 2 * UNITS * (b - 1))
                    for k in range(DC):
                        last = act.activation(xTh[:, b % 2, k], pT[:, k], ACT.Copy)
                    last.then_inc(xTh_ready, 1)

                high(0)
                for m in range(2, 4):
                    act.wait_ge(ld_w[m], 16)
                    act.activation(wh[:, m], w[:, m], ACT.Copy).then_inc(wh_ready, 1)
                roots(1, TPB, TILES)
                act.wait_ge(ld_small, 32)
                act.wait_ge(nbias_ready, 1)
                for b in range(BATCH):
                    for u in range(UNITS):
                        n, way, ch = b * UNITS + u, u // DC, u % DC
                        for i in pieces_at(n):
                            act.wait_ge(ld_piece[i % RAW], 16 * (i // RAW + 1))
                            _, raw, hi, _ = pieces[i]
                            act.activation(hi, raw(i % RAW), ACT.Copy).then_inc(piece_hi, 1)
                        if u == 2 and b + 1 < BATCH:
                            high(b + 1)
                        act.wait_ge(proj_mm, 2 * n + 1)
                        if n >= ZB:
                            act.wait_ge(h_ready, n - ZB + 1)
                        zp = pP[:, (2 * n) % 4]
                        act.activation(z[:, n % ZB], zp, ACT.Sigmoid,
                                       bias=bias[:, 2 * way, ch:ch + 1]).then_inc(gates, 1)
                        act.activation(c[:, n % ZB], zp, ACT.Sigmoid, scale=-1.0,
                                       bias=nbias[:, 2 * way, ch:ch + 1]).then_inc(gates, 1)
                        act.wait_ge(proj_mm, 2 * n + 2)
                        if n >= 2:
                            act.wait_ge(g_ready, n - 1)
                        act.activation(sg[:, u % 2], pP[:, (2 * n + 1) % 4], ACT.Sigmoid,
                                       bias=bias[:, 2 * way + 1, ch:ch + 1]).then_inc(gates, 1)
                        if n == UNITS - 1:
                            act.wait_ge(prep_mm, 1)
                            act.activation(Mh[:], pO[:, 0], ACT.Copy).then_inc(prep_hi, 1)
                            act.wait_ge(ld_wa, 48)
                            act.activation(WvTh[:], wvT[:], ACT.Copy).then_inc(prep_hi, 1)
                act.wait_ge(ve2_ready, 1)
                act.activation(root[:, 0:TPB], ve[:, 0:TPB], ACT.Sqrt).then_inc(root_ready, 1)
                for k in range(DC):
                    act.wait_ge(x0_mm, k + 1)
                    act.activation(xTh[:, 0, k], pP[:, k], ACT.Copy).then_inc(x0_high, 1)
                for k in range(DC):
                    act.wait_ge(q0_mm, k + 1)
                    act.activation(q0h[:, k], pP[:, 2 + k], ACT.Copy).then_inc(q0_high, 1)

            @block.vector
            def _(dve):
                chained = [0]

                def link(ins):
                    chained[0] += 1
                    ins.then_inc(dve_chain, 1)
                    dve.wait_ge(dve_chain, chained[0])

                def moments(tiles, out, stat):
                    for t in tiles:
                        last = dve.bn_stats(stat[:, t], x_all[:, t])
                    link(last)
                    for t in tiles:
                        last = dve.bn_aggr(out[:, t], stat[:, t])
                    link(last)

                def normalise(b):
                    if b >= 2:
                        dve.wait_ge(xT_mm, b - 1)
                    for t in range(TPB):
                        i = b * TPB + t
                        last = dve.tensor_scalar(xn[:, b % 2, t], x_all[:, i], mv1[:, i, 0:1], rstd[:, i:i + 1],
                                                 ALU.subtract, ALU.mult)
                    last.then_inc(xn_ready, 1)

                def low(b):
                    dve.wait_ge(xTh_ready, b + 1)
                    if b >= 2:
                        dve.wait_ge(proj_mm, 2 * UNITS * (b - 1))
                    for k in range(DC):
                        last = dve.tensor_tensor(xTl[:, b % 2, k], pT[:, k], xTh[:, b % 2, k].bitcast(F32),
                                                 ALU.subtract)
                    last.then_inc(xTl_ready, 1)

                def weight_low(m):
                    dve.wait_ge(wh_ready, m + 1)
                    dve.tensor_tensor(wl[:, m], w[:, m], wh[:, m].bitcast(F32), ALU.subtract).then_inc(wl_dve, 1)

                def variances(b, e):
                    for i in range(b, e):
                        dve.wait_ge(ld_x[i], 16)
                    moments(range(b * TPB, e * TPB), mv1, stats)

                def shifted(n, a, e):
                    dve.tensor_scalar(ve[:, a:e], mv1[:, a:e, 1], LN_EPS, None, ALU.add).then_inc(ve_ready, 1)
                    dve.wait_ge(ve_ready, n + 1)

                def inverse_roots(n, a, e):
                    dve.wait_ge(root_ready, n + 1)
                    link(rstd_tail(dve, link, ve[:, a:e], root[:, a:e], y0[:, a:e], t0[:, a:e], u0[:, a:e],
                                   rstd[:, a:e]))

                variances(0, 1)
                shifted(0, 0, TPB)
                inverse_roots(0, 0, TPB)
                normalise(0)
                weight_low(1)
                variances(1, 2)
                low(0)
                dve.wait_ge(ld_small, 32)
                dve.tensor_scalar(nbias[:], bias[:], -1.0, None, ALU.mult).then_inc(nbias_ready, 1)
                variances(2, BATCH)
                shifted(1, TPB, TILES)
                weight_low(3)
                inverse_roots(1, TPB, TILES)
                normalise(1)

                def scan(b, u):
                    n = b * UNITS + u
                    dve.wait_ge(zg_ready, n + 1)
                    dve.wait_ge(gates, 3 * n + 2)
                    if b >= 2 and u == 0:
                        dve.wait_ge(out_mm, TPB * (b - 1))
                    keepg, add = c[:, n % ZB], z[:, n % ZB]
                    if u >= DC:
                        keepg, add = c[:, n % ZB, ::-1], z[:, n % ZB, ::-1]
                    dve.tensor_tensor_scan(hT[:, b % 2, u], keepg, add, 0.0, ALU.mult, ALU.add).then_inc(h_ready, 1)

                def residual(b):
                    dve.wait_ge(xb_ready, b + 1)
                    xb = x_all[:, b * TPB:(b + 1) * TPB, :]
                    if b < BATCH - 1:
                        for n in range(2):
                            dve.wait_ge(out_mm, TPB * b + 2 * (n + 1))
                            last = dve.tensor_tensor(xb[:, 2 * n:2 * n + 2], pO[:, n], xb[:, 2 * n:2 * n + 2], ALU.add)
                    else:
                        for t in range(TPB):
                            dve.wait_ge(out_mm, TPB * b + t + 1)
                            last = dve.tensor_tensor(xb[:, t], last_bank(t), xb[:, t], ALU.add)
                    last.then_inc(x2_ready, 1)
                    dve.wait_ge(x2_ready, b + 1)
                    if b < UNDONE:
                        moments(range(b * TPB, (b + 1) * TPB), mv2, stats2)

                for b in range(BATCH):
                    for u in range(UNITS):
                        n, way, ch = b * UNITS + u, u // DC, u % DC
                        if u == 2 and b + 1 < BATCH:
                            low(b + 1)
                        dve.wait_ge(gates, 3 * n + 3)
                        hp = pP[:, (2 * n + 1) % 4]
                        if n >= 2:
                            dve.wait_ge(zg_ready, n - 1)
                        dve.tensor_scalar(g[:, u % 2], hp, bias[:, 2 * way + 1, ch:ch + 1], 0.0,
                                          ALU.add, ALU.max).then_inc(relu_ready, 1)
                        dve.wait_ge(relu_ready, n + 1)
                        dve.scalar_tensor_tensor(out=g[:, u % 2], in0=sg[:, u % 2], scalar=0.5, in1=g[:, u % 2],
                                                 op0=ALU.min, op1=ALU.add).then_inc(g_ready, 1)
                        if n >= 1:
                            scan((n - 1) // UNITS, (n - 1) % UNITS)
                        if n == 1:
                            normalise(2)
                        if n == UNITS + 2:
                            normalise(3)
                        if n == UNITS:
                            dve.wait_ge(prep_hi, 1)
                            dve.tensor_tensor(Ml[:], pO[:, 0], Mh[:].bitcast(F32), ALU.subtract).then_inc(prep_lo, 1)
                            dve.wait_ge(prep_hi, 2)
                            dve.tensor_tensor(WvTl[:], wvT[:], WvTh[:].bitcast(F32), ALU.subtract).then_inc(prep_lo, 1)
                        if u == 0 and b >= 2:
                            residual(b - 2)
                            if b == 2:
                                dve.tensor_scalar(ve[:, 0:TPB], mv2[:, 0:TPB, 1], LN_EPS, None, ALU.add)\
                                    .then_inc(ve2_ready, 1)
                    if b == BATCH - 1:
                        residual(b - 1)
                scan(BATCH - 1, UNITS - 1)
                dve.wait_ge(root_ready, 3)
                link(rstd_tail(dve, link, ve[:, 0:TPB], root[:, 0:TPB], y0[:, 0:TPB], t0[:, 0:TPB], u0[:, 0:TPB],
                               rstd[:, 0:TPB]))
                dve.wait_ge(xT_mm, BATCH - 1)
                for t in range(TPB):
                    last = dve.tensor_scalar(xn[:, 0, t], x_all[:, t], mv2[:, t, 0:1], rstd[:, t:t + 1],
                                             ALU.subtract, ALU.mult)
                last.then_inc(xn_ready, 1)
                for k in range(DC):
                    dve.wait_ge(x0_high, k + 1)
                    dve.tensor_tensor(xTl[:, 0, k], pP[:, k], xTh[:, 0, k].bitcast(F32), ALU.subtract).then_inc(x0_low, 1)
                residual(BATCH - 1)
                for k in range(DC):
                    dve.wait_ge(q0_high, k + 1)
                    dve.tensor_tensor(q0l[:, k], pP[:, 2 + k], q0h[:, k].bitcast(F32), ALU.subtract)

            @block.tensor
            def _(pe):
                def attention_weights():
                    pe.wait_ge(ld_wa, 48)
                    for ch in range(DC):
                        for k in range(DC):
                            last = pe.matmul(pO[:, 0, ch], wa[:, 0, k, ch * P:(ch + 1) * P], wa[:, 1, k],
                                             start=(k == 0), stop=(k == DC - 1))
                    last.then_inc(prep_mm, 1)

                def transposes(b):
                    pe.wait_ge(xn_ready, b + 1)
                    if b >= 1:
                        pe.wait_ge(xTl_ready, b)
                    for k in range(DC):
                        for t in range(TPB):
                            last = pe.transpose(pT[:, k, t * P:(t + 1) * P], xn[:, b % 2, t, k * P:(k + 1) * P],
                                                ident[:])
                    last.then_inc(xT_mm, 1)

                def output(b, t):
                    if t == 0:
                        pe.wait_ge(h_ready, UNITS * (b + 1))
                        if b >= 1:
                            pe.wait_ge(x2_ready, b)
                    for k in range(2 * DC):
                        last = pe.matmul(pO[:, t // 2, t % 2], hT[:, b % 2, k, t * P:(t + 1) * P], wout[:, k],
                                         start=(k == 0), stop=(k == 2 * DC - 1))
                    last.then_inc(out_mm, 1)

                def last_output(b):
                    def add(k, t):
                        pe.wait_ge(h_ready, UNITS * b + k + 1)
                        return pe.matmul(last_bank(t), hT[:, b % 2, k, t * P:(t + 1) * P], wout[:, k],
                                         start=(k == 0), stop=(k == 2 * DC - 1))

                    for half in (range(2, TPB), range(2)):
                        if half[0] == 0:
                            pe.wait_ge(x2_ready, b)
                        for k in range(2 * DC - 1):
                            for t in half:
                                add(k, t)
                    pe.wait_ge(xn_ready, BATCH + 1)
                    pe.wait_ge(gates, 3 * BATCH * UNITS)
                    pe.wait_ge(relu_ready, BATCH * UNITS)
                    for c in range(DC):
                        for t in range(TPB):
                            mm = pe.transpose(pP[:, c, t * P:(t + 1) * P], xn[:, 0, t, c * P:(c + 1) * P], ident[:])
                        mm.then_inc(x0_mm, 1)
                    for t in range(TPB):
                        add(2 * DC - 1, t).then_inc(out_mm, 1)

                pe.wait_ge(ident_ready, 1)
                transposes(0)
                for b in range(BATCH):
                    pe.wait_ge(xTl_ready, b + 1)
                    for j in range(2 * UNITS):
                        n = 2 * UNITS * b + j
                        way, ch, m = j // (2 * DC), (j // 2) % DC, j % 2
                        if n >= 4:
                            if m == 0:
                                pe.wait_ge(gates, 3 * ((n - 4) // 2) + 2)
                            else:
                                pe.wait_ge(gates, 3 * ((n - 4) // 2) + 3)
                                pe.wait_ge(relu_ready, (n - 4) // 2 + 1)
                        if n == 0:
                            pe.wait_ge(wl_pool, 1)
                        if n == 1:
                            pe.wait_ge(wl_dve, 1)
                        if n == 2 * DC:
                            pe.wait_ge(wl_pool, 2)
                            pe.wait_ge(wl_dve, 2)
                        cols = slice(ch * P, (ch + 1) * P)
                        split_products(pe, pP[:, n % 4], [
                            ((wh[:, 2 * way + m, k, cols], wl[:, 2 * way + m, k, cols]),
                             (xTh[:, b % 2, k], xTl[:, b % 2, k])) for k in range(DC)]).then_inc(proj_mm, 1)
                        if j == UNITS and b + 1 < BATCH:
                            transposes(b + 1)
                        if n == UNITS:
                            attention_weights()
                        if n == 3 * UNITS - 1:
                            pe.wait_ge(ld_wout, 16)
                            pe.wait_ge(prep_lo, 1)
                        if j >= UNITS and b >= 1:
                            output(b - 1, j - UNITS)
                last_output(BATCH - 1)
                pe.wait_ge(x0_low, DC)
                for c in range(DC):
                    split_products(pe, pP[:, 2 + c], [
                        ((Mh[:, k, c * P:(c + 1) * P], Ml[:, k, c * P:(c + 1) * P]), (xTh[:, 0, k], xTl[:, 0, k]))
                        for k in range(DC)]).then_inc(q0_mm, 1)


def stage_attention(nc, keep, d):
    x_all, ident, mv2, mv3 = keep["x"], keep["ident"], keep["mv2"], keep["mv3"]
    Mh, Ml, WvTh, WvTl = keep["Mh"], keep["Ml"], keep["WvTh"], keep["WvTl"]
    cTh, cTl, cNh, cNl = keep["cTh"], keep["cTl"], keep["cNh"], keep["cNl"]
    xT, qT0 = keep["xT0"], keep["qT0"]
    KB = -(-CPAD // SEQ)
    RING = 3
    GROUPS = [range(i, min(i + 4, CT)) for i in range(0, CT, 4)]
    NG = len(GROUPS)

    ORDER = "V P0 P1 E O P2 S A0 P3 A1 A2 A3"

    def at_tile(g):
        out = []
        for kind in ORDER.split():
            a = g - {"V": 2, "O": 2, "S": 2, "E": 0}.get(kind[0], 1)
            if 0 <= a < TILES:
                out.append((kind[0], a, int(kind[1:] or 0)))
        b = g // TPB + 1
        if b < BATCH and g % TPB == 1:
            out += [("X", b, 0), ("X", b, 1)]
        if b < BATCH and g % TPB == 2:
            out += [("Q", b, 0), ("Q", b, 1)]
        if g == TILES + 1:
            out.insert(1, ("X", BATCH, 0))
            out.insert(3, ("X", BATCH, 1))
        return out

    BESIDE = ("P0", "P2", "P3")
    EARLY = {"V0": 3, "P0": 3}

    def between_scores(g, j):
        return [it for it in SLOTS[g] if g < TILES and EARLY.get(f"{it[0]}{it[2]}") == j]

    LOWS = {"V0": 3, "P0": 4}

    def lows(g, j):
        return [it for it in SLOTS[g] if g < TILES and LOWS.get(f"{it[0]}{it[2]}") == j]

    def early(g):
        return [it for j in range(KB) for it in between_scores(g, j)]

    SLOTS = [at_tile(g) for g in range(TILES + 2)]
    ring = [it for slot in SLOTS for it in slot if it[0] not in "ESA"]
    place = {it: n for n, it in enumerate(ring)}
    halved = {it: n for n, it in enumerate([it for it in ring if it[0] != "O"])}

    with ExitStack() as ctx:
        st = Stage(nc, ctx, "att")
        ve, root, y0, t0, u0, rstd = (st.sb(n, [P, TILES]) for n in ("ve", "root", "y0", "t0", "u0", "rstd"))
        xn = st.sb("xn", [P, TPB, D])
        qT1 = [st.sb(n, [P, DC, SEQ], F32R) for n in ("qT1h", "qT1l")]
        qT = (qT0, qT1)
        prob = st.sb("prob", [P, 2, CTX])
        pT = [st.sb(n, [P, CT, P], F32R) for n in ("pTh", "pTl")]
        vT = [st.sb(n, [P, 2, DC, P], F32R) for n in ("vTh", "vTl")]
        val = st.sb("val", [P, 2, D])
        mx = st.sb("mx", [P, 2, KB])
        nmax = st.sb("nmax", [P, 2])
        tmax = st.sb("tmax", [P, 2])
        rowsum = st.sb("rowsum", [P, 2])
        rinv = st.sb("rinv", [P, 2])
        stats = st.sb("stats", [P, TILES, 6])
        pS = st.ps("pS", [P, KB * SEQ])
        pA = st.ps("pA", [P, SEQ])
        pR = st.ps("pR", [P, RING, SEQ])

        dve_chain, root_ready, ve_ready, xn_ready = (st.sem(n) for n in ("dve_chain", "root_ready", "ve_ready", "xn_ready"))
        ld_piece = [st.sem(f"ld_piece{n}") for n in range(RAW)]
        piece_hi, piece_lo, pad_set = st.sem("piece_hi"), st.sem("piece_lo"), st.sem("pad_set")
        bank_full, bank_high, bank_free = st.sem("bank_full"), st.sem("bank_high"), st.sem("bank_free")
        score_mm, max_ready, exp_ready, rinv_ready = (st.sem(n) for n in ("score_mm", "max_ready", "exp_ready", "rinv_ready"))
        value_mm, val_ready, x3_ready = st.sem("value_mm"), st.sem("val_ready"), st.sem("x3_ready")
        pieces = [p for b in range(1, BATCH) for p in context_pieces(d, keep, b)]
        for k in range(DC):
            pieces.append((d["fWq"][k * P:(k + 1) * P, :], lambda s: keep["raw"][:, s], keep["wqh"][:, k], keep["wql"][:, k]))

        def pieces_at(g):
            b, q = g // TPB, -(-PIECES // TPB)
            if b + 1 >= BATCH:
                n = PIECES * (BATCH - 1) + g - TPB * (BATCH - 1)
                return range(n, min(n + 1, len(pieces)))
            return range(b * PIECES + min(q * (g % TPB), PIECES), b * PIECES + min(q * (g % TPB + 1), PIECES))

        def wait_context(eng, i):
            b, n = i // PIECES + 1, i % PIECES
            if 2 <= b < BATCH:
                if n < DC * -(-CTX // SEQ):
                    eng.wait_ge(score_mm, KB * TPB * (b - 1))
                else:
                    eng.wait_ge(value_mm, NG * TPB * (b - 1))

        def half(it, which, n):
            kind, a, i = it
            bank = pR[:, n % RING]
            if kind == "X":
                return xT[which][:, i], bank
            if kind == "Q":
                return qT[a % 2][which][:, i], bank
            if kind == "P":
                rows = CLAST if GROUPS[i][-1] == CT - 1 else P
                m = len(GROUPS[i])
                return pT[which][0:rows, GROUPS[i][0]:GROUPS[i][0] + m], \
                    bank[0:rows, 0:m * P].rearrange("p (t n) -> p t n", n=P)
            return vT[which][:, a % 2], bank[:, 0:DC * P].rearrange("p (t n) -> p t n", n=P)

        def wait_overwrite(eng, it):
            kind, a, i = it
            if kind == "X" and a >= 2:
                eng.wait_ge(bank_full, place[("Q", a - 1, DC - 1)] + 1)
            elif kind == "Q" and a >= 2:
                eng.wait_ge(score_mm, KB * TPB * (a - 1))
            elif kind == "P" and a >= 1:
                eng.wait_ge(value_mm, NG * (a - 1) + i + 1)
            elif kind == "V" and a >= 2:
                eng.wait_ge(bank_full, place[("O", a - 2, 0)] + 1)

        with nc.Block() as block:
            @block.sync
            def _(sp):
                for n, (src, raw, _, _) in enumerate(pieces):
                    if n >= RAW:
                        sp.wait_ge(piece_lo, n - RAW + 1)
                    sp.dma_start(raw(n % RAW), src).then_inc(ld_piece[n % RAW], 16)

            @block.gpsimd
            def _(pool):
                for m in (cTh[1], cTl[1]):
                    pool.memset(m[:, :, CTX:CPAD].bitcast(F32), 0.0).then_inc(pad_set, 1)
                for g in range(TILES):
                    for i in pieces_at(g):
                        pool.wait_ge(piece_hi, i + 1)
                        wait_context(pool, i)
                        _, raw, hi, lo = pieces[i]
                        pool.tensor_tensor(lo, raw(i % RAW), hi.bitcast(F32), ALU.subtract).then_inc(piece_lo, 1)

            @block.scalar
            def _(act):
                act.wait_ge(ve_ready, 1)
                act.activation(root[:, TPB:], ve[:, TPB:], ACT.Sqrt).then_inc(root_ready, 1)

                def high(it):
                    n = place[it]
                    act.wait_ge(bank_full, n + 1)
                    wait_overwrite(act, it)
                    to, bank = half(it, 0, n)
                    act.activation(to, bank, ACT.Copy).then_inc(bank_high, 1)

                def values(g):
                    act.wait_ge(value_mm, NG * (g + 1))
                    act.wait_ge(rinv_ready, g + 1)
                    if g >= 2:
                        act.wait_ge(bank_full, place[("V", g - 2, 0)] + 1)
                    act.activation(val[:, g % 2], pA[:, 0:D], ACT.Copy, scale=rinv[:, g % 2:g % 2 + 1])\
                        .then_inc(val_ready, 1)

                def piece_high(i):
                    act.wait_ge(ld_piece[i % RAW], 16 * (i // RAW + 1))
                    wait_context(act, i)
                    _, raw, hi, _ = pieces[i]
                    act.activation(hi, raw(i % RAW), ACT.Copy).then_inc(piece_hi, 1)

                for g in range(TILES + 2):
                    if 0 <= g - 2 < TILES:
                        values(g - 2)
                    left = list(pieces_at(g)) if g < TILES else []
                    for it in SLOTS[g]:
                        if it[0] == "E":
                            act.wait_ge(max_ready, g + 1)
                            if g >= 2:
                                act.wait_ge(bank_full, place[("P", g - 2, NG - 1)] + 1)
                                act.wait_ge(rinv_ready, g - 1)
                            act.activation(prob[:, g % 2], pS[:, 0:CTX], ACT.Exp, bias=nmax[:, g % 2:g % 2 + 1],
                                           scale=ATT_SCALE, accum_out=rowsum[:, g % 2:g % 2 + 1]).then_inc(exp_ready, 1)
                        elif it[0] not in "SAO":
                            high(it)
                        if left and f"{it[0]}{it[2]}" in BESIDE:
                            piece_high(left.pop(0))
                    for i in left:
                        piece_high(i)
                    if g == TILES - 1:
                        act.wait_ge(ve_ready, 2)
                        act.activation(root[:, 0:TPB], ve[:, 0:TPB], ACT.Sqrt).then_inc(root_ready, 1)

            @block.vector
            def _(dve):
                chained = [0]

                def note(ins):
                    ins.then_inc(dve_chain, 1)
                    chained[0] += 1
                    return chained[0]

                def link(ins):
                    dve.wait_ge(dve_chain, note(ins))

                def inverse_roots(a, e):
                    return rstd_tail(dve, link, ve[:, a:e], root[:, a:e], y0[:, a:e], t0[:, a:e], u0[:, a:e],
                                     rstd[:, a:e])

                def normalise(b):
                    if b >= 2:
                        dve.wait_ge(bank_full, place[("X", b - 1, DC - 1)] + 1)
                    for t in range(TPB):
                        i = (b % BATCH) * TPB + t
                        mv = mv2 if b < BATCH else mv3
                        last = dve.tensor_scalar(xn[:, t], x_all[:, i], mv[:, i, 0:1], rstd[:, i:i + 1],
                                                 ALU.subtract, ALU.mult)
                    last.then_inc(xn_ready, 1)

                def low(it):
                    n = place[it]
                    dve.wait_ge(bank_high, halved[it] + 1)
                    wait_overwrite(dve, it)
                    to, bank = half(it, 1, n)
                    dve.tensor_tensor(to, bank, half(it, 0, n)[0].bitcast(F32), ALU.subtract).then_inc(bank_free, 1)

                def output(g):
                    n = place[("O", g, 0)]
                    dve.wait_ge(bank_full, n + 1)
                    dve.tensor_tensor(x_all[:, g], pR[:, n % RING, 0:D], x_all[:, g], ALU.add).then_inc(bank_free, 1)

                def new_moments(g):
                    dve.wait_ge(bank_free, place[("O", g, 0)] + 1)
                    link(dve.bn_stats(stats[:, g], x_all[:, g]))
                    dve.bn_aggr(mv3[:, g], stats[:, g]).then_inc(x3_ready, 1)

                def row_max(g):
                    h = g % 2
                    for j in range(KB):
                        for it in lows(g, j):
                            low(it)
                        dve.wait_ge(score_mm, KB * g + j + 1)
                        last = dve.tensor_reduce(mx[:, h, j:j + 1], pS[:, j * SEQ:min((j + 1) * SEQ, CTX)], AX.X, ALU.max)
                    at = note(last)
                    for it in lows(g, KB):
                        low(it)
                    dve.wait_ge(dve_chain, at)
                    link(dve.tensor_reduce(tmax[:, h:h + 1], mx[:, h], AX.X, ALU.max))
                    dve.tensor_scalar(nmax[:, h:h + 1], tmax[:, h:h + 1], -ATT_SCALE, None, ALU.mult).then_inc(max_ready, 1)

                left = range(keep["moments_left"] * TPB, TILES)
                for t in left:
                    last = dve.bn_stats(stats[:, t], x_all[:, t])
                link(last)
                for t in left:
                    last = dve.bn_aggr(mv2[:, t], stats[:, t])
                link(last)
                dve.tensor_scalar(ve[:, TPB:], mv2[:, TPB:, 1], LN_EPS, None, ALU.add).then_inc(ve_ready, 1)
                for g in range(TILES + 2):
                    if 0 <= g - 1 < TILES:
                        dve.wait_ge(exp_ready, g)
                        if g >= 3:
                            dve.wait_ge(val_ready, g - 2)
                        dve.reciprocal(rinv[:, (g - 1) % 2:(g - 1) % 2 + 1], rowsum[:, (g - 1) % 2:(g - 1) % 2 + 1])\
                            .then_inc(rinv_ready, 1)
                    if g < TILES:
                        row_max(g)
                    for it in SLOTS[g]:
                        if it[0] == "O":
                            output(it[1])
                        elif it[0] == "S":
                            new_moments(it[1])
                        elif it[0] not in "AE" and it not in [i for j in range(KB + 1) for i in lows(g, j)]:
                            low(it)
                    if g == 0:
                        dve.wait_ge(root_ready, 1)
                        link(inverse_roots(TPB, TILES))
                    if g % TPB == 0 and g // TPB + 1 < BATCH:
                        normalise(g // TPB + 1)
                    if g == TPB + 1:
                        dve.wait_ge(x3_ready, TPB)
                        dve.tensor_scalar(ve[:, 0:TPB], mv3[:, 0:TPB, 1], LN_EPS, None, ALU.add).then_inc(ve_ready, 1)
                    if g == TILES - 1:
                        dve.wait_ge(root_ready, 2)
                        link(inverse_roots(0, TPB))
                        normalise(BATCH)

            @block.tensor
            def _(pe):
                def scores(g):
                    b, t = g // TPB, g % TPB
                    if b >= 1:
                        pe.wait_ge(bank_free, place[("Q", b, DC - 1)] + 1)
                    if b >= 1 and t == 0:
                        pe.wait_ge(piece_lo, PIECES * b)
                        pe.wait_ge(pad_set, 2)
                    if g >= 1:
                        pe.wait_ge(exp_ready, g)
                    for j in range(KB):
                        for it in between_scores(g, j):
                            item(it)
                        a, e = j * SEQ, min((j + 1) * SEQ, CPAD)
                        split_products(pe, pS[:, a:e], [
                            (tuple(q[:, k, t * P:(t + 1) * P] for q in qT[b % 2]),
                             (cTh[b % 2][:, k, a:e], cTl[b % 2][:, k, a:e])) for k in range(DC)]).then_inc(score_mm, 1)

                def item(it):
                    kind, a, i = it
                    if kind == "A":
                        pe.wait_ge(bank_free, place[("P", a, i)] + 1)
                        if i == 0 and a >= 1:
                            pe.wait_ge(val_ready, a)
                        for kt in GROUPS[i]:
                            rows, par = (CLAST if kt == CT - 1 else P), (a // TPB) % 2
                            l = [p[0:rows, kt] for p in pT]
                            r = [c[par][0:rows, kt] for c in (cNh, cNl)]
                            pe.matmul(pA[:, 0:D], l[0], r[0], start=(kt == 0), stop=False)
                            pe.matmul(pA[:, 0:D], l[0], r[1], start=False, stop=False)
                            last = pe.matmul(pA[:, 0:D], l[1], r[0], start=False, stop=(kt == CT - 1))
                        last.then_inc(value_mm, 1)
                        return
                    n = place[it]
                    if n >= RING:
                        pe.wait_ge(bank_free, n - RING + 1)
                    bank = pR[:, n % RING]
                    if kind == "X":
                        pe.wait_ge(xn_ready, a)
                        for t in range(TPB):
                            last = pe.transpose(bank[:, t * P:(t + 1) * P], xn[:, t, i * P:(i + 1) * P], ident[:])
                    elif kind == "Q":
                        pe.wait_ge(bank_free, place[("X", a, DC - 1)] + 1)
                        last = split_products(pe, bank, [
                            ((Mh[:, k, i * P:(i + 1) * P], Ml[:, k, i * P:(i + 1) * P]), (xT[0][:, k], xT[1][:, k]))
                            for k in range(DC)])
                    elif kind == "P":
                        pe.wait_ge(exp_ready, a + 1)
                        for m, kt in enumerate(GROUPS[i]):
                            rows = CLAST if kt == CT - 1 else P
                            last = pe.transpose(bank[0:rows, m * P:(m + 1) * P], prob[:, a % 2, kt * P:kt * P + rows],
                                                ident[:])
                    elif kind == "V":
                        pe.wait_ge(val_ready, a + 1)
                        for k in range(DC):
                            last = pe.transpose(bank[:, k * P:(k + 1) * P], val[:, a % 2, k * P:(k + 1) * P], ident[:])
                    else:
                        pe.wait_ge(bank_free, place[("V", a, 0)] + 1)
                        last = split_products(pe, bank[:, 0:D], [
                            ((vT[0][:, a % 2, k], vT[1][:, a % 2, k]), (WvTh[:, k], WvTl[:, k])) for k in range(DC)])
                    last.then_inc(bank_full, 1)

                for g in range(TILES + 2):
                    if g < TILES:
                        scores(g)
                    for it in SLOTS[g]:
                        if it[0] not in "ES" and it not in early(g):
                            item(it)


def stage_ffn(nc, keep, d):
    x_all, ident, mv3 = keep["x"], keep["ident"], keep["mv3"]
    wqh, wql = keep["wqh"], keep["wql"]
    PER = 2
    GROUPS = TILES // PER
    HALVES = 2 * HEADS
    ROW = KEYS + TOPK
    ABOVE = 8.0
    FIRSTS = EXPERTS // KEYS
    COLS = PER * P
    WEIGH, SUM = 5, 3
    PB = 3
    QS = BATCH * QC
    ES = BATCH * DC
    with ExitStack() as ctx:
        st = Stage(nc, ctx, "ffn")
        down = st.sb("down", [P, DC, D])
        dnh, dnl = (st.sb(n, [P, DC, D], F32R) for n in ("dnh", "dnl"))
        up = st.sb("up", [P, DC, D])
        bq = st.sb("bq", [P, QC])
        affine = st.sb("affine", [P, 2])
        key = st.sb("key", [P, P])
        keysq, keyn, keyT = st.sb("keysq", [P, P]), st.sb("keyn", [P, P]), st.sb("keyT", [P, P])
        k2, kroot, ky, kt, ku, kinv = (st.sb(n, [P, 1]) for n in ("k2", "kroot", "ky", "kt", "ku", "kinv"))
        pair = st.sb("pair", [P, P])
        group_of = st.sb("group_of", [P, 4])
        ve, root, y0, t0, u0, rstd = (st.sb(n, [P, TILES]) for n in ("ve", "root", "y0", "t0", "u0", "rstd"))
        xn = st.sb("xn", [P, 2, TPB, D])
        xTs = [keep["xT0"]] + [[st.sb(f"xT{b}{n}", [P, DC, SEQ], F32R) for n in "hl"] for b in range(1, BATCH)]
        qT = st.sb("qT", [P, QC, TOKENS])
        gT = st.sb("gT", [P, DC, TOKENS])
        stats = st.sb("stats", [P, QS, 6])
        mv, avg = st.sb("mv", [P, 2]), st.sb("avg", [P, 2])
        nmean, diff, bve, broot, by, bt, bu, brstd = (
            st.sb(n, [P, 1]) for n in ("nmean", "diff", "bve", "broot", "by", "bt", "bu", "brstd"))
        bn = st.sb("bn", [P, 2])
        sq = st.sb("sq", [P, QC, COLS])
        n2, nroot, ny, nt, nu, ninv = (st.sb(n, [P, 2, PER * HALVES]) for n in ("n2", "nroot", "ny", "nt", "nu", "ninv"))
        s = st.sb("s", [P, 2, PER, HALVES, ROW])
        picked = st.sb("picked", [P, PER, HALVES, ROW])
        top = st.sb("top", [P, 2, PER, HALVES, 2 * TOPK])
        e = st.sb("e", [P, 2, PER, HALVES, KEYS])
        etop = st.sb("etop", [P, 2, PER, HALVES, TOPK])
        total = st.sb("total", [P, PER, HEADS, 2])
        inv = st.sb("inv", [P, PER, HEADS, 2])
        both = st.sb("both", [P, PER * HEADS])
        raw1 = st.sb("raw1", [P, PER * HEADS, FIRSTS])
        sum1, rest, restn = (st.sb(n, [P, PER, HEADS]) for n in ("sum1", "rest", "restn"))
        first = st.sb("first", [P, 2, PER, HEADS, FIRSTS])
        second = st.sb("second", [P, 2, PER, HEADS, KEYS])
        clamped = st.sb("clamped", [P, 2, PER])
        prod = st.sb("prod", [P, PB, HEADS, EXPERTS])
        hT = st.sb("hT", [P, 2, DC, P])
        y = st.sb("y", [P, 2, D])
        pT = pW = st.ps("pT", [P, DC, SEQ])
        pO = st.ps("pO", [P, 2, SEQ])
        pS = st.ps("pS", [P, 2, SEQ])
        pK = pN = st.ps("pK", [P, SEQ])
        pB = st.ps("pB", [P, SEQ])

        def query_bank(n):
            return pO[:, n % 4] if n % 4 < 2 else pS[:, n % 4 - 2]

        def expert_bank(m):
            return pO[:, m % 4] if m % 4 < 2 else pT[:, m % 4 - 2]

        ld_down, ld_small, ld_key, ld_up = st.sem("ld_down"), st.sem("ld_small"), st.sem("ld_key"), st.sem("ld_up")
        zeroed, pair_ready, const_ready, dve_chain = (st.sem(n) for n in ("zeroed", "pair_ready", "const_ready", "dve_chain"))
        ve_ready, root_ready, down_high, down_low = (st.sem(n) for n in ("ve_ready", "root_ready", "down_high", "down_low"))
        keyn_ready, key_mm, key_ready = st.sem("keyn_ready"), st.sem("key_mm"), st.sem("key_ready")
        xn_ready, xT_mm, xTh_ready, xTl_ready = (st.sem(n) for n in ("xn_ready", "xT_mm", "xTh_ready", "xTl_ready"))
        query_mm, query_read, expert_mm, gelu_ready = (
            st.sem(n) for n in ("query_mm", "query_read", "expert_mm", "gelu_ready"))
        mv_ready, avg_mm, bn_ready = st.sem("mv_ready"), st.sem("avg_mm"), st.sem("bn_ready")
        sq_ready, norm_mm, n2_ready, nroot_ready = (
            st.sem(n) for n in ("sq_ready", "norm_mm", "n2_ready", "nroot_ready"))
        q_ready_dve, q_ready_pool, q_ready_act = (st.sem(n) for n in ("q_ready_dve", "q_ready_pool", "q_ready_act"))
        score_mm, s_ready, top_ready, e_ready, etop_ready = (
            st.sem(n) for n in ("score_mm", "s_ready", "top_ready", "e_ready", "etop_ready"))
        weights_ready, prod_ready, prod_done, part_ready, weight_mm, h_ready, out_mm = (
            st.sem(n) for n in ("weights_ready", "prod_ready", "prod_done", "part_ready", "weight_mm", "h_ready", "out_mm"))
        out_read, y_ready, stored = st.sem("out_read"), st.sem("y_ready"), st.sem("stored")
        ADD = WEIGH + 2
        POOL_ADDS = TILES - WEIGH
        FIRST_POOL, FIRST_ACT = 2, 4
        LEFT = TILES - WEIGH + 1
        LASTS = TILES - PER
        SHARE = 5
        FOLDED = (4, 2)
        FOLD_AT = (LEFT, LEFT + 1)

        def wait_query(eng, n, chunks):
            if n < FIRST_POOL:
                eng.wait_ge(q_ready_dve, QC * n + chunks)
            elif n < FIRST_ACT:
                eng.wait_ge(q_ready_pool, QC * (n - FIRST_POOL) + chunks)
            else:
                eng.wait_ge(q_ready_act, QC * (n - FIRST_ACT) + chunks)

        def outer(eng, i, a, b):
            n, t = i // PER, i % PER
            shape = [P, b - a, FIRSTS, KEYS]
            return eng.tensor_tensor(prod[:, i % PB, a:b].rearrange("p h (i j) -> p h i j", j=KEYS),
                                     first[:, n % 2, t, a:b].unsqueeze(3).broadcast_to(shape),
                                     second[:, n % 2, t, a:b].unsqueeze(2).broadcast_to(shape), ALU.mult)

        with nc.Block() as block:
            @block.sync
            def _(sp):
                sp.dma_start(bq[:], d["fbq"]).then_inc(ld_small, 16)
                sp.dma_start(affine[:], d["bn"]).then_inc(ld_small, 16)
                sp.dma_start(down[:], d["downT"].rearrange("(k p) n -> p k n", p=P)).then_inc(ld_down, 16)
                sp.wait_ge(zeroed, 1)
                for h in range(2):
                    for half in range(2):
                        q = (2 * h + half) * HALF
                        sp.dma_start(key[q:q + HALF, q:q + HALF], d["keys"][half]).then_inc(ld_key, 16)
                sp.dma_start(up[:], d["up"].rearrange("(c p) n -> p c n", p=P)).then_inc(ld_up, 16)
                o = d["out"].rearrange("b (t p) d -> (b t) p d", p=P)
                for i in range(TILES):
                    sp.wait_ge(y_ready, i + 1)
                    sp.dma_start(o[i], x_all[:, i]).then_inc(stored, 16)
                sp.wait_ge(stored, 16 * TILES)

            @block.gpsimd
            def _(pool):
                pool.memset(key[:], 0.0).then_inc(zeroed, 1)
                pool.memset(pair[:], 0.0).then_inc(pair_ready, 1)
                pool.memset(group_of[:], 0.0).then_inc(const_ready, 1)
                for n, off in enumerate((0, QD, -QD)):
                    pool.wait_ge(pair_ready, n + 1)
                    pool.affine_select(out=pair[:], in_=pair[:], compare_op=ALU.not_equal, fill=0.5, base=off,
                                       pattern=[[-1, P]], channel_multiplier=1).then_inc(pair_ready, 1)
                pool.wait_ge(const_ready, 1)
                pool.wait_ge(pair_ready, 4)
                for q in range(4):
                    pool.memset(group_of[q * HALF:(q + 1) * HALF, q:q + 1], 1.0).then_inc(const_ready, 1)
                pool.wait_ge(const_ready, 5)
                pool.memset(s[:, :, :, :, KEYS:ROW], ABOVE).then_inc(const_ready, 1)

                pool.wait_ge(bn_ready, 1)
                for n in range(FIRST_POOL, FIRST_ACT):
                    for c in range(QC):
                        q = qT[:, c, n * COLS:(n + 1) * COLS]
                        pool.tensor_scalar(q, q, bn[:, 0:1], bn[:, 1:2], ALU.mult, ALU.add).then_inc(q_ready_pool, 1)

                def add_output(i):
                    pool.wait_ge(out_read, i + 1)
                    pool.tensor_tensor(x_all[:, i], y[:, i % 2], x_all[:, i], ALU.add).then_inc(y_ready, 1)

                for i in range(TILES):
                    n, t = i // PER, i % PER
                    if t == 0:
                        for j in range(max(i - ADD, 0), i - ADD + PER):
                            add_output(j)
                    pool.wait_ge(weights_ready, n + 1)
                    if i >= PB:
                        pool.wait_ge(weight_mm, i - PB + 1)
                    if i < LASTS:
                        outer(pool, i, 0, HEADS // 2).then_inc(prod_ready, 1)
                        pool.wait_ge(prod_ready, i + 1)
                        last = prod[:, i % PB, 0, EXPERTS - 1:EXPERTS]
                        pool.tensor_tensor(last, last, clamped[:, n % 2, t:t + 1], ALU.add).then_inc(prod_done, 1)
                        outer(pool, i, HEADS // 2, HEADS).then_inc(prod_done, 1)
                    else:
                        outer(pool, i, SHARE, HEADS).then_inc(part_ready, 1)
                for i in range(TILES - ADD, POOL_ADDS):
                    add_output(i)

            @block.scalar
            def _(act):
                act.wait_ge(ve_ready, 1)
                act.activation(root[:, TPB:], ve[:, TPB:], ACT.Sqrt).then_inc(root_ready, 1)

                def high(b):
                    act.wait_ge(xT_mm, b)
                    for k in range(DC):
                        last = act.activation(xTs[b][0][:, k], pT[:, k], ACT.Copy)
                    last.then_inc(xTh_ready, 1)

                act.wait_ge(ld_small, 32)
                for b in range(BATCH):
                    for j in range(QC):
                        n = b * QC + j
                        act.wait_ge(query_mm, n + 1)
                        act.activation(qT[:, j, b * SEQ:(b + 1) * SEQ], query_bank(n), ACT.Identity,
                                       bias=bq[:, j:j + 1]).then_inc(query_read, 1)
                        if j == 1 and b + 1 < BATCH:
                            high(b + 1)
                    if b == 0:
                        act.wait_ge(ve_ready, 2)
                        act.activation(kroot[:], k2[:], ACT.Sqrt).then_inc(root_ready, 1)
                        act.wait_ge(ld_down, 16)
                        act.activation(dnh[:], down[:], ACT.Copy).then_inc(down_high, 1)
                act.wait_ge(ve_ready, 3)
                act.activation(broot[:], bve[:], ACT.Sqrt).then_inc(root_ready, 1)

                def normed(n):
                    for c in range(QC):
                        q = qT[:, c, n * COLS:(n + 1) * COLS]
                        act.activation(q, q, ACT.Identity, scale=bn[:, 0:1], bias=bn[:, 1:2])\
                            .then_inc(q_ready_act, 1)

                def squared(n):
                    if n >= 1:
                        act.wait_ge(norm_mm, n)
                    for c in range(QC):
                        wait_query(act, n, c + 1)
                        last = act.activation(sq[:, c], qT[:, c, n * COLS:(n + 1) * COLS], ACT.Square)
                    last.then_inc(sq_ready, 1)

                def norm_root(n):
                    act.wait_ge(n2_ready, n + 1)
                    act.activation(nroot[:, n % 2], n2[:, n % 2], ACT.Sqrt).then_inc(nroot_ready, 1)

                def exponentials(i):
                    n, t = i // PER, i % PER
                    act.wait_ge(s_ready, i + 1)
                    if n >= 2:
                        act.wait_ge(weights_ready, n - 1)
                    act.activation(e[:, n % 2, t], s[:, n % 2, t, :, 0:KEYS], ACT.Exp).then_inc(e_ready, 1)

                def read_output(i):
                    act.wait_ge(out_mm, i + 1)
                    if i >= 2:
                        act.wait_ge(y_ready, i - 1)
                    act.activation(y[:, i % 2], pO[:, i % 2, 0:D], ACT.Copy).then_inc(out_read, 1)

                for n in range(2):
                    squared(n)
                    norm_root(n)
                squared(2)
                for n in range(GROUPS):
                    if n >= 1 and n + 1 < GROUPS:
                        if n + 1 >= FIRST_ACT:
                            normed(n + 1)
                        if n + 1 > 2:
                            squared(n + 1)
                    for t in range(PER):
                        i = PER * n + t
                        exponentials(i)
                        if t == 0 and i - WEIGH - 1 >= 0:
                            read_output(i - WEIGH - 1)
                    act.wait_ge(top_ready, 2 * PER * (n + 1))
                    act.activation(etop[:, n % 2], top[:, n % 2, :, :, TOPK:], ACT.Exp).then_inc(etop_ready, 1)
                    if n >= 1 and n + 1 < GROUPS:
                        norm_root(n + 1)
                    if PER * n - WEIGH >= 0:
                        read_output(PER * n - WEIGH)
                    if n == 0:
                        for m in range(ES):
                            b, c = m // DC, m % DC
                            act.wait_ge(expert_mm, m + 1)
                            act.activation(gT[:, c, b * SEQ:(b + 1) * SEQ], expert_bank(m), ACT.Gelu)\
                                .then_inc(gelu_ready, 1)
                for i in range(TILES - WEIGH - 1, POOL_ADDS):
                    read_output(i)

            @block.vector
            def _(dve):
                chained = [0]

                def note(ins):
                    ins.then_inc(dve_chain, 1)
                    chained[0] += 1
                    return chained[0]

                def need(count):
                    dve.wait_ge(dve_chain, count)

                def link(ins):
                    need(note(ins))

                def normalise(b):
                    if b >= 3:
                        dve.wait_ge(xT_mm, b - 2)
                    for t in range(TPB):
                        i = b * TPB + t
                        last = dve.tensor_scalar(xn[:, b % 2, t], x_all[:, i], mv3[:, i, 0:1], rstd[:, i:i + 1],
                                                 ALU.subtract, ALU.mult)
                    last.then_inc(xn_ready, 1)

                def low(b):
                    dve.wait_ge(xTh_ready, b)
                    for k in range(DC):
                        last = dve.tensor_tensor(xTs[b][1][:, k], pT[:, k], xTs[b][0][:, k].bitcast(F32), ALU.subtract)
                    last.then_inc(xTl_ready, 1)

                dve.tensor_scalar(ve[:, TPB:], mv3[:, TPB:, 1], LN_EPS, None, ALU.add).then_inc(ve_ready, 1)
                dve.wait_ge(root_ready, 1)
                link(rstd_tail(dve, link, ve[:, TPB:], root[:, TPB:], y0[:, TPB:], t0[:, TPB:], u0[:, TPB:], rstd[:, TPB:]))
                normalise(1)
                dve.wait_ge(ld_key, 64)
                link(dve.tensor_tensor(keysq[:], key[:], key[:], ALU.mult))
                link(dve.tensor_reduce(ku[:], keysq[:], AX.X, ALU.add))
                dve.tensor_scalar(k2[:], ku[:], NORM_EPS ** 2, None, ALU.max).then_inc(ve_ready, 1)
                for b in range(BATCH):
                    for j in range(QC):
                        n = b * QC + j
                        dve.wait_ge(query_read, n + 1)
                        last = dve.bn_stats(stats[:, n], qT[:, j, b * SEQ:(b + 1) * SEQ])
                        if j == 1 and b + 1 < BATCH:
                            low(b + 1)
                            if b + 2 < BATCH:
                                normalise(b + 2)
                    if b == 0:
                        dve.wait_ge(ve_ready, 2)
                        dve.wait_ge(root_ready, 2)
                        link(rstd_tail(dve, link, k2[:], kroot[:], ky[:], kt[:], ku[:], kinv[:]))
                        dve.tensor_scalar(keyn[:], key[:], kinv[:], None, ALU.mult).then_inc(keyn_ready, 1)
                        dve.wait_ge(down_high, 1)
                        dve.tensor_tensor(dnl[:], down[:], dnh[:].bitcast(F32), ALU.subtract).then_inc(down_low, 1)
                    if b == 1:
                        dve.wait_ge(key_mm, 1)
                        dve.tensor_copy(keyT[:], pK[:, 0:P]).then_inc(key_ready, 1)
                link(last)
                dve.bn_aggr(mv[:], stats[:]).then_inc(mv_ready, 1)
                dve.wait_ge(avg_mm, 1)
                dve.tensor_scalar(avg[:, 1:2], pB[:, 1:2], BN_EPS, None, ALU.add)
                dve.tensor_scalar(nmean[:], pB[:, 0:1], -1.0, None, ALU.mult)
                link(dve.tensor_tensor(diff[:], mv[:, 0:1], pB[:, 0:1], ALU.subtract))
                dve.tensor_scalar(bve[:], diff[:], diff[:], avg[:, 1:2], ALU.mult, ALU.add).then_inc(ve_ready, 1)
                dve.wait_ge(ve_ready, 3)
                dve.wait_ge(root_ready, 3)
                link(rstd_tail(dve, link, bve[:], broot[:], by[:], bt[:], bu[:], brstd[:]))
                link(dve.tensor_tensor(bn[:, 0:1], affine[:, 0:1], brstd[:], ALU.mult))
                dve.tensor_scalar(bn[:, 1:2], bn[:, 0:1], nmean[:], affine[:, 1:2], ALU.mult, ALU.add).then_inc(bn_ready, 1)
                dve.wait_ge(bn_ready, 1)

                def normed(n):
                    for c in range(QC):
                        q = qT[:, c, n * COLS:(n + 1) * COLS]
                        dve.tensor_scalar(q, q, bn[:, 0:1], bn[:, 1:2], ALU.mult, ALU.add).then_inc(q_ready_dve, 1)

                def squares(n):
                    dve.wait_ge(norm_mm, n + 1)
                    dve.tensor_scalar(n2[:, n % 2], pN[:, 0:PER * HALVES], NORM_EPS ** 2, None, ALU.max)\
                        .then_inc(n2_ready, 1)

                def inverse_norm_steps(n):
                    h = n % 2
                    yy, t, u = ny[:, h], nt[:, h], nu[:, h]
                    dve.wait_ge(nroot_ready, n + 1)
                    a = note(dve.reciprocal(yy, nroot[:, h]))
                    yield
                    need(a)
                    a = note(dve.tensor_tensor(t, yy, yy, ALU.mult))
                    yield
                    need(a)
                    a = note(dve.scalar_tensor_tensor(out=u, in0=t, scalar=-0.5, in1=n2[:, h], op0=ALU.mult,
                                                      op1=ALU.mult))
                    yield
                    need(a)
                    norms_at.append(note(dve.scalar_tensor_tensor(out=ninv[:, h], in0=u, scalar=1.5, in1=yy,
                                                                  op0=ALU.add, op1=ALU.mult)))
                    yield

                def top_scores(i):
                    n, t = i // PER, i % PER
                    h = n % 2
                    dve.wait_ge(score_mm, i + 1)
                    need(norms_at[n])
                    if n >= 2:
                        dve.wait_ge(e_ready, PER * (n - 1))
                    scale = ninv[:, h, t * HALVES:(t + 1) * HALVES].unsqueeze(2).broadcast_to([P, HALVES, KEYS])
                    dve.tensor_tensor(s[:, h, t, :, 0:KEYS], pS[:, i % 2].rearrange("p (g k) -> p g k", k=KEYS),
                                      scale, ALU.mult).then_inc(s_ready, 1)
                    if t > 0 and i >= WEIGH:
                        weigh(i - WEIGH)
                    dve.wait_ge(s_ready, i + 1)
                    if n >= 2:
                        dve.wait_ge(etop_ready, n - 1)
                    for g in range(HALVES):
                        ins = dve.max(top[:, h, t, g], s[:, h, t, g])
                        if g % HEADS == HEADS - 1:
                            ins.then_inc(top_ready, 1)
                    if i == 0:
                        squares(1)
                    for g in range(HALVES):
                        if g % HEADS == 0:
                            dve.wait_ge(top_ready, 2 * i + g // HEADS + 1)
                        last = dve.match_replace(picked[:, t, g], top[:, h, t, g], s[:, h, t, g], ABOVE)
                    picked_at.append(note(last))

                def weights(n, norm_step):
                    h = n % 2
                    mark = picked[:].rearrange("p t (h s) k -> p (t h) s k", s=2)
                    ex = e[:, h].rearrange("p t (h s) k -> p (t h) s k", s=2)
                    dve.wait_ge(etop_ready, n + 1)
                    sums = note(dve.tensor_reduce(total[:].rearrange("p t h s -> p (t h s)"),
                                                  etop[:, h].rearrange("p t g k -> p (t g) k"), AX.X, ALU.add))
                    dve.wait_ge(e_ready, PER * (n + 1))
                    need(picked_at[PER * n + PER - 1])
                    own = note(dve.scalar_tensor_tensor(out=raw1[:], in0=mark[:, :, 0, 0:FIRSTS], scalar=ABOVE / 2,
                                                        in1=ex[:, :, 0, 0:FIRSTS], op0=ALU.is_gt, op1=ALU.mult))
                    need(sums)
                    inverse = note(dve.reciprocal(inv[:], total[:]))
                    if n >= 2:
                        dve.wait_ge(prod_done, 2 * PER * (n - 1))
                    dve.scalar_tensor_tensor(out=second[:, h].rearrange("p t h k -> p (t h) k"),
                                             in0=mark[:, :, 1, 0:KEYS], scalar=ABOVE / 2, in1=ex[:, :, 1],
                                             op0=ALU.is_gt, op1=ALU.mult)
                    need(own)
                    owned = note(dve.tensor_reduce(sum1[:].rearrange("p t h -> p (t h)"), raw1[:], AX.X, ALU.add))
                    need(inverse)
                    product = note(dve.tensor_tensor(both[:].rearrange("p (t h) -> p t h", t=PER), inv[:, :, :, 0],
                                                     inv[:, :, :, 1], ALU.mult))
                    next(norm_step)
                    need(owned)
                    left = note(dve.tensor_tensor(rest[:], total[:, :, :, 0], sum1[:], ALU.subtract))
                    next(norm_step)
                    need(left)
                    left = note(dve.tensor_tensor(restn[:], rest[:], inv[:, :, :, 0], ALU.mult))
                    next(norm_step)
                    need(left)
                    dve.tensor_reduce(clamped[:, h], restn[:], AX.X, ALU.add)
                    need(product)
                    dve.tensor_tensor(first[:, h].rearrange("p t h i -> p (t h) i"), raw1[:],
                                      both[:].unsqueeze(2).broadcast_to([P, PER * HEADS, FIRSTS]),
                                      ALU.mult).then_inc(weights_ready, 1)
                    next(norm_step)

                def shared_products(i):
                    n, t = i // PER, i % PER
                    dve.wait_ge(weights_ready, n + 1)
                    dve.wait_ge(weight_mm, i - PB + 1)
                    a = note(outer(dve, i, 0, 1))
                    outer(dve, i, 1, SHARE)
                    last = prod[:, i % PB, 0, EXPERTS - 1:EXPERTS]
                    need(a)
                    parts_at.append(note(dve.tensor_tensor(last, last, clamped[:, n % 2, t:t + 1], ALU.add)))

                def fold(i):
                    dve.wait_ge(part_ready, i - LASTS + 1)
                    need(parts_at[i - LASTS])
                    n = HEADS
                    while n > FOLDED[i - LASTS]:
                        n //= 2
                        last = dve.tensor_tensor(prod[:, i % PB, 0:n], prod[:, i % PB, 0:n], prod[:, i % PB, n:2 * n],
                                                 ALU.add)
                        if n > FOLDED[i - LASTS]:
                            link(last)
                    last.then_inc(prod_done, 2)

                def weigh(i):
                    dve.wait_ge(weight_mm, i + 1)
                    if i >= 2:
                        dve.wait_ge(out_mm, i - 1)
                    dve.tensor_tensor(hT[:, i % 2], pW[:, i % 2, 0:DC * P].rearrange("p (c n) -> p c n", n=P),
                                      gT[:, :, i * P:(i + 1) * P], ALU.mult).then_inc(h_ready, 1)

                def output(i):
                    dve.wait_ge(out_mm, i + 1)
                    dve.wait_ge(y_ready, i)
                    dve.tensor_tensor(x_all[:, i], pO[:, i % 2, 0:D], x_all[:, i], ALU.add).then_inc(y_ready, 1)

                norms_at, picked_at, parts_at = [], [], []
                normed(0)
                normed(1)
                squares(0)
                for _ in inverse_norm_steps(0):
                    pass
                dve.wait_ge(const_ready, 6)
                for i in range(TILES):
                    n, t = i // PER, i % PER
                    if t == 0 and i >= WEIGH:
                        weigh(i - WEIGH)
                    top_scores(i)
                    if t == PER - 1:
                        if 1 <= n and n + 1 < GROUPS:
                            squares(n + 1)
                        if i == TILES - 1:
                            weigh(i - WEIGH + 1)
                        weights(n, inverse_norm_steps(n + 1) if n + 1 < GROUPS else iter(range(PER * 2)))
                shared_products(LASTS)
                shared_products(LASTS + 1)
                for i in range(LEFT, TILES):
                    if i in FOLD_AT:
                        fold(LASTS + FOLD_AT.index(i))
                    weigh(i)
                    if i - 1 >= POOL_ADDS:
                        output(i - 1)
                output(TILES - 1)

            @block.tensor
            def _(pe):
                def transposes(b):
                    pe.wait_ge(xn_ready, b)
                    if b >= 2:
                        pe.wait_ge(xTl_ready, b - 1)
                    for k in range(DC):
                        for t in range(TPB):
                            last = pe.transpose(pT[:, k, t * P:(t + 1) * P], xn[:, b % 2, t, k * P:(k + 1) * P],
                                                ident[:])
                    last.then_inc(xT_mm, 1)

                def expert_product(m):
                    b, c = m // DC, m % DC
                    if m < 2:
                        pe.wait_ge(query_read, QS - 3 + m)
                    elif m < 4:
                        pe.wait_ge(xTl_ready, BATCH - 1)
                    else:
                        pe.wait_ge(gelu_ready, m - 3)
                    split_products(pe, expert_bank(m), [
                        ((dnh[:, k, c * P:(c + 1) * P], dnl[:, k, c * P:(c + 1) * P]), (xTs[b][0][:, k], xTs[b][1][:, k]))
                        for k in range(DC)]).then_inc(expert_mm, 1)

                def norms(n):
                    pe.wait_ge(sq_ready, n + 1)
                    if n >= 1:
                        pe.wait_ge(n2_ready, n)
                    for t in range(PER):
                        for c in range(QC):
                            a = t * HALVES + 4 * c
                            last = pe.matmul(pN[:, a:a + 4], sq[:, c, t * P:(t + 1) * P], group_of[:], start=True, stop=True)
                    last.then_inc(norm_mm, 1)

                def scores(i):
                    wait_query(pe, i // PER, QC)
                    if i >= 2:
                        pe.wait_ge(s_ready, i - 1)
                    for c in range(QC):
                        last = pe.matmul(pS[:, i % 2, c * P:(c + 1) * P], qT[:, c, i * P:(i + 1) * P], keyT[:],
                                         start=True, stop=True)
                    last.then_inc(score_mm, 1)

                def sum_heads(i):
                    if i >= 2:
                        pe.wait_ge(h_ready, i - 1)
                    pe.wait_ge(prod_done, 2 * (i + 1))
                    heads = HEADS if i < LASTS else FOLDED[i - LASTS]
                    for c in range(DC):
                        for h in range(heads):
                            last = pe.matmul(pW[:, i % 2, c * P:(c + 1) * P], prod[:, i % PB, h, c * P:(c + 1) * P],
                                             ident[:], start=(h == 0), stop=(h == heads - 1))
                    last.then_inc(weight_mm, 1)

                def mix(i):
                    pe.wait_ge(h_ready, i + 1)
                    if i >= 2:
                        if i - 2 < POOL_ADDS:
                            pe.wait_ge(out_read, i - 1)
                        else:
                            pe.wait_ge(y_ready, i - 1)
                    for c in range(DC):
                        last = pe.matmul(pO[:, i % 2, 0:D], hT[:, i % 2, c], up[:, c], start=(c == 0), stop=(c == DC - 1))
                    last.then_inc(out_mm, 1)

                for b in range(BATCH):
                    if b >= 1:
                        pe.wait_ge(xTl_ready, b)
                    for j in range(QC):
                        n = b * QC + j
                        if n >= 4:
                            pe.wait_ge(query_read, n - 3)
                        split_products(pe, query_bank(n), [
                            ((wqh[:, k, j * P:(j + 1) * P], wql[:, k, j * P:(j + 1) * P]),
                             (xTs[b][0][:, k], xTs[b][1][:, k])) for k in range(DC)]).then_inc(query_mm, 1)
                        if j == 1 and b + 1 < BATCH:
                            transposes(b + 1)
                    if b == 1:
                        pe.wait_ge(keyn_ready, 1)
                        pe.transpose(pK[:, 0:P], keyn[:], ident[:]).then_inc(key_mm, 1)
                pe.wait_ge(down_low, 1)
                expert_product(0)
                pe.wait_ge(pair_ready, 4)
                pe.wait_ge(mv_ready, 1)
                pe.matmul(pB[:, 0:2], pair[:], mv[:], start=True, stop=True).then_inc(avg_mm, 1)
                for m in range(1, 3):
                    expert_product(m)
                pe.wait_ge(const_ready, 6)
                pe.wait_ge(key_ready, 1)
                pe.wait_ge(query_read, QS)
                norms(0)
                scores(0)
                norms(1)
                scores(1)
                expert_product(3)
                scores(2)
                norms(2)
                scores(3)
                for m in range(4, ES):
                    expert_product(m)
                pe.wait_ge(gelu_ready, ES)
                pe.wait_ge(ld_up, 16)
                for i in range(TILES):
                    n, t = i // PER, i % PER
                    if t == PER - 1 and 2 <= n and n + 1 < GROUPS:
                        norms(n + 1)
                    if 3 <= i and i + 1 < TILES:
                        scores(i + 1)
                    if 0 <= i - WEIGH - 1:
                        mix(i - WEIGH - 1)
                    if 0 <= i - SUM:
                        sum_heads(i - SUM)
                mix(TILES - WEIGH - 1)
                for i in range(TILES - SUM, TILES):
                    mix(i - 2)
                    sum_heads(i)
                mix(TILES - 2)
                mix(TILES - 1)


def program(nc, d):
    with ExitStack() as ctx:
        st = Stage(nc, ctx, "keep")
        keep = {"x": st.sb("x", [P, TILES, D]), "ident": st.sb("ident", [P, P]), "mv2": st.sb("mv2", [P, TILES, 2]),
                "mv3": st.sb("mv3", [P, TILES, 2]), "moments_left": BATCH - 2}
        for n in ("Mh", "Ml", "WvTh", "WvTl"):
            keep[n] = st.sb(n, [P, DC, D], F32R)
        for n in ("wqh", "wql"):
            keep[n] = st.sb(n, [P, DC, QC * P], F32R)
        keep["xT0"] = [st.sb(n, [P, DC, SEQ], F32R) for n in ("xT0h", "xT0l")]
        with ExitStack() as inner:
            att = Stage(nc, inner, "context")
            keep["raw"] = att.sb("raw", [P, RAW, SEQ])
            keep["qT0"] = [att.sb(n, [P, DC, SEQ], F32R) for n in ("qT0h", "qT0l")]

            def halves(i):
                for n in ("cTh", "cTl"):
                    keep.setdefault(n, []).append(att.sb(f"{n}{i}", [P, DC, CPAD], F32R))
                for n in ("cNh", "cNl"):
                    keep.setdefault(n, []).append(att.sb(f"{n}{i}", [P, CT, D], F32R))

            halves(0)
            stage_gru(nc, keep, d)
            halves(1)
            stage_attention(nc, keep, d)
        stage_ffn(nc, keep, d)


def layout(np, i):
    def by_feature(v):
        return v.reshape(-1, P).T

    a = {"x": i["x"], "ctx": i["ctx_1024"], "ctxT": i["ctx_1024"].transpose(0, 2, 1),
         "W_out": i["L0_attn_W_out"], "b_out": i["L0_attn_b_out"],
         "xWq": i["L0_xattn_Wq"], "xWk": i["L0_xattn_Wk"], "xWvT": i["L0_xattn_Wv"].T,
         "gate_bias": np.stack([by_feature(i["L0_attn_" + n]) for n in ("bz_f", "bh_f", "bz_b", "bh_b")], 1),
         "fWq": i["L0_ffn_Wq"], "downT": i["L0_ffn_expert_down"].T, "up": i["L0_ffn_expert_up"],
         "fbq": by_feature(i["L0_ffn_bq"]),
         "bn": np.stack([np.concatenate([i["L0_ffn_bn_gamma"]] * 2), np.concatenate([i["L0_ffn_bn_beta"]] * 2)], 1),
         "keys": np.stack([i["L0_ffn_sub_key0"], i["L0_ffn_sub_key1"]])}
    for n in ("Wz_f", "Wh_f", "Wz_b", "Wh_b"):
        a[n] = i["L0_attn_" + n]
    return {n: np.ascontiguousarray(v) for n, v in a.items()}


def kernel(**inputs):
    import numpy as np
    import concourse.bacc as bacc
    from concourse.bass_utils import run_bass_kernel_spmd

    nc = bacc.Bacc("TRN2", target_bir_lowering=False, num_devices=1)
    arrays = layout(np, {n: np.asarray(v) for n, v in inputs.items()})
    d = {n: nc.dram_tensor(f"in_{n}", v.shape, mybir.dt.from_np(v.dtype), kind="ExternalInput").ap()
         for n, v in arrays.items()}
    d["out"] = nc.dram_tensor("out", (BATCH, SEQ, D), F32, kind="ExternalOutput").ap()
    program(nc, d)
    r = run_bass_kernel_spmd(nc, [{f"in_{n}": v for n, v in arrays.items()}], core_ids=[0])
    return r.results[0]["out"]
```
